# Optimizing a Trainium2 kernel written in Bass

```python
import numpy as np
import jax
import jax.numpy as jnp

def _softmax(x, axis=-1):
    return jax.nn.softmax(x, axis=axis)

def _gelu(x):
    return jax.nn.gelu(x, approximate=True)

def _silu(x):
    return jax.nn.silu(x)

def _sigmoid(x):
    return jax.nn.sigmoid(x)

def _layernorm(x, axis=-1, eps=1e-05):
    m = jnp.mean(x, axis=axis, keepdims=True)
    v = jnp.var(x, axis=axis, keepdims=True)
    return (x - m) / jnp.sqrt(v + eps)

def _scatter_add(tgt, idx, src, axis=0):
    return tgt.at[idx].add(src)

def _segment_sum(src, seg, n):
    return jax.ops.segment_sum(src, seg, n)
kernel_name = 'mk_vit_tower_d1_tok_img768_r4_be7ed4'

def setup_inputs(seed: int=0):
    np.random.seed(seed)
    _w = jnp.asarray

    def _rec_inputs():
        import jax
        import jax.numpy as jnp
        _rk = jax.random.key(seed)
        x = -0.00016672 + 0.999947 * jax.random.normal(jax.random.fold_in(_rk, 1), (64, 224, 224, 3), jnp.float32)
        return x
    x = _rec_inputs()

    def _L0_tok_setup():
        import jax, jax.numpy as jnp
        import numpy as np
        PATCH = 16
        key = jax.random.key(seed)
        k1, k2 = jax.random.split(key)
        B, H, Wd, C = (64, 96, 96, 3)
        patch_vec = PATCH * PATCH * C
        proj_dim = 192
        images = jax.random.normal(k1, (B, H, Wd, C), dtype=jnp.float32)
        W = jax.random.normal(k2, (patch_vec, proj_dim), dtype=jnp.float32) * (1.0 / np.sqrt(patch_vec))
        b = jnp.zeros((proj_dim,), dtype=jnp.float32)
        return {'images': images, 'W': W, 'b': b}
    _L0_tok_all = _L0_tok_setup()
    _L0_tok_in = {k: v for k, v in _L0_tok_all.items() if k in ('W', 'b')}
    del _L0_tok_all

    def _L0_attn_setup():
        import math
        import jax, jax.numpy as jnp
        import numpy as np
        D_MODEL = 192
        N_HEAD = 12
        HEAD_DIM = D_MODEL // N_HEAD
        ROPE_BASE = 10000.0
        EPS = 1e-06

        def rotary_cache(seq_len, head_dim, base=ROPE_BASE):
            half = head_dim // 2
            freq = 1.0 / base ** (jnp.arange(half, dtype=jnp.float32) / half)
            freqs = jnp.arange(seq_len, dtype=jnp.float32)[:, None] * freq[None, :]
            return (jnp.cos(freqs), jnp.sin(freqs))

        def apply_rope(x, cos, sin):
            cos = cos.astype(x.dtype)
            sin = sin.astype(x.dtype)
            x1 = x[..., ::2]
            x2 = x[..., 1::2]
            out = jnp.stack((x1 * cos - x2 * sin, x1 * sin + x2 * cos), axis=-1)
            return out.reshape(x.shape)
        key = jax.random.key(seed)
        kx, kq, kk, kv, kp = jax.random.split(key, 5)
        B, S, D = (2, 512, D_MODEL)
        x = jax.random.normal(kx, (B, S, D), dtype=jnp.float32)
        scale = 0.02
        Wq = jax.random.normal(kq, (D, D), dtype=jnp.float32) * scale
        Wk = jax.random.normal(kk, (D, D), dtype=jnp.float32) * scale
        Wv = jax.random.normal(kv, (D, D), dtype=jnp.float32) * scale
        Wproj = jax.random.normal(kp, (D, D), dtype=jnp.float32) * scale
        return {'x': x, 'Wq': Wq, 'Wk': Wk, 'Wv': Wv, 'Wproj': Wproj}
    _L0_attn_all = _L0_attn_setup()
    _L0_attn_in = {k: v for k, v in _L0_attn_all.items() if k in ('Wq', 'Wk', 'Wv', 'Wproj')}
    del _L0_attn_all

    def _L0_ffn_setup():
        import math
        import jax, jax.numpy as jnp
        import numpy as np
        NUM_EXPERTS = 8
        TOP_K = 2
        CAPACITY_FACTOR = 1.25
        H = 192
        INNER = 768
        B, S = (2, 512)
        key = jax.random.key(seed)
        ks = jax.random.split(key, 9)
        scale = 0.02
        x = jax.random.normal(ks[0], (B, S, H), dtype=jnp.float32)
        Wr = jax.random.normal(ks[1], (H, NUM_EXPERTS), dtype=jnp.float32) * scale
        w1 = jax.random.normal(ks[2], (NUM_EXPERTS, H, INNER), dtype=jnp.float32) * scale
        w3 = jax.random.normal(ks[3], (NUM_EXPERTS, H, INNER), dtype=jnp.float32) * scale
        w2 = jax.random.normal(ks[4], (NUM_EXPERTS, INNER, H), dtype=jnp.float32) * scale
        s1 = jax.random.normal(ks[5], (H, INNER), dtype=jnp.float32) * scale
        s3 = jax.random.normal(ks[6], (H, INNER), dtype=jnp.float32) * scale
        s2 = jax.random.normal(ks[7], (INNER, H), dtype=jnp.float32) * scale
        return {'x': x, 'Wr': Wr, 'w1': w1, 'w3': w3, 'w2': w2, 's1': s1, 's3': s3, 's2': s2}
    _L0_ffn_all = _L0_ffn_setup()
    _L0_ffn_in = {k: v for k, v in _L0_ffn_all.items() if k in ('Wr', 'w1', 'w3', 'w2', 's1', 's3', 's2')}
    del _L0_ffn_all
    return {'x': x, 'L0_tok_W': _L0_tok_in['W'], 'L0_tok_b': _L0_tok_in['b'], 'L0_attn_Wq': _L0_attn_in['Wq'], 'L0_attn_Wk': _L0_attn_in['Wk'], 'L0_attn_Wv': _L0_attn_in['Wv'], 'L0_attn_Wproj': _L0_attn_in['Wproj'], 'L0_ffn_Wr': _L0_ffn_in['Wr'], 'L0_ffn_w1': _L0_ffn_in['w1'], 'L0_ffn_w3': _L0_ffn_in['w3'], 'L0_ffn_w2': _L0_ffn_in['w2'], 'L0_ffn_s1': _L0_ffn_in['s1'], 'L0_ffn_s3': _L0_ffn_in['s3'], 'L0_ffn_s2': _L0_ffn_in['s2']}

def reference(x, L0_tok_W, L0_tok_b, L0_attn_Wq, L0_attn_Wk, L0_attn_Wv, L0_attn_Wproj, L0_ffn_Wr, L0_ffn_w1, L0_ffn_w3, L0_ffn_w2, L0_ffn_s1, L0_ffn_s3, L0_ffn_s2):
    import jax
    import jax.numpy as jnp

    def _L0_tok_ref(images, W, b):
        import jax, jax.numpy as jnp
        import numpy as np
        PATCH = 16
        B, H, Wd, C = images.shape
        p = PATCH
        nh, nw = (H // p, Wd // p)
        x = images.reshape(B, nh, p, nw, p, C)
        x = x.transpose(0, 1, 3, 2, 4, 5)
        patches = x.reshape(B, nh * nw, p * p * C)
        return jnp.einsum('bnd,de->bne', patches, W) + b

    def _L0_attn_ref(x, Wq, Wk, Wv, Wproj):
        import math
        import jax, jax.numpy as jnp
        import numpy as np
        D_MODEL = 192
        N_HEAD = 12
        HEAD_DIM = D_MODEL // N_HEAD
        ROPE_BASE = 10000.0
        EPS = 1e-06

        def rotary_cache(seq_len, head_dim, base=ROPE_BASE):
            half = head_dim // 2
            freq = 1.0 / base ** (jnp.arange(half, dtype=jnp.float32) / half)
            freqs = jnp.arange(seq_len, dtype=jnp.float32)[:, None] * freq[None, :]
            return (jnp.cos(freqs), jnp.sin(freqs))

        def apply_rope(x, cos, sin):
            cos = cos.astype(x.dtype)
            sin = sin.astype(x.dtype)
            x1 = x[..., ::2]
            x2 = x[..., 1::2]
            out = jnp.stack((x1 * cos - x2 * sin, x1 * sin + x2 * cos), axis=-1)
            return out.reshape(x.shape)
        B, S, D = x.shape
        H, hd = (N_HEAD, HEAD_DIM)

        def heads(W):
            return (x @ W.T).reshape(B, S, H, hd).transpose(0, 2, 1, 3)
        q, k, v = (heads(Wq), heads(Wk), heads(Wv))
        cos, sin = rotary_cache(S, hd)
        cos = cos[None, None]
        sin = sin[None, None]
        q = apply_rope(q, cos, sin)
        k = apply_rope(k, cos, sin)
        scores = jnp.einsum('bhsd,bhtd->bhst', q.astype(jnp.float32), k.astype(jnp.float32))
        scores = scores / math.sqrt(hd)
        weights = jax.lax.erf(scores) + 1.0
        mask = jnp.tril(jnp.ones((S, S), dtype=bool))[None, None]
        weights = jnp.where(mask, weights, 0.0)
        denom = jnp.maximum(weights.sum(axis=-1, keepdims=True), EPS)
        y = jnp.einsum('bhst,bhtd->bhsd', weights, v.astype(jnp.float32)) / denom
        y = y.astype(v.dtype)
        y = y.transpose(0, 2, 1, 3).reshape(B, S, D)
        return y @ Wproj.T

    def _L0_ffn_ref(x, Wr, w1, w3, w2, s1, s3, s2):
        import math
        import jax, jax.numpy as jnp
        import numpy as np
        NUM_EXPERTS = 8
        TOP_K = 2
        CAPACITY_FACTOR = 1.25
        H = 192
        INNER = 768
        B, S = (2, 512)
        b, s, h = x.shape
        n = b * s
        flat = x.reshape(n, h)
        logits = flat @ Wr
        probs = jax.nn.softmax(logits, axis=-1)
        topk_p, topk_i = jax.lax.top_k(probs, TOP_K)
        topk_p = topk_p / jnp.clip(topk_p.sum(-1, keepdims=True), 1e-09)
        capacity = max(1, math.ceil(n * TOP_K / NUM_EXPERTS * CAPACITY_FACTOR))
        onehot = topk_i[None, :, :] == jnp.arange(NUM_EXPERTS)[:, None, None]
        w_tok = jnp.sum(topk_p[None] * onehot, axis=-1)
        assigned = jnp.any(onehot, axis=-1)
        score = jnp.where(assigned, w_tok, -jnp.inf)
        order = jnp.argsort(-score, axis=1)[:, :capacity]
        score_sel = jnp.take_along_axis(score, order, axis=1)
        valid = jnp.isfinite(score_sel)
        weight_sel = jnp.where(valid, score_sel, 0.0)
        dispatch = flat[order]
        gate = jax.nn.silu(jnp.einsum('ech,ehi->eci', dispatch, w1))
        up = jnp.einsum('ech,ehi->eci', dispatch, w3)
        expert_out = jnp.einsum('eci,eih->ech', gate * up, w2)
        expert_out = expert_out * weight_sel[..., None]
        routed = jnp.zeros((n, h), dtype=flat.dtype)
        routed = routed.at[order.reshape(-1)].add(expert_out.reshape(-1, h))
        shared = jax.nn.silu(flat @ s1) * (flat @ s3) @ s2
        out = routed + shared
        return out.reshape(b, s, h)
    h = _L0_tok_ref(x, L0_tok_W, L0_tok_b)
    h = h + _L0_attn_ref(_layernorm(h, axis=-1), L0_attn_Wq, L0_attn_Wk, L0_attn_Wv, L0_attn_Wproj)
    h = h + _L0_ffn_ref(_layernorm(h, axis=-1), L0_ffn_Wr, L0_ffn_w1, L0_ffn_w3, L0_ffn_w2, L0_ffn_s1, L0_ffn_s3, L0_ffn_s2)
    return h

_drawn_inputs = setup_inputs


def setup_inputs(seed=0):
    import zlib

    import numpy as np

    out = dict(_drawn_inputs(seed))
    spreads = {'L0_tok_b': (0.0, 0.1)}
    factors = {'L0_attn_Wq': 8.0,
     'L0_attn_Wk': 8.0,
     'L0_attn_Wv': 3.802,
     'L0_attn_Wproj': 3.729,
     'L0_ffn_Wr': 4.205,
     'L0_ffn_w1': 3.687,
     'L0_ffn_w3': 3.66,
     'L0_ffn_w2': 3.661,
     'L0_ffn_s1': 3.678,
     'L0_ffn_s3': 3.636,
     'L0_ffn_s2': 3.632}
    for name, (base, spread) in spreads.items():
        noise = np.random.default_rng([zlib.crc32(name.encode()), seed]).standard_normal(out[name].shape)
        drawn = base * np.exp(spread * noise) if base else spread * noise
        out[name] = jnp.asarray(drawn.astype(out[name].dtype))
    for name, factor in factors.items():
        out[name] = (out[name] * factor).astype(out[name].dtype)
    return out
```

```python
from contextlib import ExitStack

import numpy as np

import concourse.bass as bass
from concourse import mybir

ALU = mybir.AluOpType
ACT = mybir.ActivationFunctionType
AX = mybir.AxisListType
F32 = mybir.dt.float32
U32 = mybir.dt.uint32
I32 = mybir.dt.int32

B, GRID, PATCH = 64, 14, 16
S = GRID * GRID
N = B * S
D, NH, HD = 192, 12, 16
DP = PATCH * PATCH * 3
KP = DP // 128
TP = S // 2
UT = 4 * TP
UNITS = N // UT
TILES = N // TP
E, INNER = 8, 768
MI = INNER // 128
CAP = -(-N * 2 * 5 // (E * 4))
SLOTS = E * CAP
EU = CAP // UT
KD = D // 2
EPS = 1e-5
HP = 32
VW = HD + 1
SCORE_SCALE = float(np.sqrt(2.0)) / 4.0
GUARD = 1e-9
LEAST_SCORE = -3.690 * 4
assert CAP % UT == 0 and UNITS % 2 == 0


VECTOR_STEPS = 104


class Tally:

    def __init__(self):
        self.base, self.n = 0, 0

    def step(self, ins, sem):
        self.n += 1
        ins.then_inc(sem, 1)

    @property
    def value(self):
        return self.base + self.n

    def enter(self, j, per):
        self.start, self.per = self.base + self.n, per
        self.base, self.n = self.start + j * per, 0

    def leave(self, trips):
        assert self.n == self.per, (self.n, self.per)
        self.base, self.n = self.start + trips * self.per, 0


LN1T, YT, QK, VV, PROJ, TOK, QKT, X2T, ROUTE = (
    (0, 1), (2, 3), (4, 5, 7, 8), (6, 9), (10, 11), (12, 13), tuple(range(14, 20)), (20, 21), (22,))
OWN = LN1T + QK + VV + QKT
PREV = YT + PROJ + X2T + ROUTE
TURNS = {
    "pro": TOK,
    "first": OWN + TOK,
    "mid": OWN + PREV + TOK,
    "last": OWN + PREV,
    "end": PREV,
}
NB = 2
PAIRS = 2 * NH // 2


def bank_jobs(kind, bank, before=99):
    return sum(1 for p in TURNS[kind] if p % NB == bank and p < before)


def fills(kind, u, pos):
    b = pos % NB
    base = 0
    if kind != "pro":
        base += bank_jobs("pro", b)
    if kind not in ("pro", "first"):
        base += bank_jobs("first", b)
    if kind == "mid":
        base = base + (u - 1) * bank_jobs("mid", b)
    if kind in ("last", "end"):
        base += (UNITS - 2) * bank_jobs("mid", b)
    if kind == "end":
        base += bank_jobs("last", b)
    return base + bank_jobs(kind, b, pos) + 1


def root_number(kind, u, which):
    if kind in ("pro", "first"):
        return u + 2
    return 2 * u if kind == "end" else 2 * u + 2 - which


def turns(eng, turn):
    turn("pro", -1, 0, 1)
    turn("first", 0, 0, 0)
    with eng.Fori(0, (UNITS - 2) // 2) as j:
        turn("mid", 2 * j + 1, j, 1)
        turn("mid", 2 * j + 2, j, 0)
    turn("last", UNITS - 1, (UNITS - 2) // 2, 1)
    turn("end", UNITS, (UNITS - 1) // 2, 0)



def unit_rows(ap, u):
    return ap[bass.ds(u * UT, UT), :].rearrange("(t p) d -> p t d", p=TP)


def over(ap, shape):
    while ap.ndim < len(shape):
        ap = ap.unsqueeze(1)
    return ap.to_broadcast(shape)


def attention(nc, dram, logits):
    with ExitStack() as ctx:
        def sb(name, shape, dt=F32):
            return ctx.enter_context(nc.sbuf_tensor(name, shape, dt))

        def sem(name):
            return ctx.enter_context(nc.semaphore(name))

        def ps(name):
            return ctx.enter_context(nc.psum_tensor(name, [128, 512], F32))

        patches = [sb(f"patches{s}", [128, KP * UT]) for s in range(2)]
        w_tok = sb("w_tok", [128, KP * D])
        bias = sb("bias", [TP, D])
        w_qkv = sb("w_qkv", [KD, 2 * 3 * D])
        w_proj = sb("w_proj", [KD, 2 * D])
        w_route = sb("w_route", [KD, 2 * E])
        rope = sb("rope", [TP, 2 * 2 * (HD // 2)])
        ident = sb("ident", [TP, TP])
        causal = sb("causal", [TP, 2 * TP])
        zeros = sb("zeros", [128, 1568])
        h = [sb(f"h{s}", [TP, 4, D]) for s in range(2)]
        normed = sb("normed", [TP, 4, D])
        normed_t = sb("normed_t", [KD, 2, UT])
        by_cos2 = [sb(f"by_cos{s}", [TP, 2 * NH, 2, HD // 2]) for s in range(2)]
        by_sin2 = [sb(f"by_sin{s}", [TP, 2 * NH, 2, HD // 2]) for s in range(2)]
        qk = sb("qk", [TP, 4, 2 * NH, HP])
        qk_t = sb("qk_t", [128, 6, UT])
        v = sb("v", [TP, 4, NH, VW])
        x_pair = sb("x_pair", [TP, 2, 2, 3 * TP])
        weights = sb("weights", [TP, 4, 2, 3 * TP])
        x_product = sb("x_product", [TP, 3 * TP])
        recip = sb("recip", [TP, 3 * TP])
        den = sb("den", [TP, 2, 2 * NH])
        y = sb("y", [TP, 4, NH, HD])
        y_t = sb("y_t", [KD, 2, UT])
        h2 = [sb(f"h2_{s}", [TP, 4, D]) for s in range(2)]
        x2 = [sb(f"x2_{s}", [TP, 4, D]) for s in range(2)]
        x2_t = [sb(f"x2_t{s}", [KD, 2 * UT]) for s in range(2)]
        stats = sb("stats", [TP, 2, 4, 6])
        moments = sb("moments", [TP, 2, 4, 2])
        spread = sb("spread", [TP, 2, 4])
        rstd = sb("rstd", [TP, 2, 4])
        power = sb("power", [TP, 4])
        bank = [ps(f"bank{b}") for b in range(NB)]
        score = [ctx.enter_context(nc.psum_tensor(f"score{b}", [128, 2, 512], F32)) for b in range(2)]
        y_sum = [ps(f"y_sum{b}") for b in range(2)]

        consts_in, zeroed, zero_set = sem("consts_in"), sem("zeroed"), sem("zero_set")
        patches_in = [sem(f"patches_in{s}") for s in range(2)]
        full = [sem(f"bank_full{b}") for b in range(NB)]
        free = [sem(f"bank_free{b}") for b in range(NB)]
        names = ("normed_ready roped scored clamped gelued crossed weighted masked attended y_ready spread_ready "
                 "rstd_ready x2_ready vector_steps presets spacer")
        (normed_ready, roped, scored, clamped, gelued, crossed, weighted, masked, attended, y_ready, spread_ready,
         rstd_ready, x2_ready, vec, presets, spacer) = map(sem, names.split())
        rows_out = [sem(f"rows_out{s}") for s in range(2)]
        x2t_out = [sem(f"x2t_out{s}") for s in range(2)]
        block = ctx.enter_context(nc.Block())
        constants = ((w_tok, "w_tok"), (bias, "bias"), (w_qkv, "w_qkv"), (w_proj, "w_proj"),
                     (w_route, "w_route"), (rope, "rope"), (ident, "ident"), (causal, "causal"))

        @block.sync
        def _(sp):
            sp.dma_start(patches[0][:], dram["patches"][0:128, :]).then_inc(patches_in[0], 16)
            for dst, src in constants:
                sp.dma_start(dst[:], dram[src]).then_inc(consts_in, 16)

            def turn(kind, u, prior, slot):
                prev = 1 - slot
                if kind in ("first", "mid"):
                    if kind == "mid":
                        sp.wait_ge(normed_ready, 4 * u)
                    sp.dma_start(patches[prev][:], dram["patches"][bass.ds((u + 1) * 128, 128), :])\
                      .then_inc(patches_in[prev], 16)
                if kind in ("mid", "last", "end"):
                    sp.wait_ge(x2_ready, 4 * u)
                    sp.dma_start(unit_rows(dram["h2"], u - 1), h2[prev][:]).then_inc(rows_out[prev], 16)
                    sp.dma_start(unit_rows(dram["x2"], u - 1), x2[prev][:]).then_inc(rows_out[prev], 16)
                    for pos in X2T:
                        sp.wait_ge(free[pos % NB], fills(kind, u, pos))
                    sp.dma_start(dram["x2_t"][bass.ds((u - 1) * KD, KD), :], x2_t[prev][:])\
                      .then_inc(x2t_out[prev], 16)

            turns(sp, turn)
            for s in range(2):
                sp.wait_ge(rows_out[s], 32 * (UNITS // 2 + 1))
                sp.wait_ge(x2t_out[s], 16 * (UNITS // 2 + 1))

        @block.scalar
        def _(act):
            act.wait_ge(zero_set, 1)
            cols = SLOTS * D // 128
            slots_flat = dram["slots"].rearrange("n d -> (n d)").rearrange("(p c z) -> p c z", p=128, z=1568)
            act.dma_start(slots_flat, zeros[:].unsqueeze(1).to_broadcast([128, cols // 1568, 1568]))\
               .then_inc(zeroed, 16)
            act.dma_start(dram["expert_rows"][SLOTS:SLOTS + 1, :], zeros[0:1, 0:D]).then_inc(zeroed, 16)

            def turn(kind, u, prior, slot):
                prev = 1 - slot
                own, tail = kind in ("first", "mid", "last"), kind in ("mid", "last", "end")

                def arrives(pos):
                    act.wait_ge(full[pos % NB], fills(kind, u, pos))
                    return bank[pos % NB]

                if own:
                    for k, pos in enumerate(LN1T):
                        src = arrives(pos)
                        nc.scalar.copy(normed_t[:, k, :], src[0:KD, 0:UT]).then_inc(free[pos % NB], 1)
                if tail:
                    for k, pos in enumerate(YT):
                        src = arrives(pos)
                        nc.scalar.copy(y_t[:, k, :], src[0:KD, 0:UT]).then_inc(free[pos % NB], 1)
                if own:
                    for k, pos in enumerate(VV):
                        src = arrives(pos)
                        for t in range(2):
                            last = nc.scalar.copy(v[:, 2 * k + t, :, 0:HD],
                                                  src[0:TP, t * D:(t + 1) * D].rearrange("p (h d) -> p h d", h=NH))
                        last.then_inc(free[pos % NB], 1)
                    for k, pos in enumerate(QKT):
                        src = arrives(pos)
                        nc.scalar.copy(qk_t[:, k, :], src[:, 0:UT]).then_inc(free[pos % NB], 1)
                    for n in range(PAIRS):
                        pair = PAIRS * u + n
                        act.wait_ge(clamped, pair + 1)
                        if kind != "first" or n >= 4:
                            act.wait_ge(attended, pair - 3)
                        nc.scalar.activation(weights[:, n % 4], x_pair[:, n % 2], ACT.Gelu, scale=SCORE_SCALE)\
                          .then_inc(gelued, 1)
                if tail:
                    act.wait_ge(x2t_out[prev], 16 * prior + 16)
                    for k, pos in enumerate(X2T):
                        src = arrives(pos)
                        nc.scalar.copy(x2_t[prev][:, k * UT:(k + 1) * UT], src[0:KD, 0:UT])\
                          .then_inc(free[pos % NB], 1)
                    src = arrives(ROUTE[0])
                    nc.scalar.copy(logits[:, bass.ds((u - 1) * 4 * E, 4 * E)], src[0:TP, 0:4 * E])\
                      .then_inc(free[ROUTE[0] % NB], 1)

            turns(act, turn)
            act.wait_ge(zeroed, 32)

        @block.vector
        def _(dve):
            chain = Tally()

            def step(ins):
                chain.step(ins, vec)

            def settle():
                dve.wait_ge(vec, chain.value)

            for s in range(2):
                dve.sem_inc(rows_out[s], 32)
                dve.sem_inc(x2t_out[s], 16)
            nc.vector.memset(zeros[:], 0.0).then_inc(zero_set, 1)
            nc.vector.memset(v[:], 1.0).then_inc(presets, 1)
            nc.vector.memset(qk[:], 0.0).then_inc(presets, 1)
            dve.wait_ge(presets, 2)
            nc.vector.memset(qk[:, :, :, HD:HD + 1], GUARD).then_inc(presets, 1)
            nc.vector.memset(power[:], -0.5).then_inc(presets, 1)
            dve.wait_ge(consts_in, 16 * len(constants))
            tables = rope[:].rearrange("p (a c f) -> p a c f", a=2, c=2)

            def norm(which, nth, src, dst, ready):
                settle()
                for t in range(4):
                    step(nc.vector.bn_stats(stats[:, which, t, :], src[:, t, :]))
                settle()
                dve.sem_inc(spacer, 1)
                for t in range(4):
                    step(nc.vector.bn_aggr(moments[:, which, t, :], stats[:, which, t, :]))
                settle()
                nc.vector.tensor_scalar(spread[:, which, :], moments[:, which, :, 1], EPS, None, ALU.add)\
                  .then_inc(spread_ready, 1)
                dve.wait_ge(rstd_ready, nth)
                for t in range(4):
                    nc.vector.tensor_scalar(dst[:, t, :], src[:, t, :], moments[:, which, t, 0:1],
                                            rstd[:, which, t:t + 1], ALU.subtract, ALU.mult).then_inc(ready, 1)

            def turn(kind, u, prior, slot):
                prev = 1 - slot
                own, tail = kind in ("first", "mid", "last"), kind in ("mid", "last", "end")

                def arrives(pos):
                    dve.wait_ge(full[pos % NB], fills(kind, u, pos))
                    return bank[pos % NB]

                if own:
                    for t, pos in enumerate(QK):
                        by_cos, by_sin = by_cos2[t % 2], by_sin2[t % 2]
                        src = arrives(pos)[0:TP, 0:2 * D].rearrange("p (h c f) -> p h c f", h=2 * NH, c=2)
                        shape = [TP, 2 * NH, 2, HD // 2]
                        settle()
                        step(nc.vector.tensor_tensor(by_cos[:], src, over(tables[:, t % 2, 0, :], shape), ALU.mult))
                        nc.vector.tensor_tensor(by_sin[:], src, over(tables[:, t % 2, 1, :], shape), ALU.mult)\
                          .then_inc(free[pos % NB], 1)
                        settle()
                        dve.wait_ge(free[pos % NB], fills(kind, u, pos))
                        step(nc.vector.tensor_tensor(qk[:, t, :, 0:HD // 2], by_cos[:, :, 0, :],
                                                     by_sin[:, :, 1, :], ALU.subtract))
                        nc.vector.tensor_tensor(qk[:, t, :, HD // 2:HD], by_cos[:, :, 1, :],
                                                by_sin[:, :, 0, :], ALU.add).then_inc(roped, 1)
                if tail:
                    dve.wait_ge(rows_out[prev], 32 * prior + 32)
                    for k, pos in enumerate(PROJ):
                        src = arrives(pos)
                        nc.vector.tensor_tensor(h2[prev][:, 2 * k:2 * k + 2, :],
                                                src[0:TP, 0:2 * D].rearrange("p (t d) -> p t d", t=2),
                                                h[prev][:, 2 * k:2 * k + 2, :], ALU.add)\
                          .then_inc(free[pos % NB], 1)
                    for pos in PROJ:
                        dve.wait_ge(free[pos % NB], fills(kind, u, pos))
                    norm(1, root_number(kind, u, 1), h2[prev], x2[prev], x2_ready)
                if kind in ("pro", "first", "mid"):
                    for k, pos in enumerate(TOK):
                        src = arrives(pos)
                        nc.vector.tensor_tensor(h[prev][:, 2 * k:2 * k + 2, :],
                                                src[0:TP, 0:2 * D].rearrange("p (t d) -> p t d", t=2),
                                                over(bias[:], [TP, 2, D]), ALU.add).then_inc(free[pos % NB], 1)
                    for pos in TOK:
                        dve.wait_ge(free[pos % NB], fills(kind, u, pos))
                    norm(0, root_number(kind, u, 0), h[prev], normed, normed_ready)
                if own:
                    for n in range(PAIRS):
                        pair = PAIRS * u + n
                        if n == 0:
                            clamp(u, 0)
                        if n < PAIRS - 1:
                            clamp(u, n + 1)
                        dve.wait_ge(clamped, pair + 1)
                        settle()
                        step(nc.vector.scalar_tensor_tensor(x_product[:], x_pair[:, n % 2, 0], SCORE_SCALE / 2,
                                                            x_pair[:, n % 2, 1], ALU.mult, ALU.mult))
                        if kind != "first" or n >= 1:
                            dve.wait_ge(weighted, pair)
                        settle()
                        step(nc.vector.reciprocal(recip[:], x_product[:]))
                        dve.wait_ge(crossed, pair + 1)
                        settle()
                        nc.vector.tensor_tensor(weights[:, n % 4], weights[:, n % 4], over(recip[:], [TP, 2, 3 * TP]),
                                                ALU.mult).then_inc(weighted, 1)
                        if n == PAIRS // 2 + 2:
                            outputs(u, 0, kind)
                    outputs(u, 1, kind)

            def clamp(u, n):
                dve.wait_ge(scored, PAIRS * u + n + 1)
                nc.vector.tensor_scalar(x_pair[:, n % 2], score[n % 2][0:TP, :, 0:3 * TP], LEAST_SCORE, None,
                                        ALU.max).then_inc(clamped, 1)

            def outputs(u, image, kind):
                sums = y_sum[image][0:TP, 0:2 * NH * VW].rearrange("p (h d) -> p h d", d=VW)
                dve.wait_ge(attended, PAIRS * u + PAIRS // 2 * (image + 1))
                step(nc.vector.tensor_scalar(den[:, 0, :], sums[:, :, HD], 1e-6, None, ALU.max))
                settle()
                step(nc.vector.reciprocal(den[:, 1, :], den[:, 0, :]))
                settle()
                out = y[:, 2 * image:2 * image + 2, :, :].rearrange("p t h d -> p (t h) d")
                nc.vector.tensor_tensor(out, sums[:, :, 0:HD], den[:, 1, :].unsqueeze(2).to_broadcast([TP, 2 * NH, HD]),
                                        ALU.mult).then_inc(y_ready, 1)

            turn("pro", -1, 0, 1)
            turn("first", 0, 0, 0)
            with dve.Fori(0, (UNITS - 2) // 2) as j:
                chain.enter(j, VECTOR_STEPS)
                turn("mid", 2 * j + 1, j, 1)
                turn("mid", 2 * j + 2, j, 0)
            chain.leave((UNITS - 2) // 2)
            turn("last", UNITS - 1, (UNITS - 2) // 2, 1)
            turn("end", UNITS, (UNITS - 1) // 2, 0)

        @block.gpsimd
        def _(pool):
            pool.wait_ge(presets, 4)
            pool.wait_ge(consts_in, 16 * len(constants))

            def root(which, nth):
                pool.wait_ge(spread_ready, nth)
                nc.gpsimd.tensor_tensor(rstd[:, which, :], spread[:, which, :], power[:], ALU.pow)\
                  .then_inc(rstd_ready, 1)

            def turn(kind, u, prior, slot):
                if kind in ("mid", "last", "end"):
                    root(1, root_number(kind, u, 1))
                if kind in ("pro", "first", "mid"):
                    root(0, root_number(kind, u, 0))
                if kind in ("first", "mid", "last"):
                    for n in range(PAIRS + 1):
                        pair = PAIRS * u + n
                        if n < PAIRS:
                            pool.wait_ge(gelued, pair + 1)
                            nc.gpsimd.tensor_tensor(weights[:, n % 4], weights[:, n % 4], x_pair[:, n % 2, ::-1],
                                                    ALU.mult).then_inc(crossed, 1)
                        if n >= 1:
                            pool.wait_ge(weighted, pair)
                            diagonal = weights[:, (n - 1) % 4, :, 0:2 * TP]
                            nc.gpsimd.tensor_tensor(diagonal, diagonal, over(causal[:], [TP, 2, 2 * TP]), ALU.mult)\
                              .then_inc(masked, 1)

            turns(pool, turn)

        @block.tensor
        def _(pe):
            pe.wait_ge(consts_in, 16 * len(constants))
            pe.wait_ge(presets, 4)
            tok_w = w_tok[:].rearrange("p (k n) -> p k n", k=KP)
            qkv_w = w_qkv[:].rearrange("p (k n) -> p k n", k=2)
            proj_w = w_proj[:].rearrange("p (k n) -> p k n", k=2)
            route_w = w_route[:].rearrange("p (k n) -> p k n", k=2)

            def turn(kind, u, prior, slot):
                prev = 1 - slot
                own, tail = kind in ("first", "mid", "last"), kind in ("mid", "last", "end")

                def room(pos):
                    before = fills(kind, u, pos) - 1
                    if kind != "pro" and (kind != "first" or before > 0):
                        pe.wait_ge(free[pos % NB], before)
                    return bank[pos % NB]

                def copied(jobs):
                    for pos in jobs[-NB:]:
                        pe.wait_ge(free[pos % NB], fills(kind, u, pos))

                def transposed(jobs, src):
                    for k, pos in enumerate(jobs):
                        out = room(pos)
                        for t in range(4):
                            last = nc.tensor.transpose(out[0:KD, t * TP:(t + 1) * TP],
                                                       src[:, t, k * KD:(k + 1) * KD], ident[:])
                        last.then_inc(full[pos % NB], 1)

                def product(out, lhs, rhs, width):
                    for k in range(2):
                        last = nc.tensor.matmul(out, lhs[:, k, :], rhs[:, k, 0:width], start=(k == 0), stop=(k == 1))
                    return last

                def tile(x, t):
                    return x[:, :, t * TP:(t + 1) * TP]

                if own:
                    pe.wait_ge(normed_ready, 4 * u + 4)
                    transposed(LN1T, normed)
                if tail:
                    pe.wait_ge(y_ready, 2 * u)
                    transposed(YT, y[:].rearrange("p t h d -> p t (h d)"))
                if own:
                    copied(LN1T)
                    for t in range(4):
                        out = room(QK[t])
                        product(out[0:TP, 0:2 * D], tile(normed_t, t), qkv_w, 2 * D).then_inc(full[QK[t] % NB], 1)
                        if t % 2:
                            out = room(VV[t // 2])
                            for c in range(2):
                                last = product(out[0:TP, c * D:(c + 1) * D], tile(normed_t, t - 1 + c),
                                               qkv_w[:, :, 2 * D:3 * D], D)
                            last.then_inc(full[VV[t // 2] % NB], 1)
                if tail:
                    copied(YT)
                    for k, pos in enumerate(PROJ):
                        out = room(pos)
                        for c in range(2):
                            last = product(out[0:TP, c * D:(c + 1) * D], tile(y_t, 2 * k + c), proj_w, D)
                        last.then_inc(full[pos % NB], 1)
                if kind in ("pro", "first", "mid"):
                    pe.wait_ge(patches_in[prev], 16 * (prior + 2) if kind == "mid" else 16)
                    x = patches[prev][:].rearrange("p (k t) -> p k t", k=KP)
                    for k, pos in enumerate(TOK):
                        out = room(pos)
                        for c in range(2):
                            for i in range(KP):
                                last = nc.tensor.matmul(out[0:TP, c * D:(c + 1) * D],
                                                        x[:, i, (2 * k + c) * TP:(2 * k + c + 1) * TP], tok_w[:, i, :],
                                                        start=(i == 0), stop=(i == KP - 1))
                        last.then_inc(full[pos % NB], 1)
                if own:
                    pe.wait_ge(roped, 4 * u + 4)
                    for g, pos in enumerate(QKT):
                        out = room(pos)
                        for t in range(4):
                            src = qk[:, t, 4 * g:4 * g + 4, :].rearrange("p h d -> p (h d)")
                            last = nc.tensor.transpose(out[:, t * TP:(t + 1) * TP], src, ident[:])
                        last.then_inc(full[pos % NB], 1)
                    copied(QKT)
                    copied(VV)
                    for n in range(PAIRS + 2):
                        if n < PAIRS:
                            scores(kind, u, n)
                        if n >= 2:
                            attend(kind, u, n - 2)
                if tail:
                    pe.wait_ge(x2_ready, 4 * u)
                    transposed(X2T, x2[prev])
                    copied(X2T)
                    out = room(ROUTE[0])
                    x = x2_t[prev][:].rearrange("p (k t) -> p k t", k=2)
                    for t in range(4):
                        last = product(out[0:TP, t * E:(t + 1) * E], tile(x, t), route_w, E)
                    last.then_inc(full[ROUTE[0] % NB], 1)

            def scores(kind, u, n):
                image, at = n // (PAIRS // 2), 2 * (n % (PAIRS // 2))
                if kind != "first" or n >= 2:
                    pe.wait_ge(clamped, PAIRS * u + n - 1)
                for c, head in enumerate((at, at + 1)):
                    p = HP * (head % 4)
                    q = qk_t[p:p + HD + 1, head // 4, 2 * image * TP:(2 * image + 2) * TP]
                    k = qk_t[p:p + HD + 1, 3 + head // 4, 2 * image * TP:(2 * image + 2) * TP]
                    out = score[n % 2][0:TP, c, :]
                    near = out[:, 0:3 * TP].rearrange("p (c s) -> p c s", c=3)[:, 0:3:2, :]
                    nc.tensor.matmul(near, k[:, 0:TP], q.rearrange("p (c s) -> p c s", c=2), start=True, stop=True)
                    last = nc.tensor.matmul(out[:, TP:2 * TP], k[:, TP:2 * TP], q[:, TP:2 * TP], start=True,
                                            stop=True)
                last.then_inc(scored, 1)

            def attend(kind, u, n):
                image, at = n // (PAIRS // 2), 2 * (n % (PAIRS // 2))
                pe.wait_ge(masked, PAIRS * u + n + 1)
                if at == 0 and kind != "first":
                    pe.wait_ge(y_ready, 2 * u + image - 1)
                out = y_sum[image][0:TP, 0:2 * NH * VW].rearrange("p (t h d) -> p t h d", t=2, d=VW)
                for c, head in enumerate((at, at + 1)):
                    w = weights[:, n % 4, c]
                    near, far = v[:, 2 * image, head, :], v[:, 2 * image + 1, head, :]
                    nc.tensor.matmul(out[:, 0, head, :], w[:, 0:TP], near, start=True, stop=True)
                    nc.tensor.matmul(out[:, 1, head, :], w[:, 2 * TP:3 * TP], near, start=True, stop=False)
                    last = nc.tensor.matmul(out[:, 1, head, :], w[:, TP:2 * TP], far, start=False, stop=True)
                last.then_inc(attended, 1)

            turns(pe, turn)


def routing(nc, dram, logits, slot_of, weight_of):
    BITS = 30
    with ExitStack() as ctx:
        def sb(name, shape, dt=F32):
            return ctx.enter_context(nc.sbuf_tensor(name, shape, dt))

        def sem(name):
            return ctx.enter_context(nc.semaphore(name))

        full3 = [TP, TILES, E]
        probs, first, second, keep, key, scratch = (
            sb(n, full3) for n in ("probs", "first_choice", "second_choice", "keep", "key", "scratch"))
        ones_row = sb("ones_row", [TP, TILES])
        tile_sums = sb("tile_sums", full3)
        running = sb("running", full3)
        top, norm, best, w1, w2 = (sb(n, [TP, TILES]) for n in ("top", "norm", "best", "w1", "w2"))
        before = sb("before", [TP, TP])
        ones = sb("ones", [TP, TP])
        rank = sb("rank", [TP, E])
        base = sb("base", [TP, E])
        bits = sb("bits", [TP, BITS * E], I32)
        floor = sb("floor", [TP, E], I32)
        trial = sb("trial", [TP, E], I32)
        enough = sb("enough", [TP, E], I32)
        count = sb("count", [TP, E])
        room = sb("room", [TP, E])
        total = ctx.enter_context(nc.psum_tensor("total", [128, 512], F32))
        in_tile = ctx.enter_context(nc.psum_tensor("in_tile", [128, 2, 512], F32))
        of_tile = ctx.enter_context(nc.psum_tensor("of_tile", [128, 2, 512], F32))
        consts_in, shifted, powered, vec, counted, totalled, marked, summed, spacer = map(sem, (
            "route_consts_in", "shifted", "powered", "route_steps", "counted", "totalled", "marked", "prefix_summed", "route_spacer"))
        block = ctx.enter_context(nc.Block())
        constants = ((before, "before"), (ones, "ones"), (rank, "rank"), (base, "base"), (bits, "bits"))

        @block.sync
        def _(sp):
            for dst, src in constants:
                sp.dma_start(dst[:], dram[src]).then_inc(consts_in, 16)

        @block.scalar
        def _(act):
            act.wait_ge(shifted, 1)
            nc.scalar.activation(probs[:], probs[:], ACT.Exp).then_inc(powered, 1)

        @block.tensor
        def _(pe):
            pe.wait_ge(consts_in, 16 * len(constants))
            with pe.Fori(0, BITS + 1) as i:
                pe.wait_ge(counted, i + 1)
                nc.tensor.matmul(total[0:TP, 0:E], ones[:], count[:], start=True, stop=True).then_inc(totalled, 1)
            for n in range(2):
                pe.wait_ge(marked, n + 1)
                src = (key, keep)[n][:].rearrange("p t e -> p (t e)").rearrange("p (c x) -> p c x", c=2)
                for out, mat in ((in_tile, before), (of_tile, ones)):
                    for c in range(2):
                        last = nc.tensor.matmul(out[0:TP, c, :], mat[:], src[:, c, :], start=True, stop=True)
                last.then_inc(summed, 1)

        @block.vector
        def _(dve):
            chain = Tally()

            def step(ins):
                chain.step(ins, vec)
                dve.wait_ge(vec, chain.value)

            def tt(out, a, b, op):
                step(nc.vector.tensor_tensor(out, a, b, op))

            def ts(out, a, s1, s2, op0, op1=None):
                step(nc.vector.tensor_scalar(out, a, s1, s2, op0, op1) if op1 is not None
                     else nc.vector.tensor_scalar(out, a, s1, None, op0))

            def per_tile(x):
                return x[:].unsqueeze(2).to_broadcast(full3)

            def per_expert(x):
                return x.unsqueeze(1).to_broadcast(full3)

            def by_expert(x):
                return x[:].rearrange("p t e -> p e t")

            def choose(out, top):
                step(nc.vector.tensor_reduce(top[:], probs[:], AX.X, ALU.max))
                tt(out[:], probs[:], per_tile(top), ALU.is_equal)
                tt(out[:], out[:], per_expert(rank[:]), ALU.mult)
                step(nc.vector.tensor_reduce(best[:], out[:], AX.X, ALU.max))
                tt(out[:], out[:], per_tile(best), ALU.is_equal)

            def prefix(n, src):
                dve.wait_ge(summed, n + 1)
                flat = tile_sums[:].rearrange("p t e -> p (t e)").rearrange("p (c x) -> p c x", c=2)
                step(nc.vector.tensor_copy(flat, of_tile[0:TP]))
                for e in range(E):
                    step(nc.vector.tensor_tensor_scan(running[:, :, e], ones_row[:], tile_sums[:, :, e], 0.0,
                                                      ALU.mult, ALU.add))
                tt(running[:], running[:], tile_sums[:], ALU.subtract)
                flat = running[:].rearrange("p t e -> p (t e)").rearrange("p (c x) -> p c x", c=2)
                tt(flat, flat, in_tile[0:TP], ALU.add)

            dve.wait_ge(consts_in, 16 * len(constants))
            step(nc.vector.memset(ones_row[:], 1.0))
            step(nc.vector.memset(floor[:], 0))
            view = logits[:].rearrange("p (t e) -> p t e", e=E)
            step(nc.vector.tensor_reduce(top[:], view, AX.X, ALU.max))
            nc.vector.tensor_tensor(probs[:], view, per_tile(top), ALU.subtract).then_inc(shifted, 1)
            dve.wait_ge(powered, 1)
            step(nc.vector.tensor_reduce(norm[:], probs[:], AX.X, ALU.add))
            step(nc.vector.reciprocal(norm[:], norm[:]))
            tt(probs[:], probs[:], per_tile(norm), ALU.mult)
            choose(first, w1)
            step(nc.vector.scalar_tensor_tensor(probs[:], first[:], -2.0, probs[:], ALU.mult, ALU.add))
            choose(second, w2)
            tt(norm[:], w1[:], w2[:], ALU.add)
            ts(norm[:], norm[:], 1e-9, None, ALU.max)
            step(nc.vector.reciprocal(norm[:], norm[:]))
            tt(w1[:], w1[:], norm[:], ALU.mult)
            tt(w2[:], w2[:], norm[:], ALU.mult)
            shares = weight_of[:].rearrange("p (t c) -> p t c", c=2)
            step(nc.vector.tensor_copy(shares[:, :, 0], w1[:]))
            step(nc.vector.tensor_copy(shares[:, :, 1], w2[:]))
            tt(key[:], first[:], per_tile(w1), ALU.mult)
            tt(scratch[:], second[:], per_tile(w2), ALU.mult)
            tt(key[:], key[:], scratch[:], ALU.add)
            tt(scratch[:], first[:], second[:], ALU.add)
            step(nc.vector.scalar_tensor_tensor(key[:], scratch[:], -1.0, key[:], ALU.add, ALU.add))

            with dve.Fori(0, BITS) as i:
                chain.enter(i, 4)
                tt(trial[:], floor[:], bits[:, bass.ds(i * E, E)], ALU.bitwise_or)
                tt(scratch[:], key[:], per_expert(trial[:].bitcast(F32)), ALU.is_ge)
                nc.vector.tensor_reduce(count[:], by_expert(scratch), AX.X, ALU.add).then_inc(counted, 1)
                dve.wait_ge(totalled, i + 1)
                step(nc.vector.tensor_scalar(enough[:], total[0:TP, 0:E], float(CAP), None, ALU.is_ge))
                dve.sem_inc(spacer, 1)
                step(nc.vector.copy_predicated(floor[:], enough[:], trial[:]))
            chain.leave(BITS)

            level = per_expert(floor[:].bitcast(F32))
            tt(scratch[:], key[:], level, ALU.is_gt)
            nc.vector.tensor_reduce(count[:], by_expert(scratch), AX.X, ALU.add).then_inc(counted, 1)
            dve.wait_ge(totalled, BITS + 1)
            ts(room[:], total[0:TP, 0:E], -1.0, float(CAP), ALU.mult, ALU.add)
            nc.vector.tensor_tensor(key[:], key[:], level, ALU.is_equal).then_inc(marked, 1)
            prefix(0, key)
            tt(running[:], running[:], per_expert(room[:]), ALU.is_lt)
            tt(running[:], running[:], key[:], ALU.mult)
            nc.vector.tensor_tensor(keep[:], running[:], scratch[:], ALU.add).then_inc(marked, 1)
            prefix(1, keep)
            tt(running[:], running[:], per_expert(base[:]), ALU.add)
            tt(running[:], running[:], keep[:], ALU.mult)
            slots = slot_of[:].rearrange("p (t c) -> p t c", c=2)
            for c, choice in enumerate((first, second)):
                tt(scratch[:], choice[:], running[:], ALU.mult)
                step(nc.vector.tensor_reduce(best[:], scratch[:], AX.X, ALU.add))
                ts(slots[:, :, c], best[:], float(SLOTS), None, ALU.add)


def ffn_tensors(ctx, nc, of):
    def sb(name, shape, dt=F32):
        return ctx.enter_context(nc.sbuf_tensor(name, shape, dt))

    def sem(name):
        return ctx.enter_context(nc.semaphore(name))

    class T:
        pass

    T.silu = sb(f"{of}_silu", [128, 2, UT])
    T.hidden = sb(f"{of}_hidden", [128, MI, UT])
    T.gate = [ctx.enter_context(nc.psum_tensor(f"{of}_gate{b}", [128, 512], F32)) for b in range(2)]
    T.up = [ctx.enter_context(nc.psum_tensor(f"{of}_up{b}", [128, 512], F32)) for b in range(2)]
    T.out = [ctx.enter_context(nc.psum_tensor(f"{of}_out{b}", [128, 512], F32)) for b in range(2)]
    (T.gated, T.silued, T.multiplied, T.out_full, T.out_used) = (
        sem(f"{of}_{n}") for n in ("gated", "silued", "multiplied", "out_full", "out_used"))
    return T



def units_of(eng, count, first, half, unit):
    unit(first, half, 0, True)
    unit(first + 1, half, 1, False)
    with eng.Fori(1, count // 2) as j:
        unit(first + 2 * j, half + j, 0, False)
        unit(first + 2 * j + 1, half + j, 1, False)


def tensor_unit(nc, pe, T, g, x_t, w1, w3):
    for m in range(MI):
        pe.wait_ge(T.multiplied, MI * g + m + 1)
        for out, w in ((T.gate[m % 2], w1), (T.up[m % 2], w3)):
            for k in range(2):
                last = nc.tensor.matmul(out[:, 0:UT], w[:, k, m * 128:(m + 1) * 128], x_t[:, k, :],
                                        start=(k == 0), stop=(k == 1))
        last.then_inc(T.gated, 1)


def tensor_out(nc, pe, T, g, w2):
    pe.wait_ge(T.multiplied, MI * g + MI + 2)
    for n in range(2):
        pe.wait_ge(T.out_used, 2 * g + n + 1)
        for c in range(2):
            t = 2 * n + c
            for m in range(MI):
                last = nc.tensor.matmul(T.out[n][0:TP, c * D:(c + 1) * D], T.hidden[:, m, t * TP:(t + 1) * TP],
                                        w2[:, m, :], start=(m == 0), stop=(m == MI - 1))
        last.then_inc(T.out_full, 1)


def scalar_unit(nc, act, T, g):
    for m in range(MI):
        act.wait_ge(T.gated, MI * g + m + 1)
        act.wait_ge(T.multiplied, MI * g + m + 1)
        nc.scalar.activation(T.silu[:, m % 2, :], T.gate[m % 2][:, 0:UT], ACT.Silu).then_inc(T.silued, 1)


def vector_unit(nc, dve, T, g):
    for m in range(MI):
        dve.wait_ge(T.silued, MI * g + m + 1)
        nc.vector.tensor_tensor(T.hidden[:, m, :], T.up[m % 2][:, 0:UT], T.silu[:, m % 2, :], ALU.mult)\
          .then_inc(T.multiplied, 1)


def shared(nc, dram, slot_of):
    with ExitStack() as ctx:
        def sb(name, shape, dt=F32):
            return ctx.enter_context(nc.sbuf_tensor(name, shape, dt))

        def sem(name):
            return ctx.enter_context(nc.semaphore(name))

        T = ffn_tensors(ctx, nc, "shared")
        w1, w3 = (sb(n, [KD, 2 * INNER]) for n in ("s1", "s3"))
        w2 = sb("s2", [128, MI * D])
        x_t = [sb(f"x_t{s}", [KD, 2 * UT]) for s in range(2)]
        rows = [sb(f"rows{s}", [TP, 4, D]) for s in range(2)]
        sums = [sb(f"sums{s}", [TP, 4, D]) for s in range(2)]
        sent = [sb(f"sent{s}", [TP, 4, D]) for s in range(2)]
        index = [sb(f"index{s}", [TP, 8], U32) for s in range(2)]
        weights_in = sem("shared_in")
        xt_in, rows_in, sums_out, sent_in, scattered = (
            [sem(f"{n}{s}") for s in range(2)] for n in ("xt_in", "rows_in", "sums_out", "sent_in", "scattered"))
        indexed, spacer = sem("indexed"), sem("scatter_spacer")
        block = ctx.enter_context(nc.Block())
        w1v, w3v = (w[:].rearrange("p (k n) -> p k n", k=2) for w in (w1, w3))
        w2v = w2[:].rearrange("p (m n) -> p m n", m=MI)

        @block.sync
        def _(sp):
            for dst, src in ((w1, "s1"), (w3, "s3"), (w2, "s2")):
                sp.dma_start(dst[:], dram[src]).then_inc(weights_in, 16)

            def unit(g, half, slot, opens):
                sp.wait_ge(T.out_full, 2 * g)
                sp.dma_start(x_t[slot][:], dram["x2_t"][bass.ds(g * KD, KD), :]).then_inc(xt_in[slot], 16)
                sp.wait_ge(T.out_used, 2 * g)
                sp.dma_start(rows[slot][:], unit_rows(dram["h2"], g)).then_inc(rows_in[slot], 16)
                sp.wait_ge(scattered[slot], 128 * half)
                sp.dma_start(sent[slot][:], unit_rows(dram["x2"], g)).then_inc(sent_in[slot], 16)

            units_of(sp, UNITS, 0, 0, unit)

        @block.gpsimd
        def _(pool):
            def unit(g, half, slot, opens):
                pool.wait_ge(scattered[slot], 128 * half)
                pool.sem_inc(spacer, 1)
                nc.gpsimd.tensor_copy(index[slot][:], slot_of[:, bass.ds(g * 8, 8)]).then_inc(indexed, 1)
                pool.wait_ge(indexed, g + 1)
                pool.wait_ge(sent_in[slot], 16 * half + 16)
                pool.sem_inc(spacer, 1)
                for t in range(4):
                    for c in range(2):
                        nc.gpsimd.indirect_dma_start(
                            out=dram["slots"][:, :],
                            out_offset=bass.IndirectOffsetOnAxis(ap=index[slot][:, 2 * t + c:2 * t + c + 1], axis=0),
                            in_=sent[slot][:, t, :], in_offset=None, bounds_check=SLOTS - 1, oob_is_err=False)\
                          .then_inc(scattered[slot], 16)

            units_of(pool, UNITS, 0, 0, unit)
            for s in range(2):
                pool.wait_ge(scattered[s], 128 * (UNITS // 2))

        @block.tensor
        def _(pe):
            pe.wait_ge(weights_in, 48)

            def unit(g, half, slot, opens):
                if not opens:
                    tensor_out(nc, pe, T, g - 1, w2v)
                pe.wait_ge(xt_in[slot], 16 * half + 16)
                tensor_unit(nc, pe, T, g, x_t[slot][:].rearrange("p (k t) -> p k t", k=2), w1v, w3v)

            units_of(pe, UNITS, 0, 0, unit)
            tensor_out(nc, pe, T, UNITS - 1, w2v)

        @block.scalar
        def _(act):
            def store(g, slot):
                act.wait_ge(T.out_used, 2 * g + 4)
                act.dma_start(unit_rows(dram["h2"], g), sums[slot][:]).then_inc(sums_out[slot], 16)

            def unit(g, half, slot, opens):
                scalar_unit(nc, act, T, g)
                if not opens:
                    store(g - 1, 1 - slot)

            units_of(act, UNITS, 0, 0, unit)
            store(UNITS - 1, 1)
            for s in range(2):
                act.wait_ge(sums_out[s], 16 * (UNITS // 2))

        @block.vector
        def _(dve):
            dve.sem_inc(T.multiplied, 2)
            dve.sem_inc(T.out_used, 2)
            dve.sem_inc(T.out_full, 2)

            def add(g, half, slot):
                dve.wait_ge(rows_in[slot], 16 * half + 16)
                dve.wait_ge(sums_out[slot], 16 * half)
                for n in range(2):
                    dve.wait_ge(T.out_full, 2 * g + n + 3)
                    nc.vector.tensor_tensor(sums[slot][:, 2 * n:2 * n + 2, :],
                                            T.out[n][0:TP, 0:2 * D].rearrange("p (t d) -> p t d", t=2),
                                            rows[slot][:, 2 * n:2 * n + 2, :], ALU.add).then_inc(T.out_used, 1)

            def unit(g, half, slot, opens):
                if not opens:
                    add(g - 1, half - (1 - slot), 1 - slot)
                vector_unit(nc, dve, T, g)

            units_of(dve, UNITS, 0, 0, unit)
            add(UNITS - 1, UNITS // 2 - 1, 1)


def experts(nc, dram):
    with ExitStack() as ctx:
        def sb(name, shape, dt=F32):
            return ctx.enter_context(nc.sbuf_tensor(name, shape, dt))

        def sem(name):
            return ctx.enter_context(nc.semaphore(name))

        T = ffn_tensors(ctx, nc, "experts")
        w1, w3 = ([sb(f"{n}_{s}", [KD, 2 * INNER]) for s in range(2)] for n in ("w1", "w3"))
        w2 = [sb(f"w2_{s}", [128, MI * D]) for s in range(2)]
        rows = [sb(f"tokens{s}", [TP, 4, D]) for s in range(2)]
        x_t = sb("tokens_t", [KD, 2, UT])
        done = [sb(f"done{s}", [TP, 4, D]) for s in range(2)]
        ident = sb("ident2", [TP, TP])
        turned = [ctx.enter_context(nc.psum_tensor(f"turned{k}", [128, 512], F32)) for k in range(2)]
        ident_in, turned_full, xt_ready, expert_done = map(sem, ("ident_in", "turned_full", "xt_ready", "expert_done"))
        weights_in, rows_in, stored = (
            [sem(f"{n}{s}") for s in range(2)] for n in ("weights_in", "tokens_in", "stored"))
        block = ctx.enter_context(nc.Block())

        def passes(eng, expert):
            with eng.Fori(0, E // 2) as pair:
                expert(2 * pair, pair, 0)
                expert(2 * pair + 1, pair, 1)

        @block.sync
        def _(sp):
            sp.dma_start(ident[:], dram["ident"]).then_inc(ident_in, 16)

            def expert(e, pair, ws):
                sp.wait_ge(expert_done, e + 1)
                for dst, src, p in ((w1, "w1", KD), (w3, "w3", KD), (w2, "w2", 128)):
                    sp.dma_start(dst[ws][:], dram[src][bass.ds(e * p, p), :]).then_inc(weights_in[ws], 16)

                def unit(g, half, slot, opens):
                    sp.wait_ge(xt_ready, 2 * g + 2)
                    sp.dma_start(rows[slot][:], unit_rows(dram["slots"], g)).then_inc(rows_in[slot], 16)

                units_of(sp, EU, e * EU, e * (EU // 2), unit)

            passes(sp, expert)

        @block.tensor
        def _(pe):
            pe.wait_ge(ident_in, 16)

            def expert(e, pair, ws):
                w1v, w3v = (w[ws][:].rearrange("p (k n) -> p k n", k=2) for w in (w1, w3))
                w2v = w2[ws][:].rearrange("p (m n) -> p m n", m=MI)

                def unit(g, half, slot, opens):
                    pe.wait_ge(rows_in[slot], 16 * half + 16)
                    for k in range(2):
                        pe.wait_ge(xt_ready, 2 * g + k + 3)
                        for t in range(4):
                            last = nc.tensor.transpose(turned[k][0:KD, t * TP:(t + 1) * TP],
                                                       rows[slot][:, t, k * KD:(k + 1) * KD], ident[:])
                        last.then_inc(turned_full, 1)
                    if opens:
                        pe.wait_ge(weights_in[ws], 48 * pair + 48)
                    else:
                        tensor_out(nc, pe, T, g - 1, w2v)
                    pe.wait_ge(xt_ready, 2 * g + 6)
                    tensor_unit(nc, pe, T, g, x_t, w1v, w3v)

                units_of(pe, EU, e * EU, e * (EU // 2), unit)
                tensor_out(nc, pe, T, e * EU + EU - 1, w2v)

            passes(pe, expert)

        @block.scalar
        def _(act):
            def put(g, half, slot):
                act.wait_ge(stored[slot], 16 * half + 16)
                for n in range(2):
                    act.wait_ge(T.out_full, 2 * g + n + 1)
                    nc.scalar.copy(done[slot][:, 2 * n:2 * n + 2, :],
                                   T.out[n][0:TP, 0:2 * D].rearrange("p (t d) -> p t d", t=2)).then_inc(T.out_used, 1)
                act.wait_ge(T.out_used, 2 * g + 4)
                act.dma_start(unit_rows(dram["expert_rows"], g), done[slot][:]).then_inc(stored[slot], 16)

            def expert(e, pair, ws):
                def unit(g, half, slot, opens):
                    for k in range(2):
                        act.wait_ge(turned_full, 2 * g + k + 1)
                        nc.scalar.copy(x_t[:, k, :], turned[k][0:KD, 0:UT]).then_inc(xt_ready, 1)
                    if not opens:
                        put(g - 1, half - (1 - slot), 1 - slot)
                    scalar_unit(nc, act, T, g)

                units_of(act, EU, e * EU, e * (EU // 2), unit)
                put(e * EU + EU - 1, e * (EU // 2) + EU // 2 - 1, 1)
                act.sem_inc(expert_done, 1)

            passes(act, expert)
            for s in range(2):
                act.wait_ge(stored[s], 16 * (E * EU // 2 + 1))

        @block.vector
        def _(dve):
            for primed in (T.multiplied, T.out_used, expert_done):
                dve.sem_inc(primed, 2)
            dve.sem_inc(xt_ready, 4)
            for s in range(2):
                dve.sem_inc(stored[s], 16)

            def expert(e, pair, ws):
                def unit(g, half, slot, opens):
                    vector_unit(nc, dve, T, g)

                units_of(dve, EU, e * EU, e * (EU // 2), unit)

            passes(dve, expert)


def combine(nc, dram, slot_of, weight_of):
    with ExitStack() as ctx:
        def sb(name, shape, dt=F32):
            return ctx.enter_context(nc.sbuf_tensor(name, shape, dt))

        def sem(name):
            return ctx.enter_context(nc.semaphore(name))

        rows = [sb(f"base{s}", [TP, 4, D]) for s in range(2)]
        gathered = [sb(f"gathered{s}", [TP, 8, D]) for s in range(2)]
        index = [sb(f"from{s}", [TP, 8], U32) for s in range(2)]
        rows_in, gathered_in, stored = (
            [sem(f"{n}{s}") for s in range(2)] for n in ("base_in", "gathered_in", "out_stored"))
        indexed, combined, spacer = sem("from_indexed"), sem("combined"), sem("gather_spacer")
        block = ctx.enter_context(nc.Block())

        @block.sync
        def _(sp):
            def unit(g, half, slot, opens):
                sp.wait_ge(stored[slot], 16 * half)
                sp.dma_start(rows[slot][:], unit_rows(dram["h2"], g)).then_inc(rows_in[slot], 16)

            units_of(sp, UNITS, 0, 0, unit)

        @block.gpsimd
        def _(pool):
            def unit(g, half, slot, opens):
                pool.wait_ge(combined, 8 * g)
                pool.wait_ge(gathered_in[slot], 128 * half)
                pool.sem_inc(spacer, 1)
                nc.gpsimd.tensor_copy(index[slot][:], slot_of[:, bass.ds(g * 8, 8)]).then_inc(indexed, 1)
                pool.wait_ge(indexed, g + 1)
                pool.sem_inc(spacer, 1)
                for n in range(8):
                    nc.gpsimd.indirect_dma_start(
                        out=gathered[slot][:, n, :], out_offset=None, in_=dram["expert_rows"][:, :],
                        in_offset=bass.IndirectOffsetOnAxis(ap=index[slot][:, n:n + 1], axis=0),
                        bounds_check=SLOTS, oob_is_err=False).then_inc(gathered_in[slot], 16)

            units_of(pool, UNITS, 0, 0, unit)

        @block.vector
        def _(dve):
            dve.sem_inc(combined, 8)

            def unit(g, half, slot, opens):
                dve.wait_ge(rows_in[slot], 16 * half + 16)
                dve.wait_ge(gathered_in[slot], 128 * half + 128)
                for c in range(2):
                    if c:
                        dve.wait_ge(combined, 8 * g + 12)
                    for t in range(4):
                        nc.vector.scalar_tensor_tensor(
                            rows[slot][:, t, :], gathered[slot][:, 2 * t + c, :],
                            weight_of[:, bass.ds(g * 8 + 2 * t + c, 1)], rows[slot][:, t, :], ALU.mult, ALU.add)\
                          .then_inc(combined, 1)

            units_of(dve, UNITS, 0, 0, unit)

        @block.scalar
        def _(act):
            def unit(g, half, slot, opens):
                act.wait_ge(combined, 8 * g + 16)
                act.dma_start(unit_rows(dram["out"], g), rows[slot][:]).then_inc(stored[slot], 16)

            units_of(act, UNITS, 0, 0, unit)
            for s in range(2):
                act.wait_ge(stored[s], 16 * (UNITS // 2))


def build(nc, dram):
    with (nc.sbuf_tensor("logits", [TP, TILES * E], F32) as logits,
          nc.sbuf_tensor("slot_of", [TP, TILES * 2], U32) as slot_of,
          nc.sbuf_tensor("weight_of", [TP, TILES * 2], F32) as weight_of):
        attention(nc, dram, logits)
        routing(nc, dram, logits, slot_of, weight_of)
        shared(nc, dram, slot_of)
        experts(nc, dram)
        combine(nc, dram, slot_of, weight_of)


def rope_table():
    half = HD // 2
    freq = (np.float32(1.0) / np.power(np.float32(10000.0), np.arange(half, dtype=np.float32) / np.float32(half)))
    angle = np.arange(S, dtype=np.float32)[:, None] * freq.astype(np.float32)[None, :]
    table = np.stack([np.cos(angle), np.sin(angle)], 1).astype(np.float32)
    return np.ascontiguousarray(table.reshape(2, TP, 2, half).transpose(1, 0, 2, 3).reshape(TP, -1))


def halves(w):
    return np.ascontiguousarray(w.reshape(2, KD, -1).transpose(1, 0, 2).reshape(KD, -1))


def inner_rows(w):
    return np.ascontiguousarray(w.reshape(MI, 128, D).transpose(1, 0, 2).reshape(128, -1))


def layout(x, L0_tok_W, L0_tok_b, L0_attn_Wq, L0_attn_Wk, L0_attn_Wv, L0_attn_Wproj, L0_ffn_Wr, L0_ffn_w1, L0_ffn_w3,
           L0_ffn_w2, L0_ffn_s1, L0_ffn_s3, L0_ffn_s2):
    p = x.reshape(UNITS, 2, GRID, PATCH, GRID, PATCH * 3).transpose(0, 3, 5, 1, 2, 4).reshape(UNITS, KP, 128, UT)
    split = np.arange(D).reshape(NH, HD // 2, 2).transpose(0, 2, 1).reshape(-1)
    qkv = np.concatenate([L0_attn_Wq.T[:, split], L0_attn_Wk.T[:, split], L0_attn_Wv.T], 1)
    return {
        "patches": np.ascontiguousarray(p.transpose(0, 2, 1, 3)).reshape(UNITS * 128, KP * UT),
        "w_tok": np.ascontiguousarray(L0_tok_W.reshape(KP, 128, D).transpose(1, 0, 2)).reshape(128, KP * D),
        "bias": np.ascontiguousarray(np.broadcast_to(L0_tok_b, (TP, D))),
        "w_qkv": halves(qkv),
        "w_proj": halves(np.ascontiguousarray(L0_attn_Wproj.T)),
        "w_route": halves(L0_ffn_Wr),
        "rope": rope_table(),
        "ident": np.eye(TP, dtype=np.float32),
        "causal": np.tile(np.triu(np.ones((TP, TP), np.float32)), (1, 2)),
        "before": np.triu(np.ones((TP, TP), np.float32), 1),
        "ones": np.ones((TP, TP), np.float32),
        "rank": np.tile(np.arange(E, 0, -1, dtype=np.float32), (TP, 1)),
        "base": np.tile(np.arange(E, dtype=np.float32) * CAP - SLOTS, (TP, 1)),
        "bits": np.tile(np.repeat(1 << np.arange(29, -1, -1, dtype=np.int32), E), (TP, 1)).astype(np.int32),
        "s1": halves(L0_ffn_s1),
        "s3": halves(L0_ffn_s3),
        "s2": inner_rows(L0_ffn_s2),
        "w1": np.concatenate([halves(w) for w in L0_ffn_w1]),
        "w3": np.concatenate([halves(w) for w in L0_ffn_w3]),
        "w2": np.concatenate([inner_rows(w) for w in L0_ffn_w2]),
    }


def kernel(**inputs):
    import concourse.bacc as _bacc
    from concourse.bass_utils import run_bass_kernel_spmd as _run

    arrays = layout(**{k: np.asarray(v) for k, v in inputs.items()})
    nc = _bacc.Bacc("TRN2", target_bir_lowering=False, num_devices=1)
    dram = {n: nc.dram_tensor("in_" + n, a.shape, mybir.dt.from_np(a.dtype), kind="ExternalInput").ap()
            for n, a in arrays.items()}
    for n, shape in (("h2", (N, D)), ("x2", (N, D)), ("x2_t", (UNITS * KD, 2 * UT)), ("slots", (SLOTS, D)),
                     ("expert_rows", (SLOTS + 1, D))):
        dram[n] = nc.dram_tensor("dram_" + n, shape, F32, kind="Internal").ap()
    dram["out"] = nc.dram_tensor("out_rows", (N, D), F32, kind="ExternalOutput").ap()
    build(nc, dram)
    r = _run(nc, [{"in_" + n: a for n, a in arrays.items()}], core_ids=[0])
    return r.results[0]["out_rows"].reshape(B, S, D)
```

```python
from contextlib import ExitStack

import numpy as np

import concourse.bass as bass
from concourse import mybir

ALU = mybir.AluOpType
ACT = mybir.ActivationFunctionType
AX = mybir.AxisListType
F32 = mybir.dt.float32
F16 = mybir.dt.float16
U32 = mybir.dt.uint32
I32 = mybir.dt.int32

B, GRID, PATCH = 64, 14, 16
S = GRID * GRID
N = B * S
D, NH, HD = 192, 12, 16
DP = PATCH * PATCH * 3
KP = DP // 128
TP = S // 2
UT = 4 * TP
UNITS = N // UT
TILES = N // TP
E, INNER = 8, 768
MI = INNER // 128
CAP = -(-N * 2 * 5 // (E * 4))
SLOTS = E * CAP
EU = CAP // UT
KD = D // 2
EPS = 1e-5
HP = 32
VW = HD + 1
SCORE_SCALE = float(np.sqrt(2.0)) / 4.0
GUARD = 1e-9
FLOOR = 3 * 2.0 ** -24
assert CAP % UT == 0 and UNITS % 2 == 0


VECTOR_STEPS = 74


class Tally:

    def __init__(self):
        self.base, self.n = 0, 0

    def step(self, ins, sem):
        self.n += 1
        ins.then_inc(sem, 1)

    @property
    def value(self):
        return self.base + self.n

    def enter(self, j, per):
        self.start, self.per = self.base + self.n, per
        self.base, self.n = self.start + j * per, 0

    def leave(self, trips):
        assert self.n == self.per, (self.n, self.per)
        self.base, self.n = self.start + trips * self.per, 0


TOK, LN1T, YT, QK, VV, PROJ, QKT, X2T, ROUTE = (
    (0, 1), (2, 3), (4, 5), (6, 7, 9, 10), (8, 11), (12, 13), tuple(range(14, 20)), (20, 21), (22,))
NEXT = TOK + LN1T + QK + VV + QKT
PREV = YT + PROJ + X2T + ROUTE
TURNS = {
    "pro": NEXT,
    "first": NEXT,
    "mid": NEXT + PREV,
    "last": PREV,
    "end": PREV,
}
NB = 2
PAIRS = 2 * NH // 2
LAG = 4
ZERO_PARTS = UNITS - 2
assert SLOTS * D % (128 * ZERO_PARTS) == 0


def fills(kind, u, pos):
    def jobs(kind, before=99):
        return sum(1 for p in TURNS[kind] if p % NB == pos % NB and p < before)

    earlier = {"pro": (), "first": ("pro",), "mid": ("pro", "first"), "last": ("pro", "first"),
               "end": ("pro", "first", "last")}[kind]
    count = sum(jobs(k) for k in earlier) + jobs(kind, pos) + 1
    if kind == "mid":
        return count + (u - 1) * jobs("mid")
    return count + ((UNITS - 2) * jobs("mid") if kind in ("last", "end") else 0)


def root_number(kind, u, which):
    if kind in ("pro", "first"):
        return u + 2
    return 2 * u + 1 + which if kind == "mid" else UNITS + u


def parts_of(kind):
    return kind in ("first", "mid", "last"), kind in ("pro", "first", "mid"), kind in ("mid", "last", "end")


def turns(eng, turn):
    turn("pro", -1, 0, 1)
    turn("first", 0, 0, 0)
    with eng.Fori(0, (UNITS - 2) // 2) as j:
        turn("mid", 2 * j + 1, j, 1)
        turn("mid", 2 * j + 2, j, 0)
    turn("last", UNITS - 1, (UNITS - 2) // 2, 1)
    turn("end", UNITS, (UNITS - 1) // 2, 0)


def unit_rows(ap, u):
    return ap[bass.ds(u * UT, UT), :].rearrange("(t p) d -> p t d", p=TP)


def over(ap, shape):
    while ap.ndim < len(shape):
        ap = ap.unsqueeze(1)
    return ap.to_broadcast(shape)


def turn_near(nc, out, rows, ident):
    return nc.tensor.transpose(out, rows[:, 0:128], ident)


def turn_far(nc, out, rows, ident):
    nc.tensor.transpose(out, rows[:, D - 128:D], ident)
    return nc.tensor.transpose(out[0:D - 128], rows[:, 128:D], ident)


def attention(nc, dram, logits):
    with ExitStack() as ctx:
        def sb(name, shape, dt=F32):
            return ctx.enter_context(nc.sbuf_tensor(name, shape, dt))

        def sem(name):
            return ctx.enter_context(nc.semaphore(name))

        def ps(name):
            return ctx.enter_context(nc.psum_tensor(name, [128, 512], F32))

        patches = [sb(f"patches{s}", [128, KP * UT]) for s in range(2)]
        w_tok = sb("w_tok", [128, KP * D])
        bias = sb("bias", [TP, D])
        w_qkv = sb("w_qkv", [KD, 2 * 3 * D])
        w_proj = sb("w_proj", [KD, 2 * D])
        w_route = sb("w_route", [128, 2 * E])
        rope = sb("rope", [TP, 2 * 2 * (HD // 2)])
        ident = sb("ident", [TP, TP])
        causal = sb("causal", [TP, TP])
        zeros = sb("zeros", [128, SLOTS * D // 128 // ZERO_PARTS])
        h_new = sb("h_new", [TP, 4, D])
        h = [sb(f"h{s}", [TP, 4, D]) for s in range(2)]
        normed = sb("normed", [TP, 4, D])
        normed_t = sb("normed_t", [KD, 2, UT])
        qk_raw = sb("qk_raw", [TP, 4, 2 * D])
        by_cos = [sb(f"by_cos{s}", [TP, 2 * NH, 2, HD // 2]) for s in range(2)]
        by_sin = [sb(f"by_sin{s}", [TP, 2 * NH, 2, HD // 2]) for s in range(2)]
        qk = sb("qk", [TP, 4, 2 * NH, HP])
        qk_t = [sb(f"qk_t{s}", [128, 6, UT]) for s in range(2)]
        v = [sb(f"v{s}", [TP, 4, NH, VW]) for s in range(2)]
        x_pair = sb("x_pair", [TP, 4, 2, 3 * TP])
        weights = sb("weights", [TP, 4, 2, 3 * TP])
        x_product = sb("x_product", [TP, 2, 3 * TP])
        recip = sb("recip", [TP, 2, 3 * TP])
        den = sb("den", [TP, 2, 2 * NH])
        y = sb("y", [TP, 4, NH, HD])
        y_t = sb("y_t", [KD, 2, UT])
        h2 = [sb(f"h2_{s}", [TP, 4, D]) for s in range(2)]
        x2 = [sb(f"x2_{s}", [TP, 4, D]) for s in range(2)]
        x2_t = [sb(f"x2_t{s}", [128, 2 * UT]) for s in range(2)]
        stats = sb("stats", [TP, 2, 4, 6])
        moments = sb("moments", [TP, 2, 4, 2])
        spread = sb("spread", [TP, 2, 4])
        rstd = sb("rstd", [TP, 2, 4])
        minus_half = sb("minus_half", [TP, 4])
        bank = [ps(f"bank{b}") for b in range(NB)]
        score = [ctx.enter_context(nc.psum_tensor(f"score{b}", [128, 2, 512], F32)) for b in range(2)]
        y_sum = [ps(f"y_sum{b}") for b in range(2)]

        consts_in, zeroed, zero_set = sem("consts_in"), sem("zeroed"), sem("zero_set")
        patches_in = [sem(f"patches_in{s}") for s in range(2)]
        full = [sem(f"bank_full{b}") for b in range(NB)]
        free = [sem(f"bank_free{b}") for b in range(NB)]
        names = ("normed_ready roped scored copied_out gelued crossed multiplied_x inverted weighted floored masked attended "
                 "y_ready spread_ready rstd_ready x2_ready vector_steps presets spacer biased h_kept")
        (normed_ready, roped, scored, copied_out, gelued, crossed, multiplied_x, inverted, weighted, floored, masked, attended,
         y_ready, spread_ready, rstd_ready, x2_ready, vec, presets, spacer, biased, h_kept) = (
             map(sem, names.split()))
        rows_out = [sem(f"rows_out{s}") for s in range(2)]
        x2t_out = [sem(f"x2t_out{s}") for s in range(2)]
        block = ctx.enter_context(nc.Block())
        constants = ((w_tok, "w_tok"), (bias, "bias"), (w_qkv, "w_qkv"), (w_proj, "w_proj"),
                     (w_route, "w_route"), (rope, "rope"), (ident, "ident"), (causal, "causal"))

        @block.sync
        def _(sp):
            sp.dma_start(patches[0][:], dram["patches"][0:128, :]).then_inc(patches_in[0], 16)
            for dst, src in constants:
                sp.dma_start(dst[:], dram[src]).then_inc(consts_in, 16)

            def turn(kind, u, prior, slot):
                prev = 1 - slot
                if kind in ("first", "mid"):
                    if kind == "mid":
                        sp.wait_ge(normed_ready, 4 * u)
                    sp.dma_start(patches[prev][:], dram["patches"][bass.ds((u + 1) * 128, 128), :])\
                      .then_inc(patches_in[prev], 16)
                if kind in ("mid", "last", "end"):
                    sp.wait_ge(x2_ready, 4 * u)
                    sp.dma_start(unit_rows(dram["h2"], u - 1), h2[prev][:]).then_inc(rows_out[prev], 16)
                    sp.dma_start(unit_rows(dram["x2"], u - 1), x2[prev][:]).then_inc(rows_out[prev], 16)
                    for pos in X2T:
                        sp.wait_ge(free[pos % NB], fills(kind, u, pos))
                    sp.dma_start(dram["x2_t"][bass.ds((u - 1) * 128, 128), :], x2_t[prev][:])\
                      .then_inc(x2t_out[prev], 16)

            turns(sp, turn)
            for s in range(2):
                sp.wait_ge(rows_out[s], 32 * (UNITS // 2 + 1))
                sp.wait_ge(x2t_out[s], 16 * (UNITS // 2 + 1))

        @block.scalar
        def _(act):
            act.wait_ge(zero_set, 1)
            slots_flat = dram["slots"].rearrange("n d -> (n d)")\
                .rearrange("(p c z) -> p c z", p=128, c=ZERO_PARTS)
            act.dma_start(dram["expert_rows"][SLOTS:SLOTS + 1, :], zeros[0:1, 0:D]).then_inc(zeroed, 16)

            def turn(kind, u, prior, slot):
                prev = 1 - slot
                pairs, has_next, has_prev = parts_of(kind)

                def copy_out(pos, dst, rows, cols=UT):
                    act.wait_ge(full[pos % NB], fills(kind, u, pos))
                    nc.scalar.copy(dst, bank[pos % NB][0:rows, 0:cols]).then_inc(free[pos % NB], 1)

                for n in range(PAIRS):
                    if pairs:
                        pair = PAIRS * u + n
                        act.wait_ge(scored, pair + 1)
                        if kind != "first" or n >= 4:
                            act.wait_ge(weighted, pair - 3)
                        nc.scalar.copy(x_pair[:, n % 4], score[n % 2][0:TP, :, 0:3 * TP]).then_inc(copied_out, 1)
                        act.wait_ge(copied_out, pair + 1)
                        if kind != "first" or n >= 4:
                            act.wait_ge(attended, pair - 3)
                        nc.scalar.activation(weights[:, n % 4], x_pair[:, n % 4], ACT.Gelu, scale=SCORE_SCALE)\
                          .then_inc(gelued, 1)
                    if n == 1 and has_next:
                        if kind != "pro":
                            act.wait_ge(h_kept, u + 1)
                        for k, pos in enumerate(TOK):
                            copy_out(pos, h_new[:, 2 * k:2 * k + 2, :].rearrange("p t d -> p (t d)"), TP, 2 * D)
                    if n == 3 and kind == "mid":
                        act.dma_start(slots_flat[:, bass.ds(u - 1, 1), :], zeros[:].unsqueeze(1)).then_inc(zeroed, 16)
                    if n == 4 and has_next:
                        for k, pos in enumerate(LN1T):
                            copy_out(pos, normed_t[:, k, :], KD)
                    if n == 5 and has_prev:
                        for k, pos in enumerate(YT):
                            copy_out(pos, y_t[:, k, :], KD)
                    if n in (6, 7) and has_next:
                        for t in range(2 * n - 12, 2 * n - 10):
                            copy_out(QK[t], qk_raw[:, t, :], TP, 2 * D)
                        pos = VV[n - 6]
                        act.wait_ge(full[pos % NB], fills(kind, u, pos))
                        for t in range(2):
                            last = nc.scalar.copy(v[prev][:, 2 * (n - 6) + t, :, 0:HD],
                                                  bank[pos % NB][0:TP, t * D:(t + 1) * D]
                                                  .rearrange("p (h d) -> p h d", h=NH))
                        last.then_inc(free[pos % NB], 1)
                    if n == 8 and has_prev:
                        act.wait_ge(rows_out[prev], 32 * prior + 32)
                        for k, pos in enumerate(PROJ):
                            copy_out(pos, h2[prev][:, 2 * k:2 * k + 2, :].rearrange("p t d -> p (t d)"), TP, 2 * D)
                    if n == 10 and has_next:
                        if has_prev:
                            act.wait_ge(spread_ready, root_number(kind, u, 1))
                        act.wait_ge(biased, u + 2)
                        nc.scalar.copy(h[prev][:], h_new[:]).then_inc(h_kept, 1)
                    if n >= 9 and has_next:
                        for g in range(2 * n - 18, 2 * n - 16):
                            copy_out(QKT[g], qk_t[prev][:, g, :], 128)
                    if n == 11 and has_prev:
                        act.wait_ge(x2t_out[prev], 16 * prior + 16)
                        for k, pos in enumerate(X2T):
                            copy_out(pos, x2_t[prev][:, k * UT:(k + 1) * UT], 128)
                        pos = ROUTE[0]
                        act.wait_ge(full[pos % NB], fills(kind, u, pos))
                        nc.scalar.copy(logits[:, bass.ds((u - 1) * 4 * E, 4 * E)], bank[pos % NB][0:TP, 0:4 * E])\
                          .then_inc(free[pos % NB], 1)

            turns(act, turn)
            act.wait_ge(zeroed, 16 * (ZERO_PARTS + 1))

        @block.vector
        def _(dve):
            chain = Tally()

            def step(ins):
                chain.step(ins, vec)

            def settle():
                dve.wait_ge(vec, chain.value)

            for s in range(2):
                dve.sem_inc(rows_out[s], 32)
                dve.sem_inc(x2t_out[s], 16)
            nc.vector.memset(zeros[:], 0.0).then_inc(zero_set, 1)
            for s in range(2):
                nc.vector.memset(v[s][:], 1.0).then_inc(presets, 1)
            nc.vector.memset(qk[:], 0.0).then_inc(presets, 1)
            dve.wait_ge(presets, 3)
            nc.vector.memset(qk[:, :, :, HD:HD + 1], GUARD).then_inc(presets, 1)
            nc.vector.memset(minus_half[:], -0.5).then_inc(presets, 1)
            dve.wait_ge(consts_in, 16 * len(constants))
            tables = rope[:].rearrange("p (a c f) -> p a c f", a=2, c=2)

            def norm(which, nth, src, dst, ready):
                settle()
                for t in range(4):
                    step(nc.vector.bn_stats(stats[:, which, t, :], src[:, t, :]))
                settle()
                dve.sem_inc(spacer, 1)
                for t in range(4):
                    step(nc.vector.bn_aggr(moments[:, which, t, :], stats[:, which, t, :]))
                settle()
                nc.vector.tensor_scalar(spread[:, which, :], moments[:, which, :, 1], EPS, None, ALU.add)\
                  .then_inc(spread_ready, 1)
                dve.wait_ge(rstd_ready, nth)
                for t in range(4):
                    nc.vector.tensor_scalar(dst[:, t, :], src[:, t, :], moments[:, which, t, 0:1],
                                            rstd[:, which, t:t + 1], ALU.subtract, ALU.mult).then_inc(ready, 1)

            def multiply_x(u, n):
                dve.wait_ge(copied_out, PAIRS * u + n + 1)
                nc.vector.scalar_tensor_tensor(x_product[:, n % 2], x_pair[:, n % 4, 0], SCORE_SCALE / 2,
                                               x_pair[:, n % 4, 1], ALU.mult, ALU.mult).then_inc(multiplied_x, 1)

            def weigh(u, n):
                dve.wait_ge(crossed, PAIRS * u + n + 1)
                dve.wait_ge(inverted, PAIRS * u + n + 1)
                nc.vector.tensor_tensor(weights[:, n % 4], weights[:, n % 4], over(recip[:, n % 2], [TP, 2, 3 * TP]),
                                        ALU.mult).then_inc(weighted, 1)

            def floor(u, n):
                dve.wait_ge(weighted, PAIRS * u + n + 1)
                diagonal = weights[:, n % 4, :, 0:TP]
                nc.vector.scalar_tensor_tensor(diagonal, diagonal, FLOOR, over(causal[:], [TP, 2, TP]),
                                               ALU.max, ALU.mult).then_inc(floored, 1)

            def outputs(u, image):
                sums = y_sum[image][0:TP, 0:2 * NH * VW].rearrange("p (h d) -> p h d", d=VW)
                dve.wait_ge(attended, PAIRS * u + PAIRS // 2 * (image + 1))
                step(nc.vector.tensor_scalar(den[:, 0, :], sums[:, :, HD], 1e-6, None, ALU.max))
                settle()
                step(nc.vector.reciprocal(den[:, 1, :], den[:, 0, :]))
                settle()
                out = y[:, 2 * image:2 * image + 2, :, :].rearrange("p t h d -> p (t h) d")
                nc.vector.tensor_tensor(out, sums[:, :, 0:HD], den[:, 1, :].unsqueeze(2).to_broadcast([TP, 2 * NH, HD]),
                                        ALU.mult).then_inc(y_ready, 1)

            def turn(kind, u, prior, slot):
                prev = 1 - slot
                pairs, has_next, has_prev = parts_of(kind)

                def out_of(jobs):
                    for pos in jobs[-NB:]:
                        dve.wait_ge(free[pos % NB], fills(kind, u, pos))

                for n in range(PAIRS):
                    if pairs:
                        pair = PAIRS * u + n
                        if n < PAIRS - 1:
                            if kind != "first" or n >= 1:
                                dve.wait_ge(inverted, pair)
                            multiply_x(u, n + 1)
                        if n >= 1:
                            weigh(u, n - 1)
                    if n == 0 and has_prev:
                        weigh(u - 1, PAIRS - 1)
                    if pairs:
                        dve.wait_ge(multiplied_x, pair + 1)
                        if kind != "first" or n >= 2:
                            dve.wait_ge(weighted, pair - 1)
                        nc.vector.reciprocal(recip[:, n % 2], x_product[:, n % 2]).then_inc(inverted, 1)
                        if n >= 1:
                            floor(u, n - 1)
                    if n == 0 and has_prev:
                        floor(u - 1, PAIRS - 1)
                    if n == 1 and has_next:
                        out_of(TOK)
                        nc.vector.tensor_tensor(h_new[:], h_new[:], over(bias[:], [TP, 4, D]), ALU.add)\
                          .then_inc(biased, 1)
                        dve.wait_ge(biased, u + 2)
                        norm(0, root_number(kind, u, 0), h_new, normed, normed_ready)
                    if n == 2 and has_prev:
                        outputs(u - 1, 1)
                    if n in (6, 7) and has_next:
                        shape = [TP, 2 * NH, 2, HD // 2]
                        for i in range(2):
                            t = 2 * (n - 6) + i
                            dve.wait_ge(free[QK[t] % NB], fills(kind, u, QK[t]))
                            src = qk_raw[:, t, :].rearrange("p (h c f) -> p h c f", h=2 * NH, c=2)
                            if i == 0:
                                settle()
                            step(nc.vector.tensor_tensor(by_cos[i][:], src, over(tables[:, i, 0, :], shape), ALU.mult))
                            step(nc.vector.tensor_tensor(by_sin[i][:], src, over(tables[:, i, 1, :], shape), ALU.mult))
                        for i in range(2):
                            t = 2 * (n - 6) + i
                            settle()
                            step(nc.vector.tensor_tensor(qk[:, t, :, 0:HD // 2], by_cos[i][:, :, 0, :],
                                                         by_sin[i][:, :, 1, :], ALU.subtract))
                            step(nc.vector.tensor_tensor(qk[:, t, :, HD // 2:HD], by_cos[i][:, :, 1, :],
                                                         by_sin[i][:, :, 0, :], ALU.add))
                        settle()
                        dve.sem_inc(roped, 2)
                    if n == 8 and has_prev:
                        out_of(PROJ)
                        dve.wait_ge(h_kept, u)
                        step(nc.vector.tensor_tensor(h2[prev][:], h2[prev][:], h[prev][:], ALU.add))
                        norm(1, root_number(kind, u, 1), h2[prev], x2[prev], x2_ready)
                    if n == 9 and pairs:
                        outputs(u, 0)
                if has_next:
                    if pairs:
                        dve.wait_ge(inverted, PAIRS * u + PAIRS - 1)
                    multiply_x(u + 1, 0)

            turn("pro", -1, 0, 1)
            turn("first", 0, 0, 0)
            with dve.Fori(0, (UNITS - 2) // 2) as j:
                chain.enter(j, VECTOR_STEPS)
                turn("mid", 2 * j + 1, j, 1)
                turn("mid", 2 * j + 2, j, 0)
            chain.leave((UNITS - 2) // 2)
            turn("last", UNITS - 1, (UNITS - 2) // 2, 1)
            turn("end", UNITS, (UNITS - 1) // 2, 0)

        @block.gpsimd
        def _(pool):
            pool.wait_ge(presets, 5)
            pool.wait_ge(consts_in, 16 * len(constants))

            def root(which, nth):
                pool.wait_ge(spread_ready, nth)
                nc.gpsimd.tensor_tensor(rstd[:, which, :], spread[:, which, :], minus_half[:], ALU.pow)\
                  .then_inc(rstd_ready, 1)

            def cross(u, n):
                pool.wait_ge(gelued, PAIRS * u + n + 1)
                nc.gpsimd.tensor_tensor(weights[:, n % 4], weights[:, n % 4], x_pair[:, n % 4, ::-1], ALU.mult)\
                  .then_inc(crossed, 1)

            def mask(u, n):
                pool.wait_ge(weighted, PAIRS * u + n + 1)
                diagonal = weights[:, n % 4, :, TP:2 * TP]
                nc.gpsimd.tensor_tensor(diagonal, diagonal, over(causal[:], [TP, 2, TP]), ALU.mult)\
                  .then_inc(masked, 1)

            def turn(kind, u, prior, slot):
                pairs, has_next, has_prev = parts_of(kind)
                for n in range(PAIRS):
                    if pairs:
                        cross(u, n)
                    if n >= 1 and pairs:
                        mask(u, n - 1)
                    if n == 0 and has_prev:
                        mask(u - 1, PAIRS - 1)
                    if n == 1 and has_next:
                        root(0, root_number(kind, u, 0))
                    if n == 8 and has_prev:
                        root(1, root_number(kind, u, 1))

            turns(pool, turn)

        @block.tensor
        def _(pe):
            pe.wait_ge(consts_in, 16 * len(constants))
            pe.wait_ge(presets, 5)
            tok_w = w_tok[:].rearrange("p (k n) -> p k n", k=KP)
            qkv_w = w_qkv[:].rearrange("p (k n) -> p k n", k=2)
            proj_w = w_proj[:].rearrange("p (k n) -> p k n", k=2)
            route_w = w_route[:].rearrange("p (k n) -> p k n", k=2)

            def turn(kind, u, prior, slot):
                prev = 1 - slot
                pairs, has_next, has_prev = parts_of(kind)

                def room(pos):
                    before = fills(kind, u, pos) - 1
                    if kind != "pro" or before > 0:
                        pe.wait_ge(free[pos % NB], before)
                    return bank[pos % NB]

                def copied(jobs):
                    for pos in jobs[-NB:]:
                        pe.wait_ge(free[pos % NB], fills(kind, u, pos))

                def transposed(jobs, src):
                    for k, pos in enumerate(jobs):
                        out = room(pos)
                        for t in range(4):
                            last = nc.tensor.transpose(out[0:KD, t * TP:(t + 1) * TP],
                                                       src[:, t, k * KD:(k + 1) * KD], ident[:])
                        last.then_inc(full[pos % NB], 1)

                def product(out, lhs, rhs, width):
                    for k in range(2):
                        last = nc.tensor.matmul(out, lhs[:, k, :], rhs[:, k, 0:width], start=(k == 0), stop=(k == 1))
                    return last

                def tile(x, t):
                    return x[:, :, t * TP:(t + 1) * TP]

                for n in range(PAIRS):
                    if pairs:
                        scores(kind, u, n, qk_t[slot])
                        if n >= LAG:
                            attend(kind, u, n - LAG, v[slot])
                    if n < LAG and has_prev:
                        attend("mid", u - 1, n - LAG + PAIRS, v[prev])
                    if n in (0, 1) and has_next:
                        if n == 0:
                            pe.wait_ge(patches_in[prev], 16 * (prior + 2) if kind == "mid" else 16)
                        x = patches[prev][:].rearrange("p (k t) -> p k t", k=KP)
                        out = room(TOK[n])
                        for c in range(2):
                            for i in range(KP):
                                last = nc.tensor.matmul(out[0:TP, c * D:(c + 1) * D],
                                                        x[:, i, (2 * n + c) * TP:(2 * n + c + 1) * TP], tok_w[:, i, :],
                                                        start=(i == 0), stop=(i == KP - 1))
                        last.then_inc(full[TOK[n] % NB], 1)
                    if n == 4 and has_next:
                        pe.wait_ge(normed_ready, 4 * u + 8)
                        transposed(LN1T, normed)
                    if n == 5 and has_prev:
                        pe.wait_ge(y_ready, 2 * u)
                        transposed(YT, y[:].rearrange("p t h d -> p t (h d)"))
                    if n in (6, 7) and has_next:
                        if n == 6:
                            copied(LN1T)
                        for t in range(2 * n - 12, 2 * n - 10):
                            out = room(QK[t])
                            product(out[0:TP, 0:2 * D], tile(normed_t, t), qkv_w, 2 * D).then_inc(full[QK[t] % NB], 1)
                        pos = VV[n - 6]
                        out = room(pos)
                        for c in range(2):
                            last = product(out[0:TP, c * D:(c + 1) * D], tile(normed_t, 2 * (n - 6) + c),
                                           qkv_w[:, :, 2 * D:3 * D], D)
                        last.then_inc(full[pos % NB], 1)
                    if n == 8 and has_prev:
                        copied(YT)
                        for k, pos in enumerate(PROJ):
                            out = room(pos)
                            for c in range(2):
                                last = product(out[0:TP, c * D:(c + 1) * D], tile(y_t, 2 * k + c), proj_w, D)
                            last.then_inc(full[pos % NB], 1)
                    if n >= 9 and has_next:
                        if n == 9:
                            pe.wait_ge(roped, 4 * u + 8)
                        for g in range(2 * n - 18, 2 * n - 16):
                            out = room(QKT[g])
                            for t in range(4):
                                src = qk[:, t, 4 * g:4 * g + 4, :].rearrange("p h d -> p (h d)")
                                last = nc.tensor.transpose(out[:, t * TP:(t + 1) * TP], src, ident[:])
                            last.then_inc(full[QKT[g] % NB], 1)
                    if n == 11 and has_prev:
                        pe.wait_ge(x2_ready, 4 * u)
                        for pos, turn_part in zip(X2T, (turn_near, turn_far)):
                            out = room(pos)
                            for t in range(4):
                                last = turn_part(nc, out[:, t * TP:(t + 1) * TP], x2[prev][:, t, :], ident[:])
                            last.then_inc(full[pos % NB], 1)
                        copied(X2T)
                        out = room(ROUTE[0])
                        x = x2_t[prev][:].rearrange("p (k t) -> p k t", k=2)
                        for t in range(4):
                            logit = out[0:TP, t * E:(t + 1) * E]
                            nc.tensor.matmul(logit, tile(x, t)[:, 0], route_w[:, 0], start=True, stop=False)
                            last = nc.tensor.matmul(logit, tile(x, t)[0:D - 128, 1], route_w[0:D - 128, 1],
                                                    start=False, stop=True)
                        last.then_inc(full[ROUTE[0] % NB], 1)
                if has_next:
                    copied(QKT)

            def scores(kind, u, n, qk_t):
                image, at = n // (PAIRS // 2), 2 * (n % (PAIRS // 2))
                if kind != "first" or n >= 2:
                    pe.wait_ge(copied_out, PAIRS * u + n - 1)
                for c, head in enumerate((at, at + 1)):
                    p = HP * (head % 4)
                    q = qk_t[p:p + HD + 1, head // 4, 2 * image * TP:(2 * image + 2) * TP]
                    k = qk_t[p:p + HD + 1, 3 + head // 4, 2 * image * TP:(2 * image + 2) * TP]
                    out = score[n % 2][0:TP, c, :]
                    near = out[:, 0:3 * TP].rearrange("p (c s) -> p c s", c=3)[:, 0:3:2, :]
                    nc.tensor.matmul(near, k[:, 0:TP], q.rearrange("p (c s) -> p c s", c=2), start=True, stop=True)
                    last = nc.tensor.matmul(out[:, TP:2 * TP], k[:, TP:2 * TP], q[:, TP:2 * TP], start=True,
                                            stop=True)
                last.then_inc(scored, 1)

            def attend(kind, u, n, v):
                image, at = n // (PAIRS // 2), 2 * (n % (PAIRS // 2))
                pe.wait_ge(floored, PAIRS * u + n + 1)
                pe.wait_ge(masked, PAIRS * u + n + 1)
                if at == 0 and kind != "first":
                    pe.wait_ge(y_ready, 2 * u + image - 1)
                out = y_sum[image][0:TP, 0:2 * NH * VW].rearrange("p (t h d) -> p t h d", t=2, d=VW)
                for c, head in enumerate((at, at + 1)):
                    w = weights[:, n % 4, c]
                    near, far = v[:, 2 * image, head, :], v[:, 2 * image + 1, head, :]
                    nc.tensor.matmul(out[:, 0, head, :], w[:, 0:TP], near, start=True, stop=True)
                    nc.tensor.matmul(out[:, 1, head, :], w[:, 2 * TP:3 * TP], near, start=True, stop=False)
                    last = nc.tensor.matmul(out[:, 1, head, :], w[:, TP:2 * TP], far, start=False, stop=True)
                last.then_inc(attended, 1)

            turns(pe, turn)


def routing(nc, dram, logits, slot_of, weight_of):
    BITS = 30
    with ExitStack() as ctx:
        def sb(name, shape, dt=F32):
            return ctx.enter_context(nc.sbuf_tensor(name, shape, dt))

        def sem(name):
            return ctx.enter_context(nc.semaphore(name))

        full3 = [TP, TILES, E]
        probs, first, second, keep, key, scratch = (
            sb(n, full3) for n in ("probs", "first_choice", "second_choice", "keep", "key", "scratch"))
        ones_row = sb("ones_row", [TP, TILES])
        tile_sums = sb("tile_sums", full3)
        running = sb("running", full3)
        top, norm, best, w1, w2 = (sb(n, [TP, TILES]) for n in ("top", "norm", "best", "w1", "w2"))
        before = sb("before", [TP, TP])
        ones = sb("ones", [TP, TP])
        rank = sb("rank", [TP, E])
        base = sb("base", [TP, E])
        bits = sb("bits", [TP, BITS * E], I32)
        floor = sb("floor", [TP, E], I32)
        trial = sb("trial", [TP, E], I32)
        enough = sb("enough", [TP, E], I32)
        count = sb("count", [TP, E])
        room = sb("room", [TP, E])
        total = ctx.enter_context(nc.psum_tensor("total", [128, 512], F32))
        in_tile = ctx.enter_context(nc.psum_tensor("in_tile", [128, 2, 512], F32))
        of_tile = ctx.enter_context(nc.psum_tensor("of_tile", [128, 2, 512], F32))
        consts_in, shifted, powered, vec, counted, totalled, marked, summed, spacer = map(sem, (
            "route_consts_in", "shifted", "powered", "route_steps", "counted", "totalled", "marked", "prefix_summed", "route_spacer"))
        block = ctx.enter_context(nc.Block())
        constants = ((before, "before"), (ones, "ones"), (rank, "rank"), (base, "base"), (bits, "bits"))

        @block.sync
        def _(sp):
            for dst, src in constants:
                sp.dma_start(dst[:], dram[src]).then_inc(consts_in, 16)

        @block.scalar
        def _(act):
            act.wait_ge(shifted, 1)
            nc.scalar.activation(probs[:], probs[:], ACT.Exp).then_inc(powered, 1)

        @block.tensor
        def _(pe):
            pe.wait_ge(consts_in, 16 * len(constants))
            with pe.Fori(0, BITS + 1) as i:
                pe.wait_ge(counted, i + 1)
                nc.tensor.matmul(total[0:TP, 0:E], ones[:], count[:], start=True, stop=True).then_inc(totalled, 1)
            for n in range(2):
                pe.wait_ge(marked, n + 1)
                src = (key, keep)[n][:].rearrange("p t e -> p (t e)").rearrange("p (c x) -> p c x", c=2)
                for out, mat in ((in_tile, before), (of_tile, ones)):
                    for c in range(2):
                        last = nc.tensor.matmul(out[0:TP, c, :], mat[:], src[:, c, :], start=True, stop=True)
                last.then_inc(summed, 1)

        @block.vector
        def _(dve):
            chain = Tally()

            def step(ins):
                chain.step(ins, vec)
                dve.wait_ge(vec, chain.value)

            def tt(out, a, b, op):
                step(nc.vector.tensor_tensor(out, a, b, op))

            def ts(out, a, s1, s2, op0, op1=None):
                step(nc.vector.tensor_scalar(out, a, s1, s2, op0, op1) if op1 is not None
                     else nc.vector.tensor_scalar(out, a, s1, None, op0))

            def per_tile(x):
                return x[:].unsqueeze(2).to_broadcast(full3)

            def per_expert(x):
                return x.unsqueeze(1).to_broadcast(full3)

            def by_expert(x):
                return x[:].rearrange("p t e -> p e t")

            def choose(out, top):
                step(nc.vector.tensor_reduce(top[:], probs[:], AX.X, ALU.max))
                tt(out[:], probs[:], per_tile(top), ALU.is_equal)
                tt(out[:], out[:], per_expert(rank[:]), ALU.mult)
                step(nc.vector.tensor_reduce(best[:], out[:], AX.X, ALU.max))
                tt(out[:], out[:], per_tile(best), ALU.is_equal)

            def prefix(n, src):
                dve.wait_ge(summed, n + 1)
                flat = tile_sums[:].rearrange("p t e -> p (t e)").rearrange("p (c x) -> p c x", c=2)
                step(nc.vector.tensor_copy(flat, of_tile[0:TP]))
                for e in range(E):
                    step(nc.vector.tensor_tensor_scan(running[:, :, e], ones_row[:], tile_sums[:, :, e], 0.0,
                                                      ALU.mult, ALU.add))
                tt(running[:], running[:], tile_sums[:], ALU.subtract)
                flat = running[:].rearrange("p t e -> p (t e)").rearrange("p (c x) -> p c x", c=2)
                tt(flat, flat, in_tile[0:TP], ALU.add)

            dve.wait_ge(consts_in, 16 * len(constants))
            step(nc.vector.memset(ones_row[:], 1.0))
            step(nc.vector.memset(floor[:], 0))
            view = logits[:].rearrange("p (t e) -> p t e", e=E)
            step(nc.vector.tensor_reduce(top[:], view, AX.X, ALU.max))
            nc.vector.tensor_tensor(probs[:], view, per_tile(top), ALU.subtract).then_inc(shifted, 1)
            dve.wait_ge(powered, 1)
            step(nc.vector.tensor_reduce(norm[:], probs[:], AX.X, ALU.add))
            step(nc.vector.reciprocal(norm[:], norm[:]))
            tt(probs[:], probs[:], per_tile(norm), ALU.mult)
            choose(first, w1)
            step(nc.vector.scalar_tensor_tensor(probs[:], first[:], -2.0, probs[:], ALU.mult, ALU.add))
            choose(second, w2)
            tt(norm[:], w1[:], w2[:], ALU.add)
            ts(norm[:], norm[:], 1e-9, None, ALU.max)
            step(nc.vector.reciprocal(norm[:], norm[:]))
            tt(w1[:], w1[:], norm[:], ALU.mult)
            tt(w2[:], w2[:], norm[:], ALU.mult)
            shares = weight_of[:].rearrange("p (t c) -> p t c", c=2)
            step(nc.vector.tensor_copy(shares[:, :, 0], w1[:]))
            step(nc.vector.tensor_copy(shares[:, :, 1], w2[:]))
            tt(key[:], first[:], per_tile(w1), ALU.mult)
            tt(scratch[:], second[:], per_tile(w2), ALU.mult)
            tt(key[:], key[:], scratch[:], ALU.add)
            tt(scratch[:], first[:], second[:], ALU.add)
            step(nc.vector.scalar_tensor_tensor(key[:], scratch[:], -1.0, key[:], ALU.add, ALU.add))

            with dve.Fori(0, BITS) as i:
                chain.enter(i, 4)
                tt(trial[:], floor[:], bits[:, bass.ds(i * E, E)], ALU.bitwise_or)
                tt(scratch[:], key[:], per_expert(trial[:].bitcast(F32)), ALU.is_ge)
                nc.vector.tensor_reduce(count[:], by_expert(scratch), AX.X, ALU.add).then_inc(counted, 1)
                dve.wait_ge(totalled, i + 1)
                step(nc.vector.tensor_scalar(enough[:], total[0:TP, 0:E], float(CAP), None, ALU.is_ge))
                dve.sem_inc(spacer, 1)
                step(nc.vector.copy_predicated(floor[:], enough[:], trial[:]))
            chain.leave(BITS)

            level = per_expert(floor[:].bitcast(F32))
            tt(scratch[:], key[:], level, ALU.is_gt)
            nc.vector.tensor_reduce(count[:], by_expert(scratch), AX.X, ALU.add).then_inc(counted, 1)
            dve.wait_ge(totalled, BITS + 1)
            ts(room[:], total[0:TP, 0:E], -1.0, float(CAP), ALU.mult, ALU.add)
            nc.vector.tensor_tensor(key[:], key[:], level, ALU.is_equal).then_inc(marked, 1)
            prefix(0, key)
            tt(running[:], running[:], per_expert(room[:]), ALU.is_lt)
            tt(running[:], running[:], key[:], ALU.mult)
            nc.vector.tensor_tensor(keep[:], running[:], scratch[:], ALU.add).then_inc(marked, 1)
            prefix(1, keep)
            tt(running[:], running[:], per_expert(base[:]), ALU.add)
            tt(running[:], running[:], keep[:], ALU.mult)
            slots = slot_of[:].rearrange("p (t c) -> p t c", c=2)
            for c, choice in enumerate((first, second)):
                tt(scratch[:], choice[:], running[:], ALU.mult)
                step(nc.vector.tensor_reduce(best[:], scratch[:], AX.X, ALU.add))
                ts(slots[:, :, c], best[:], float(SLOTS), None, ALU.add)


TOKEN_SCALE, WEIGHT_SCALE, HIDDEN_SCALE = 2.0 ** 6, 2.0 ** 6, 2.0 ** 4


def ffn_tensors(ctx, nc, of, slots):
    def sb(name, shape, dt=F32):
        return ctx.enter_context(nc.sbuf_tensor(f"{of}_{name}", shape, dt))

    def sem(name):
        return ctx.enter_context(nc.semaphore(f"{of}_{name}"))

    class T:
        pass

    T.raw = [sb(f"raw{n}", [128, 2 * INNER]) for n in (1, 3)] + [sb("raw2", [128, MI * D])]
    T.w_hi = [[sb(f"w{n}_hi{s}", [128, 2 * INNER], F16) for n in (1, 3)] + [sb(f"w2_hi{s}", [128, MI * D], F16)]
              for s in range(slots)]
    T.w_lo = [[sb(f"w{n}_lo{s}", [128, 2 * INNER], F16) for n in (1, 3)] + [sb(f"w2_lo{s}", [128, MI * D], F16)]
              for s in range(slots)]
    T.tokens_near_hi = sb("tokens_near_hi", [128, UT], F16)
    T.tokens_near_lo = sb("tokens_near_lo", [128, UT], F16)
    T.tokens_far = sb("tokens_far", [128, UT], F16)
    T.silu = sb("silu", [128, 2, UT])
    T.hidden = sb("hidden", [128, 2, UT])
    T.hidden_hi = [sb(f"hidden_hi{s}", [128, MI, UT], F16) for s in range(2)]
    T.hidden_lo = [sb(f"hidden_lo{s}", [128, MI, UT], F16) for s in range(2)]
    T.gate, T.up, T.out = (
        [ctx.enter_context(nc.psum_tensor(f"{of}_{name}{b}", [128, 512], F32)) for b in range(2)]
        for name in ("gate", "up", "out"))
    (T.gated, T.silued, T.multiplied, T.hi_ready, T.lo_ready, T.out_full, T.out_used, T.tokens_hi, T.tokens_lo,
     T.weights_hi, T.weights_lo) = map(sem, (
         "gated", "silued", "multiplied", "hi_ready", "lo_ready", "out_full", "out_used", "tokens_hi", "tokens_lo",
         "weights_hi", "weights_lo"))
    return T


def weights_hi(nc, T, ws):
    for raw, hi in zip(T.raw, T.w_hi[ws]):
        nc.scalar.activation(hi[:], raw[:], ACT.Copy, scale=WEIGHT_SCALE).then_inc(T.weights_hi, 1)


def weights_lo(nc, T, ws):
    for raw, hi, lo in zip(T.raw, T.w_hi[ws], T.w_lo[ws]):
        nc.vector.scalar_tensor_tensor(lo[:], raw[:], WEIGHT_SCALE, hi[:], ALU.mult, ALU.subtract)\
          .then_inc(T.weights_lo, 1)


def tokens_hi(nc, T, near, far):
    nc.scalar.activation(T.tokens_near_hi[:], near, ACT.Copy, scale=TOKEN_SCALE).then_inc(T.tokens_hi, 1)
    nc.scalar.activation(T.tokens_far[:], far, ACT.Copy, scale=TOKEN_SCALE).then_inc(T.tokens_hi, 1)


def tokens_lo(nc, dve, T, g, near, far):
    dve.wait_ge(T.tokens_hi, 2 * g + 2)
    nc.vector.scalar_tensor_tensor(T.tokens_near_lo[:], near, TOKEN_SCALE, T.tokens_near_hi[:],
                                   ALU.mult, ALU.subtract).then_inc(T.tokens_lo, 1)
    nc.vector.scalar_tensor_tensor(T.tokens_far[D - 128:128], far, TOKEN_SCALE, T.tokens_far[D - 128:128],
                                   ALU.mult, ALU.subtract).then_inc(T.tokens_lo, 1)


def units_of(eng, count, first, half, unit):
    unit(first, half, 0, "first")
    with eng.Fori(0, count // 2 - 1) as j:
        unit(first + 2 * j + 1, half + j, 1, "mid")
        unit(first + 2 * j + 2, half + j + 1, 0, "mid")
    unit(first + count - 1, half + count // 2 - 1, 1, "last")


def pairs_of_units(eng, unit):
    unit(0, 0, 0)
    unit(1, 0, 1)
    with eng.Fori(1, UNITS // 2) as half:
        unit(2 * half, half, 0)
        unit(2 * half + 1, half, 1)


def tensor_unit(nc, pe, T, g, ws):
    pe.wait_ge(T.tokens_lo, 2 * g + 6)
    for m in range(MI):
        pe.wait_ge(T.multiplied, MI * g + m + 1)
        near = slice(m * 128, (m + 1) * 128)
        far = slice(INNER + m * 128, INNER + (m + 1) * 128)
        for out, hi, lo in ((T.gate[m % 2], T.w_hi[ws][0], T.w_lo[ws][0]), (T.up[m % 2], T.w_hi[ws][1], T.w_lo[ws][1])):
            out = out[:, 0:UT]
            nc.tensor.matmul(out, hi[:, near], T.tokens_near_hi[:], start=True, stop=False)
            nc.tensor.matmul(out, hi[:, near], T.tokens_near_lo[:], start=False, stop=False)
            nc.tensor.matmul(out, lo[:, near], T.tokens_near_hi[:], start=False, stop=False)
            nc.tensor.matmul(out, hi[:, far], T.tokens_far[:], start=False, stop=False)
            last = nc.tensor.matmul(out, lo[0:D - 128, far], T.tokens_far[0:D - 128], start=False, stop=True)
        last.then_inc(T.gated, 1)


def tensor_out(nc, pe, T, g, slot, ws):
    pe.wait_ge(T.lo_ready, MI * g + MI + 2)
    w_hi, w_lo = (w[ws][2][:].rearrange("p (m n) -> p m n", m=MI) for w in (T.w_hi, T.w_lo))
    for n in range(2):
        pe.wait_ge(T.out_used, 2 * g + n + 1)
        for c in range(2):
            tokens = slice((2 * n + c) * TP, (2 * n + c + 1) * TP)
            out = T.out[n][0:TP, c * D:(c + 1) * D]
            for m in range(MI):
                hi, lo = T.hidden_hi[slot][:, m, tokens], T.hidden_lo[slot][:, m, tokens]
                nc.tensor.matmul(out, hi, w_hi[:, m, :], start=(m == 0), stop=False)
                nc.tensor.matmul(out, hi, w_lo[:, m, :], start=False, stop=False)
                last = nc.tensor.matmul(out, lo, w_hi[:, m, :], start=False, stop=(m == MI - 1))
        last.then_inc(T.out_full, 1)


def scalar_unit(nc, act, T, g, slot):
    def hi(m):
        act.wait_ge(T.multiplied, MI * g + m + 3)
        nc.scalar.copy(T.hidden_hi[slot][:, m, :], T.hidden[:, m % 2, :]).then_inc(T.hi_ready, 1)

    for m in range(MI):
        act.wait_ge(T.gated, MI * g + m + 1)
        act.wait_ge(T.multiplied, MI * g + m + 1)
        nc.scalar.activation(T.silu[:, m % 2, :], T.gate[m % 2][:, 0:UT], ACT.Silu,
                             scale=1.0 / (TOKEN_SCALE * WEIGHT_SCALE)).then_inc(T.silued, 1)
        if m:
            hi(m - 1)
    hi(MI - 1)


def vector_unit(nc, dve, T, g, slot):
    def lo(m):
        dve.wait_ge(T.hi_ready, MI * g + m + 1)
        nc.vector.tensor_tensor(T.hidden_lo[slot][:, m, :], T.hidden[:, m % 2, :], T.hidden_hi[slot][:, m, :],
                                ALU.subtract).then_inc(T.lo_ready, 1)

    for m in range(MI):
        dve.wait_ge(T.silued, MI * g + m + 1)
        dve.wait_ge(T.lo_ready, MI * g + m + 1)
        nc.vector.scalar_tensor_tensor(T.hidden[:, m % 2, :], T.up[m % 2][:, 0:UT],
                                       HIDDEN_SCALE / (TOKEN_SCALE * WEIGHT_SCALE), T.silu[:, m % 2, :],
                                       ALU.mult, ALU.mult).then_inc(T.multiplied, 1)
        if m:
            lo(m - 1)
    lo(MI - 1)


def shared(nc, dram, slot_of):
    with ExitStack() as ctx:
        def sb(name, shape, dt=F32):
            return ctx.enter_context(nc.sbuf_tensor(name, shape, dt))

        def sem(name):
            return ctx.enter_context(nc.semaphore(name))

        T = ffn_tensors(ctx, nc, "shared", 1)
        x_t = [sb(f"x_t{s}", [128, 2 * UT]) for s in range(2)]
        rows = [sb(f"rows{s}", [TP, 4, D]) for s in range(2)]
        sums = [sb(f"sums{s}", [TP, 4, D]) for s in range(2)]
        sent = [sb(f"sent{s}", [TP, 4, D]) for s in range(2)]
        index = [sb(f"index{s}", [TP, 8], U32) for s in range(2)]
        weights_in = sem("shared_in")
        xt_in, rows_in, sums_out, sent_in, scattered = (
            [sem(f"{n}{s}") for s in range(2)] for n in ("xt_in", "rows_in", "sums_out", "sent_in", "scattered"))
        indexed, spacer = sem("indexed"), sem("scatter_spacer")
        block = ctx.enter_context(nc.Block())

        @block.sync
        def _(sp):
            for dst, src in zip(T.raw, ("w1", "w3", "w2")):
                sp.dma_start(dst[:], dram[src][E * 128:(E + 1) * 128, :]).then_inc(weights_in, 16)

            def unit(g, half, slot):
                sp.wait_ge(T.tokens_lo, 2 * g + 2)
                sp.dma_start(x_t[slot][:], dram["x2_t"][bass.ds(g * 128, 128), :]).then_inc(xt_in[slot], 16)
                sp.wait_ge(T.out_used, 2 * g)
                sp.dma_start(rows[slot][:], unit_rows(dram["h2"], g)).then_inc(rows_in[slot], 16)
                sp.wait_ge(scattered[slot], 128 * half)
                sp.dma_start(sent[slot][:], unit_rows(dram["x2"], g)).then_inc(sent_in[slot], 16)

            pairs_of_units(sp, unit)

        @block.gpsimd
        def _(pool):
            def unit(g, half, slot):
                pool.wait_ge(scattered[slot], 128 * half)
                pool.sem_inc(spacer, 1)
                nc.gpsimd.tensor_copy(index[slot][:], slot_of[:, bass.ds(g * 8, 8)]).then_inc(indexed, 1)
                pool.wait_ge(indexed, g + 1)
                pool.wait_ge(sent_in[slot], 16 * half + 16)
                pool.sem_inc(spacer, 1)
                for t in range(4):
                    for c in range(2):
                        nc.gpsimd.indirect_dma_start(
                            out=dram["slots"][:, :],
                            out_offset=bass.IndirectOffsetOnAxis(ap=index[slot][:, 2 * t + c:2 * t + c + 1], axis=0),
                            in_=sent[slot][:, t, :], in_offset=None, bounds_check=SLOTS - 1, oob_is_err=False)\
                          .then_inc(scattered[slot], 16)

            pairs_of_units(pool, unit)
            for s in range(2):
                pool.wait_ge(scattered[s], 128 * (UNITS // 2))

        @block.tensor
        def _(pe):
            pe.wait_ge(T.weights_lo, 3)

            def unit(g, half, slot, place):
                tensor_unit(nc, pe, T, g, 0)
                if place != "first":
                    tensor_out(nc, pe, T, g - 1, 1 - slot, 0)

            units_of(pe, UNITS, 0, 0, unit)
            tensor_out(nc, pe, T, UNITS - 1, 1, 0)

        @block.scalar
        def _(act):
            def store(g, slot):
                act.wait_ge(T.out_used, 2 * g + 4)
                act.dma_start(unit_rows(dram["h2"], g), sums[slot][:]).then_inc(sums_out[slot], 16)

            def split(g, half, slot):
                act.wait_ge(xt_in[slot], 16 * half + 16)
                tokens_hi(nc, T, x_t[slot][:, 0:UT], x_t[slot][:, UT:2 * UT])

            act.wait_ge(weights_in, 48)
            weights_hi(nc, T, 0)
            split(0, 0, 0)

            def unit(g, half, slot, place):
                scalar_unit(nc, act, T, g, slot)
                if place != "last":
                    split(g + 1, half + slot, 1 - slot)
                if place != "first":
                    store(g - 1, 1 - slot)

            units_of(act, UNITS, 0, 0, unit)
            store(UNITS - 1, 1)
            for s in range(2):
                act.wait_ge(sums_out[s], 16 * (UNITS // 2 + 1))

        @block.vector
        def _(dve):
            for primed in (T.multiplied, T.lo_ready, T.out_used):
                dve.sem_inc(primed, 2)
            dve.sem_inc(T.tokens_lo, 4)
            for s in range(2):
                dve.sem_inc(sums_out[s], 16)
            dve.wait_ge(T.weights_hi, 3)
            weights_lo(nc, T, 0)

            def split(g, slot):
                tokens_lo(nc, dve, T, g, x_t[slot][:, 0:UT], x_t[slot][D - 128:128, UT:2 * UT])

            split(0, 0)

            def add(g, half, slot):
                dve.wait_ge(rows_in[slot], 16 * half + 16)
                dve.wait_ge(sums_out[slot], 16 * half + 16)
                for n in range(2):
                    dve.wait_ge(T.out_full, 2 * g + n + 1)
                    nc.vector.scalar_tensor_tensor(
                        sums[slot][:, 2 * n:2 * n + 2, :],
                        T.out[n][0:TP, 0:2 * D].rearrange("p (t d) -> p t d", t=2),
                        1.0 / (HIDDEN_SCALE * WEIGHT_SCALE), rows[slot][:, 2 * n:2 * n + 2, :],
                        ALU.mult, ALU.add).then_inc(T.out_used, 1)

            def unit(g, half, slot, place):
                vector_unit(nc, dve, T, g, slot)
                if place != "last":
                    split(g + 1, 1 - slot)
                if place != "first":
                    add(g - 1, half - (1 - slot), 1 - slot)

            units_of(dve, UNITS, 0, 0, unit)
            add(UNITS - 1, UNITS // 2 - 1, 1)


def experts(nc, dram):
    with ExitStack() as ctx:
        def sb(name, shape, dt=F32):
            return ctx.enter_context(nc.sbuf_tensor(name, shape, dt))

        def sem(name):
            return ctx.enter_context(nc.semaphore(name))

        T = ffn_tensors(ctx, nc, "experts", 2)
        rows = [sb(f"tokens{s}", [TP, 4, D]) for s in range(2)]
        done = [sb(f"done{s}", [TP, 4, D]) for s in range(2)]
        ident = sb("ident2", [TP, TP])
        turned = [ctx.enter_context(nc.psum_tensor(f"turned{k}", [128, 512], F32)) for k in range(2)]
        ident_in, turned_full, weights_in = map(sem, ("ident_in", "turned_full", "weights_in"))
        rows_in, stored = ([sem(f"{n}{s}") for s in range(2)] for n in ("tokens_in", "stored"))
        block = ctx.enter_context(nc.Block())

        def passes(eng, expert):
            with eng.Fori(0, E // 2) as pair:
                expert(2 * pair, 0)
                expert(2 * pair + 1, 1)

        @block.sync
        def _(sp):
            sp.dma_start(ident[:], dram["ident"]).then_inc(ident_in, 16)

            def load(e):
                for dst, src in zip(T.raw, ("w1", "w3", "w2")):
                    sp.dma_start(dst[:], dram[src][bass.ds(e * 128, 128), :]).then_inc(weights_in, 16)

            load(0)

            def expert(e, ws):
                def unit(g, half, slot, place):
                    sp.wait_ge(T.tokens_lo, 2 * g + 2)
                    sp.dma_start(rows[slot][:], unit_rows(dram["slots"], g)).then_inc(rows_in[slot], 16)
                    if place == "first":
                        sp.wait_ge(T.weights_lo, 3 * e + 3)
                        load(e + 1)

                units_of(sp, EU, e * EU, e * (EU // 2), unit)

            passes(sp, expert)
            sp.wait_ge(weights_in, 48 * (E + 1))

        @block.tensor
        def _(pe):
            pe.wait_ge(ident_in, 16)

            def expert(e, ws):
                def turn(g, half, slot):
                    pe.wait_ge(rows_in[slot], 16 * half + 16)
                    pe.wait_ge(T.tokens_lo, 2 * g + 4)
                    for t in range(4):
                        src = rows[slot][:, t, :]
                        tokens = slice(t * TP, (t + 1) * TP)
                        turn_near(nc, turned[0][:, tokens], src, ident[:])
                        last = turn_far(nc, turned[1][:, tokens], src, ident[:])
                    last.then_inc(turned_full, 1)

                def unit(g, half, slot, place):
                    if place == "first":
                        turn(g, half, slot)
                        pe.wait_ge(T.weights_lo, 3 * e + 3)
                    tensor_unit(nc, pe, T, g, ws)
                    if place != "last":
                        turn(g + 1, half + slot, 1 - slot)
                    if place != "first":
                        tensor_out(nc, pe, T, g - 1, 1 - slot, ws)

                units_of(pe, EU, e * EU, e * (EU // 2), unit)
                tensor_out(nc, pe, T, e * EU + EU - 1, 1, ws)

            passes(pe, expert)

        @block.scalar
        def _(act):
            def put(g, half, slot):
                act.wait_ge(stored[slot], 16 * half + 16)
                for n in range(2):
                    act.wait_ge(T.out_full, 2 * g + n + 1)
                    nc.scalar.activation(done[slot][:, 2 * n:2 * n + 2, :],
                                         T.out[n][0:TP, 0:2 * D].rearrange("p (t d) -> p t d", t=2),
                                         ACT.Copy, scale=1.0 / (HIDDEN_SCALE * WEIGHT_SCALE)).then_inc(T.out_used, 1)
                act.wait_ge(T.out_used, 2 * g + 4)
                act.dma_start(unit_rows(dram["expert_rows"], g), done[slot][:]).then_inc(stored[slot], 16)

            def split(g):
                act.wait_ge(turned_full, g + 1)
                tokens_hi(nc, T, turned[0][:, 0:UT], turned[1][:, 0:UT])

            act.wait_ge(weights_in, 48)
            weights_hi(nc, T, 0)

            def expert(e, ws):
                def unit(g, half, slot, place):
                    if place == "first":
                        split(g)
                    scalar_unit(nc, act, T, g, slot)
                    if place != "last":
                        split(g + 1)
                    if place == "first":
                        act.wait_ge(weights_in, 48 * e + 96)
                        weights_hi(nc, T, 1 - ws)
                    else:
                        put(g - 1, half - (1 - slot), 1 - slot)

                units_of(act, EU, e * EU, e * (EU // 2), unit)
                put(e * EU + EU - 1, e * (EU // 2) + EU // 2 - 1, 1)

            passes(act, expert)
            for s in range(2):
                act.wait_ge(stored[s], 16 * (E * EU // 2 + 1))

        @block.vector
        def _(dve):
            for primed in (T.multiplied, T.lo_ready, T.out_used):
                dve.sem_inc(primed, 2)
            dve.sem_inc(T.tokens_lo, 4)
            for s in range(2):
                dve.sem_inc(stored[s], 16)
            dve.wait_ge(T.weights_hi, 3)
            weights_lo(nc, T, 0)

            def split(g):
                tokens_lo(nc, dve, T, g, turned[0][:, 0:UT], turned[1][D - 128:128, 0:UT])

            def expert(e, ws):
                def unit(g, half, slot, place):
                    if place == "first":
                        split(g)
                    vector_unit(nc, dve, T, g, slot)
                    if place != "last":
                        split(g + 1)
                    if place == "first":
                        dve.wait_ge(T.weights_hi, 3 * e + 6)
                        weights_lo(nc, T, 1 - ws)

                units_of(dve, EU, e * EU, e * (EU // 2), unit)

            passes(dve, expert)


def combine(nc, dram, slot_of, weight_of):
    with ExitStack() as ctx:
        def sb(name, shape, dt=F32):
            return ctx.enter_context(nc.sbuf_tensor(name, shape, dt))

        def sem(name):
            return ctx.enter_context(nc.semaphore(name))

        rows = [sb(f"base{s}", [TP, 4, D]) for s in range(2)]
        gathered = [sb(f"gathered{s}", [TP, 8, D]) for s in range(2)]
        index = [sb(f"from{s}", [TP, 8], U32) for s in range(2)]
        rows_in, gathered_in, stored = (
            [sem(f"{n}{s}") for s in range(2)] for n in ("base_in", "gathered_in", "out_stored"))
        indexed, combined, spacer = sem("from_indexed"), sem("combined"), sem("gather_spacer")
        block = ctx.enter_context(nc.Block())

        @block.sync
        def _(sp):
            def unit(g, half, slot):
                sp.wait_ge(stored[slot], 16 * half)
                sp.dma_start(rows[slot][:], unit_rows(dram["h2"], g)).then_inc(rows_in[slot], 16)

            pairs_of_units(sp, unit)

        @block.gpsimd
        def _(pool):
            def unit(g, half, slot):
                pool.wait_ge(combined, 8 * g)
                pool.wait_ge(gathered_in[slot], 128 * half)
                pool.sem_inc(spacer, 1)
                nc.gpsimd.tensor_copy(index[slot][:], slot_of[:, bass.ds(g * 8, 8)]).then_inc(indexed, 1)
                pool.wait_ge(indexed, g + 1)
                pool.sem_inc(spacer, 1)
                for n in range(8):
                    nc.gpsimd.indirect_dma_start(
                        out=gathered[slot][:, n, :], out_offset=None, in_=dram["expert_rows"][:, :],
                        in_offset=bass.IndirectOffsetOnAxis(ap=index[slot][:, n:n + 1], axis=0),
                        bounds_check=SLOTS, oob_is_err=False).then_inc(gathered_in[slot], 16)

            pairs_of_units(pool, unit)

        @block.vector
        def _(dve):
            dve.sem_inc(combined, 8)

            def unit(g, half, slot):
                dve.wait_ge(rows_in[slot], 16 * half + 16)
                dve.wait_ge(gathered_in[slot], 128 * half + 128)
                for c in range(2):
                    if c:
                        dve.wait_ge(combined, 8 * g + 12)
                    for t in range(4):
                        nc.vector.scalar_tensor_tensor(
                            rows[slot][:, t, :], gathered[slot][:, 2 * t + c, :],
                            weight_of[:, bass.ds(g * 8 + 2 * t + c, 1)], rows[slot][:, t, :], ALU.mult, ALU.add)\
                          .then_inc(combined, 1)

            pairs_of_units(dve, unit)

        @block.scalar
        def _(act):
            def unit(g, half, slot):
                act.wait_ge(combined, 8 * g + 16)
                act.dma_start(unit_rows(dram["out"], g), rows[slot][:]).then_inc(stored[slot], 16)

            pairs_of_units(act, unit)
            for s in range(2):
                act.wait_ge(stored[s], 16 * (UNITS // 2))


def build(nc, dram):
    with (nc.sbuf_tensor("logits", [TP, TILES * E], F32) as logits,
          nc.sbuf_tensor("slot_of", [TP, TILES * 2], U32) as slot_of,
          nc.sbuf_tensor("weight_of", [TP, TILES * 2], F32) as weight_of):
        attention(nc, dram, logits)
        routing(nc, dram, logits, slot_of, weight_of)
        shared(nc, dram, slot_of)
        experts(nc, dram)
        combine(nc, dram, slot_of, weight_of)


def rope_table():
    half = HD // 2
    freq = (np.float32(1.0) / np.power(np.float32(10000.0), np.arange(half, dtype=np.float32) / np.float32(half)))
    angle = np.arange(S, dtype=np.float32)[:, None] * freq.astype(np.float32)[None, :]
    table = np.stack([np.cos(angle), np.sin(angle)], 1).astype(np.float32)
    return np.ascontiguousarray(table.reshape(2, TP, 2, half).transpose(1, 0, 2, 3).reshape(TP, -1))


def halves(w):
    return np.ascontiguousarray(w.reshape(2, KD, -1).transpose(1, 0, 2).reshape(KD, -1))


def near_far(w):
    return np.concatenate([w[:128], np.concatenate([w[128:], w[128:]])], 1)


def inner_rows(w):
    return np.ascontiguousarray(w.reshape(MI, 128, D).transpose(1, 0, 2).reshape(128, -1))


def layout(x, L0_tok_W, L0_tok_b, L0_attn_Wq, L0_attn_Wk, L0_attn_Wv, L0_attn_Wproj, L0_ffn_Wr, L0_ffn_w1, L0_ffn_w3,
           L0_ffn_w2, L0_ffn_s1, L0_ffn_s3, L0_ffn_s2):
    p = x.reshape(UNITS, 2, GRID, PATCH, GRID, PATCH * 3).transpose(0, 3, 5, 1, 2, 4).reshape(UNITS, KP, 128, UT)
    split = np.arange(D).reshape(NH, HD // 2, 2).transpose(0, 2, 1).reshape(-1)
    qkv = np.concatenate([L0_attn_Wq.T[:, split], L0_attn_Wk.T[:, split], L0_attn_Wv.T], 1)
    return {
        "patches": np.ascontiguousarray(p.transpose(0, 2, 1, 3)).reshape(UNITS * 128, KP * UT),
        "w_tok": np.ascontiguousarray(L0_tok_W.reshape(KP, 128, D).transpose(1, 0, 2)).reshape(128, KP * D),
        "bias": np.ascontiguousarray(np.broadcast_to(L0_tok_b, (TP, D))),
        "w_qkv": halves(qkv),
        "w_proj": halves(np.ascontiguousarray(L0_attn_Wproj.T)),
        "w_route": near_far(L0_ffn_Wr),
        "rope": rope_table(),
        "ident": np.eye(TP, dtype=np.float32),
        "causal": np.triu(np.ones((TP, TP), np.float32)),
        "before": np.triu(np.ones((TP, TP), np.float32), 1),
        "ones": np.ones((TP, TP), np.float32),
        "rank": np.tile(np.arange(E, 0, -1, dtype=np.float32), (TP, 1)),
        "base": np.tile(np.arange(E, dtype=np.float32) * CAP - SLOTS, (TP, 1)),
        "bits": np.tile(np.repeat(1 << np.arange(29, -1, -1, dtype=np.int32), E), (TP, 1)).astype(np.int32),
        "w1": np.concatenate([near_far(w) for w in (*L0_ffn_w1, L0_ffn_s1)]),
        "w3": np.concatenate([near_far(w) for w in (*L0_ffn_w3, L0_ffn_s3)]),
        "w2": np.concatenate([inner_rows(w) for w in (*L0_ffn_w2, L0_ffn_s2)]),
    }


def kernel(**inputs):
    import concourse.bacc as _bacc
    from concourse.bass_utils import run_bass_kernel_spmd as _run

    arrays = layout(**{k: np.asarray(v) for k, v in inputs.items()})
    nc = _bacc.Bacc("TRN2", target_bir_lowering=False, num_devices=1)
    dram = {n: nc.dram_tensor("in_" + n, a.shape, mybir.dt.from_np(a.dtype), kind="ExternalInput").ap()
            for n, a in arrays.items()}
    for n, shape in (("h2", (N, D)), ("x2", (N, D)), ("x2_t", (UNITS * 128, 2 * UT)), ("slots", (SLOTS, D)),
                     ("expert_rows", (SLOTS + 1, D))):
        dram[n] = nc.dram_tensor("dram_" + n, shape, F32, kind="Internal").ap()
    dram["out"] = nc.dram_tensor("out_rows", (N, D), F32, kind="ExternalOutput").ap()
    build(nc, dram)
    r = _run(nc, [{"in_" + n: a for n, a in arrays.items()}], core_ids=[0])
    return r.results[0]["out_rows"].reshape(B, S, D)
```

```python
from contextlib import ExitStack

import numpy as np

import concourse.bass as bass
from concourse import mybir

ALU = mybir.AluOpType
ACT = mybir.ActivationFunctionType
AX = mybir.AxisListType
F32 = mybir.dt.float32
F16 = mybir.dt.float16
U32 = mybir.dt.uint32
I32 = mybir.dt.int32

B, GRID, PATCH = 64, 14, 16
S = GRID * GRID
N = B * S
D, NH, HD = 192, 12, 16
DP = PATCH * PATCH * 3
KP = DP // 128
TP = S // 2
UT = 4 * TP
UNITS = N // UT
TILES = N // TP
E, INNER = 8, 768
MI = INNER // 128
CAP = -(-N * 2 * 5 // (E * 4))
SLOTS = E * CAP
EU = CAP // UT
KD = D // 2
HALF = UNITS // 2
EPS = 1e-5
VW = HD + 1
SCORE_SCALE = float(np.sqrt(2.0)) / 4.0
QK_SCALE = 2.0 ** 5
QW = 64
QR = 3 * HD + 1
GUARD = 2.0 ** -14
FLOOR = 3 * 2.0 ** -24
assert CAP % UT == 0 and UNITS % 2 == 0


VECTOR_STEPS = 74


class Tally:

    def __init__(self):
        self.base, self.n = 0, 0

    def step(self, ins, sem):
        self.n += 1
        ins.then_inc(sem, 1)

    @property
    def value(self):
        return self.base + self.n

    def enter(self, j, per):
        self.start, self.per = self.base + self.n, per
        self.base, self.n = self.start + j * per, 0

    def leave(self, trips):
        assert self.n == self.per, (self.n, self.per)
        self.base, self.n = self.start + trips * self.per, 0


TOK, YT, PROJ, LN1T, QK, VV, X2T, ROUTE, QKT = (
    (0, 1), (2, 3), (4, 5), (6, 7), (8, 9, 11, 12), (10, 13), (14, 15), (16,), tuple(range(17, 23)))
NEXT = TOK + LN1T + QK + VV + QKT
PREV = YT + PROJ + X2T + ROUTE
TURNS = {
    "pro": NEXT,
    "first": NEXT,
    "mid": NEXT + PREV,
    "last": PREV,
    "end": PREV,
}
NB = 2
PAIRS = 2 * NH // 2
LAG = 4
ZERO_PARTS = UNITS - 2
assert SLOTS * D % (128 * ZERO_PARTS) == 0


def fills(kind, u, pos):
    def jobs(kind, before=99):
        return sum(1 for p in TURNS[kind] if p % NB == pos % NB and p < before)

    earlier = {"pro": (), "first": ("pro",), "mid": ("pro", "first"), "last": ("pro", "first"),
               "end": ("pro", "first", "last")}[kind]
    count = sum(jobs(k) for k in earlier) + jobs(kind, pos) + 1
    if kind == "mid":
        return count + (u - 1) * jobs("mid")
    return count + ((UNITS - 2) * jobs("mid") if kind in ("last", "end") else 0)


def root_number(kind, u, which):
    if kind in ("pro", "first"):
        return u + 2
    return 2 * u + 1 + which if kind == "mid" else UNITS + u


def parts_of(kind):
    return kind in ("first", "mid", "last"), kind in ("pro", "first", "mid"), kind in ("mid", "last", "end")


def turns(eng, turn):
    turn("pro", -1, 0, 1)
    turn("first", 0, 0, 0)
    with eng.Fori(0, (UNITS - 2) // 2) as j:
        turn("mid", 2 * j + 1, j, 1)
        turn("mid", 2 * j + 2, j, 0)
    turn("last", UNITS - 1, (UNITS - 2) // 2, 1)
    turn("end", UNITS, (UNITS - 1) // 2, 0)


def unit_rows(ap, u):
    return ap[bass.ds(u * UT, UT), :].rearrange("(t p) d -> p t d", p=TP)


def over(ap, shape):
    while ap.ndim < len(shape):
        ap = ap.unsqueeze(1)
    return ap.to_broadcast(shape)


def turn_near(nc, out, rows, ident):
    return nc.tensor.transpose(out, rows[:, 0:128], ident)


def turn_far(nc, out, rows, ident):
    nc.tensor.transpose(out, rows[:, D - 128:D], ident)
    return nc.tensor.transpose(out[0:D - 128], rows[:, 128:D], ident)


def heads_of(qk, a):
    flat = qk.rearrange("p a x -> p (a x)")[:, a * NH * QW:(a + 1) * NH * QW]
    return flat.rearrange("p (h c d) -> p h c d", h=NH, d=HD)


def halfwords(bank):
    return bank[:].bitcast(F16)


def attention(nc, dram, logits):
    with ExitStack() as ctx:
        def sb(name, shape, dt=F32):
            return ctx.enter_context(nc.sbuf_tensor(name, shape, dt))

        def sem(name):
            return ctx.enter_context(nc.semaphore(name))

        def ps(name):
            return ctx.enter_context(nc.psum_tensor(name, [128, 512], F32))

        patches = [sb(f"patches{s}", [128, KP * UT]) for s in range(2)]
        w_tok = sb("w_tok", [128, KP * D])
        bias = sb("bias", [TP, D])
        w_qkv = sb("w_qkv", [KD, 2 * 3 * D])
        w_proj = sb("w_proj", [KD, 2 * D])
        w_route = sb("w_route", [128, 2 * E])
        rope = sb("rope", [TP, 2 * 2 * (HD // 2)])
        ident = sb("ident", [TP, TP])
        ident16 = sb("ident16", [TP, TP], F16)
        causal = sb("causal", [TP, TP])
        zeros = sb("zeros", [128, SLOTS * D // 128 // ZERO_PARTS])
        h_new = sb("h_new", [TP, 4, D])
        h = [sb(f"h{s}", [TP, 4, D]) for s in range(2)]
        normed = sb("normed", [TP, 4, D])
        normed_t = sb("normed_t", [KD, 2, UT])
        qk_raw = sb("qk_raw", [TP, 4, 2 * D])
        by_cos = [sb(f"by_cos{s}", [TP, 2 * NH, 2, HD // 2]) for s in range(2)]
        by_sin = [sb(f"by_sin{s}", [TP, 2 * NH, 2, HD // 2]) for s in range(2)]
        rotated = sb("rotated", [TP, 4, 2 * NH, HD])
        qk = sb("qk", [TP, 4, 2, NH * QW + HD], F16)
        qk_t = [sb(f"qk_t{s}", [128, 12, UT], F16) for s in range(2)]
        v = [sb(f"v{s}", [TP, 4, NH, VW]) for s in range(2)]
        x_pair = sb("x_pair", [TP, 4, 2, 3 * TP])
        weights = sb("weights", [TP, 4, 2, 3 * TP])
        x_product = sb("x_product", [TP, 2, 3 * TP])
        recip = sb("recip", [TP, 2, 3 * TP])
        den = sb("den", [TP, 2, 2 * NH])
        y = sb("y", [TP, 4, NH, HD])
        y_t = sb("y_t", [KD, 2, UT])
        h2 = [sb(f"h2_{s}", [TP, 4, D]) for s in range(2)]
        x2 = [sb(f"x2_{s}", [TP, 4, D]) for s in range(2)]
        x2_t = [sb(f"x2_t{s}", [128, 2 * UT]) for s in range(2)]
        stats = sb("stats", [TP, 2, 4, 6])
        moments = sb("moments", [TP, 2, 4, 2])
        spread = sb("spread", [TP, 2, 4])
        rstd = sb("rstd", [TP, 2, 4])
        minus_half = sb("minus_half", [TP, 4])
        bank = [ps(f"bank{b}") for b in range(NB)]
        score = [ctx.enter_context(nc.psum_tensor(f"score{b}", [128, 2, 512], F32)) for b in range(2)]
        y_sum = [ps(f"y_sum{b}") for b in range(2)]

        consts_in, zeroed, zero_set = sem("consts_in"), sem("zeroed"), sem("zero_set")
        patches_in = [sem(f"patches_in{s}") for s in range(2)]
        full = [sem(f"bank_full{b}") for b in range(NB)]
        free = [sem(f"bank_free{b}") for b in range(NB)]
        names = ("normed_ready roped scored copied_out gelued crossed multiplied_x inverted weighted floored masked attended "
                 "y_ready qk_rotated qk_hi spread_ready rstd_ready x2_ready vector_steps presets spacer biased h_kept")
        (normed_ready, roped, scored, copied_out, gelued, crossed, multiplied_x, inverted, weighted, floored, masked, attended,
         y_ready, qk_rotated, qk_hi, spread_ready, rstd_ready, x2_ready, vec, presets, spacer, biased, h_kept) = (
             map(sem, names.split()))
        rows_out = [sem(f"rows_out{s}") for s in range(2)]
        x2t_out = [sem(f"x2t_out{s}") for s in range(2)]
        block = ctx.enter_context(nc.Block())
        constants = ((w_tok, "w_tok"), (bias, "bias"), (w_qkv, "w_qkv"), (w_proj, "w_proj"),
                     (w_route, "w_route"), (rope, "rope"), (ident, "ident"), (causal, "causal"))

        @block.sync
        def _(sp):
            sp.dma_start(patches[0][:], dram["patches"][0:128, :]).then_inc(patches_in[0], 16)
            for dst, src in constants:
                sp.dma_start(dst[:], dram[src]).then_inc(consts_in, 16)

            def turn(kind, u, prior, slot):
                prev = 1 - slot
                if kind in ("first", "mid"):
                    if kind == "mid":
                        sp.wait_ge(normed_ready, 4 * u)
                    sp.dma_start(patches[prev][:], dram["patches"][bass.ds((u + 1) * 128, 128), :])\
                      .then_inc(patches_in[prev], 16)
                if kind in ("mid", "last", "end"):
                    sp.wait_ge(x2_ready, 4 * u)
                    sp.dma_start(unit_rows(dram["h2"], u - 1), h2[prev][:]).then_inc(rows_out[prev], 16)
                    sp.dma_start(unit_rows(dram["x2"], u - 1), x2[prev][:]).then_inc(rows_out[prev], 16)
                    for pos in X2T:
                        sp.wait_ge(free[pos % NB], fills(kind, u, pos))
                    sp.dma_start(dram["x2_t"][bass.ds((u - 1) * 128, 128), :], x2_t[prev][:])\
                      .then_inc(x2t_out[prev], 16)

            turns(sp, turn)
            for s in range(2):
                sp.wait_ge(rows_out[s], 32 * (UNITS // 2 + 1))
                sp.wait_ge(x2t_out[s], 16 * (UNITS // 2 + 1))

        @block.scalar
        def _(act):
            act.wait_ge(zero_set, 1)
            slots_flat = dram["slots"].rearrange("n d -> (n d)")\
                .rearrange("(p c z) -> p c z", p=128, c=ZERO_PARTS)
            act.dma_start(dram["expert_rows"][SLOTS:SLOTS + 1, :], zeros[0:1, 0:D]).then_inc(zeroed, 16)

            def turn(kind, u, prior, slot):
                prev = 1 - slot
                pairs, has_next, has_prev = parts_of(kind)

                def copy_out(pos, dst, rows, cols=UT):
                    act.wait_ge(full[pos % NB], fills(kind, u, pos))
                    nc.scalar.copy(dst, bank[pos % NB][0:rows, 0:cols]).then_inc(free[pos % NB], 1)

                def copy_out_qk(g):
                    pos = QKT[g]
                    act.wait_ge(full[pos % NB], fills(kind, u, pos))
                    nc.scalar.copy(qk_t[prev][:, 2 * g:2 * g + 2, :],
                                   halfwords(bank[pos % NB])[:, 0:2 * UT].rearrange("p (g t) -> p g t", g=2))\
                      .then_inc(free[pos % NB], 1)

                def copy_scores(u, n, opens):
                    pair = PAIRS * u + n
                    act.wait_ge(scored, pair + 1)
                    if not opens:
                        act.wait_ge(weighted, pair - 3)
                    nc.scalar.activation(x_pair[:, n % 4], score[n % 2][0:TP, :, 0:3 * TP], ACT.Copy,
                                         scale=QK_SCALE ** -2).then_inc(copied_out, 1)

                for n in range(PAIRS):
                    if pairs:
                        if n < PAIRS - 1:
                            copy_scores(u, n + 1, kind == "first" and n < 3)
                        pair = PAIRS * u + n
                        act.wait_ge(copied_out, pair + 1)
                        if kind != "first" or n >= 4:
                            act.wait_ge(attended, pair - 3)
                        nc.scalar.activation(weights[:, n % 4], x_pair[:, n % 4], ACT.Gelu, scale=SCORE_SCALE)\
                          .then_inc(gelued, 1)
                    if n in (1, 3) and has_next:
                        if kind != "pro" and n == 1:
                            act.wait_ge(h_kept, u + 1)
                        copy_out(TOK[n // 2], h_new[:, n - 1:n + 1, :].rearrange("p t d -> p (t d)"), TP, 2 * D)
                    if n == 3 and kind == "mid":
                        act.dma_start(slots_flat[:, bass.ds(u - 1, 1), :], zeros[:].unsqueeze(1)).then_inc(zeroed, 16)
                    if n == 4 and has_prev:
                        for k, pos in enumerate(YT):
                            copy_out(pos, y_t[:, k, :], KD)
                    if n == 5 and has_prev:
                        act.wait_ge(rows_out[prev], 32 * prior + 32)
                        for k, pos in enumerate(PROJ):
                            copy_out(pos, h2[prev][:, 2 * k:2 * k + 2, :].rearrange("p t d -> p (t d)"), TP, 2 * D)
                    if n == 6 and has_next:
                        for k, pos in enumerate(LN1T):
                            copy_out(pos, normed_t[:, k, :], KD)
                    if n in (6, 7) and has_next:
                        for t in range(2 * n - 12, 2 * n - 10):
                            copy_out(QK[t], qk_raw[:, t, :], TP, 2 * D)
                        pos = VV[n - 6]
                        act.wait_ge(full[pos % NB], fills(kind, u, pos))
                        for t in range(2):
                            last = nc.scalar.copy(v[prev][:, 2 * (n - 6) + t, :, 0:HD],
                                                  bank[pos % NB][0:TP, t * D:(t + 1) * D]
                                                  .rearrange("p (h d) -> p h d", h=NH))
                        last.then_inc(free[pos % NB], 1)
                    if n in (8, 9) and has_next:
                        for t in range(2 * n - 16, 2 * n - 14):
                            act.wait_ge(qk_rotated, 4 * u + 5 + t)
                            for a, parts in ((0, slice(0, 3, 2)), (1, slice(0, 2))):
                                src = rotated[:, t, a * NH:(a + 1) * NH, :].unsqueeze(2).to_broadcast([TP, NH, 2, HD])
                                nc.scalar.copy(heads_of(qk[:, t], a)[:, :, parts, :], src).then_inc(qk_hi, 1)
                    if n == 9 and has_prev:
                        act.wait_ge(x2t_out[prev], 16 * prior + 16)
                        for k, pos in enumerate(X2T):
                            copy_out(pos, x2_t[prev][:, k * UT:(k + 1) * UT], 128)
                    if n == 10 and has_next:
                        if has_prev:
                            act.wait_ge(spread_ready, root_number(kind, u, 1))
                        act.wait_ge(biased, u + 2)
                        nc.scalar.copy(h[prev][:], h_new[:]).then_inc(h_kept, 1)
                    if n == 10 and has_prev:
                        pos = ROUTE[0]
                        act.wait_ge(full[pos % NB], fills(kind, u, pos))
                        nc.scalar.copy(logits[:, bass.ds((u - 1) * 4 * E, 4 * E)], bank[pos % NB][0:TP, 0:4 * E])\
                          .then_inc(free[pos % NB], 1)
                    if n == 11 and has_next:
                        for g in range(6):
                            copy_out_qk(g)
                if has_next:
                    copy_scores(u + 1, 0, kind == "pro")

            turns(act, turn)
            act.wait_ge(zeroed, 16 * (ZERO_PARTS + 1))

        @block.vector
        def _(dve):
            chain = Tally()

            def step(ins):
                chain.step(ins, vec)

            def settle():
                dve.wait_ge(vec, chain.value)

            for s in range(2):
                dve.sem_inc(rows_out[s], 32)
                dve.sem_inc(x2t_out[s], 16)
            nc.vector.memset(zeros[:], 0.0).then_inc(zero_set, 1)
            for s in range(2):
                nc.vector.memset(v[s][:], 1.0).then_inc(presets, 1)
            nc.vector.memset(qk[:], 0.0).then_inc(presets, 1)
            dve.wait_ge(presets, 3)
            for t in range(4):
                for a in range(2):
                    nc.vector.memset(heads_of(qk[:, t], a)[:, :, 3, 0:1], GUARD).then_inc(presets, 1)
            nc.vector.memset(minus_half[:], -0.5).then_inc(presets, 1)
            dve.wait_ge(consts_in, 16 * len(constants))
            nc.vector.tensor_copy(ident16[:], ident[:]).then_inc(presets, 1)
            tables = rope[:].rearrange("p (a c f) -> p a c f", a=2, c=2)

            def spread_of(which, src):
                settle()
                for t in range(4):
                    step(nc.vector.bn_stats(stats[:, which, t, :], src[:, t, :]))
                settle()
                dve.sem_inc(spacer, 1)
                for t in range(4):
                    step(nc.vector.bn_aggr(moments[:, which, t, :], stats[:, which, t, :]))
                settle()
                nc.vector.tensor_scalar(spread[:, which, :], moments[:, which, :, 1], EPS, None, ALU.add)\
                  .then_inc(spread_ready, 1)

            def norm(which, nth, src, dst, ready):
                dve.wait_ge(rstd_ready, nth)
                for t in range(4):
                    nc.vector.tensor_scalar(dst[:, t, :], src[:, t, :], moments[:, which, t, 0:1],
                                            rstd[:, which, t:t + 1], ALU.subtract, ALU.mult).then_inc(ready, 1)

            def multiply_x(u, n):
                dve.wait_ge(copied_out, PAIRS * u + n + 1)
                nc.vector.scalar_tensor_tensor(x_product[:, n % 2], x_pair[:, n % 4, 0], SCORE_SCALE / 2,
                                               x_pair[:, n % 4, 1], ALU.mult, ALU.mult).then_inc(multiplied_x, 1)

            def weigh(u, n):
                dve.wait_ge(crossed, PAIRS * u + n + 1)
                dve.wait_ge(inverted, PAIRS * u + n + 1)
                nc.vector.tensor_tensor(weights[:, n % 4], weights[:, n % 4], over(recip[:, n % 2], [TP, 2, 3 * TP]),
                                        ALU.mult).then_inc(weighted, 1)

            def floor(u, n):
                dve.wait_ge(weighted, PAIRS * u + n + 1)
                diagonal = weights[:, n % 4, :, 0:TP]
                nc.vector.scalar_tensor_tensor(diagonal, diagonal, FLOOR, over(causal[:], [TP, 2, TP]),
                                               ALU.max, ALU.mult).then_inc(floored, 1)

            def outputs(u, image):
                sums = y_sum[image][0:TP, 0:2 * NH * VW].rearrange("p (h d) -> p h d", d=VW)
                dve.wait_ge(attended, PAIRS * u + PAIRS // 2 * (image + 1))
                step(nc.vector.tensor_scalar(den[:, 0, :], sums[:, :, HD], 1e-6, None, ALU.max))
                settle()
                step(nc.vector.reciprocal(den[:, 1, :], den[:, 0, :]))
                settle()
                out = y[:, 2 * image:2 * image + 2, :, :].rearrange("p t h d -> p (t h) d")
                nc.vector.tensor_tensor(out, sums[:, :, 0:HD], den[:, 1, :].unsqueeze(2).to_broadcast([TP, 2 * NH, HD]),
                                        ALU.mult).then_inc(y_ready, 1)

            def turn(kind, u, prior, slot):
                prev = 1 - slot
                pairs, has_next, has_prev = parts_of(kind)

                def out_of(jobs):
                    for pos in jobs[-NB:]:
                        dve.wait_ge(free[pos % NB], fills(kind, u, pos))

                for n in range(PAIRS):
                    if pairs:
                        pair = PAIRS * u + n
                        if n < PAIRS - 1:
                            if kind != "first" or n >= 1:
                                dve.wait_ge(inverted, pair)
                            multiply_x(u, n + 1)
                        if n >= 1:
                            weigh(u, n - 1)
                    if n == 0 and has_prev:
                        weigh(u - 1, PAIRS - 1)
                    if pairs:
                        dve.wait_ge(multiplied_x, pair + 1)
                        if kind != "first" or n >= 2:
                            dve.wait_ge(weighted, pair - 1)
                        nc.vector.reciprocal(recip[:, n % 2], x_product[:, n % 2]).then_inc(inverted, 1)
                        if n >= 1:
                            floor(u, n - 1)
                    if n == 0 and has_prev:
                        floor(u - 1, PAIRS - 1)
                    if n == 2 and has_prev:
                        outputs(u - 1, 1)
                    if n == 3 and has_next:
                        out_of(TOK)
                        nc.vector.tensor_tensor(h_new[:], h_new[:], over(bias[:], [TP, 4, D]), ALU.add)\
                          .then_inc(biased, 1)
                        dve.wait_ge(biased, u + 2)
                        spread_of(0, h_new)
                    if n == 4 and has_next:
                        norm(0, root_number(kind, u, 0), h_new, normed, normed_ready)
                    if n == 5 and has_prev:
                        out_of(PROJ)
                        dve.wait_ge(h_kept, u)
                        step(nc.vector.tensor_tensor(h2[prev][:], h2[prev][:], h[prev][:], ALU.add))
                        spread_of(1, h2[prev])
                    if n == 6 and has_prev:
                        norm(1, root_number(kind, u, 1), h2[prev], x2[prev], x2_ready)
                    if n in (6, 7) and has_next:
                        shape = [TP, 2 * NH, 2, HD // 2]
                        for i in range(2):
                            t = 2 * (n - 6) + i
                            dve.wait_ge(free[QK[t] % NB], fills(kind, u, QK[t]))
                            src = qk_raw[:, t, :].rearrange("p (h c f) -> p h c f", h=2 * NH, c=2)
                            if i == 0:
                                settle()
                            step(nc.vector.tensor_tensor(by_cos[i][:], src, over(tables[:, i, 0, :], shape), ALU.mult))
                            step(nc.vector.tensor_tensor(by_sin[i][:], src, over(tables[:, i, 1, :], shape), ALU.mult))
                        settle()
                        for i in range(2):
                            t = 2 * (n - 6) + i
                            step(nc.vector.tensor_tensor(rotated[:, t, :, 0:HD // 2], by_cos[i][:, :, 0, :],
                                                         by_sin[i][:, :, 1, :], ALU.subtract))
                            step(nc.vector.tensor_tensor(rotated[:, t, :, HD // 2:HD], by_cos[i][:, :, 1, :],
                                                         by_sin[i][:, :, 0, :], ALU.add))
                        settle()
                        dve.sem_inc(qk_rotated, 2)
                    if n in (8, 9) and has_next:
                        for t in range(2 * n - 16, 2 * n - 14):
                            dve.wait_ge(qk_hi, 8 * u + 8 + 2 * t + 2)
                            lo = qk[:, t, :, HD:HD + NH * QW].rearrange("p a (h x) -> p a h x", h=NH)[:, :, :, 0:HD]
                            hi = qk[:, t].rearrange("p a x -> p (a x)")[:, 0:2 * NH * QW]\
                                .rearrange("p (a h x) -> p a h x", a=2, h=NH)[:, :, :, 0:HD]
                            src = rotated[:, t].rearrange("p (a h) d -> p a h d", a=2)
                            nc.vector.tensor_tensor(lo, src, hi, ALU.subtract).then_inc(roped, 1)
                    if n == 10 and pairs:
                        outputs(u, 0)
                if has_next:
                    if pairs:
                        dve.wait_ge(inverted, PAIRS * u + PAIRS - 1)
                    multiply_x(u + 1, 0)

            turn("pro", -1, 0, 1)
            turn("first", 0, 0, 0)
            with dve.Fori(0, (UNITS - 2) // 2) as j:
                chain.enter(j, VECTOR_STEPS)
                turn("mid", 2 * j + 1, j, 1)
                turn("mid", 2 * j + 2, j, 0)
            chain.leave((UNITS - 2) // 2)
            turn("last", UNITS - 1, (UNITS - 2) // 2, 1)
            turn("end", UNITS, (UNITS - 1) // 2, 0)

        @block.gpsimd
        def _(pool):
            pool.wait_ge(presets, 13)
            pool.wait_ge(consts_in, 16 * len(constants))

            def root(which, nth):
                pool.wait_ge(spread_ready, nth)
                nc.gpsimd.tensor_tensor(rstd[:, which, :], spread[:, which, :], minus_half[:], ALU.pow)\
                  .then_inc(rstd_ready, 1)

            def cross(u, n):
                pool.wait_ge(gelued, PAIRS * u + n + 1)
                nc.gpsimd.tensor_tensor(weights[:, n % 4], weights[:, n % 4], x_pair[:, n % 4, ::-1], ALU.mult)\
                  .then_inc(crossed, 1)

            def mask(u, n):
                pool.wait_ge(weighted, PAIRS * u + n + 1)
                diagonal = weights[:, n % 4, :, TP:2 * TP]
                nc.gpsimd.tensor_tensor(diagonal, diagonal, over(causal[:], [TP, 2, TP]), ALU.mult)\
                  .then_inc(masked, 1)

            def turn(kind, u, prior, slot):
                pairs, has_next, has_prev = parts_of(kind)
                for n in range(PAIRS):
                    if pairs:
                        cross(u, n)
                    if n >= 1 and pairs:
                        mask(u, n - 1)
                    if n == 0 and has_prev:
                        mask(u - 1, PAIRS - 1)
                    if n == 3 and has_next:
                        root(0, root_number(kind, u, 0))
                    if n == 5 and has_prev:
                        root(1, root_number(kind, u, 1))

            turns(pool, turn)

        @block.tensor
        def _(pe):
            pe.wait_ge(consts_in, 16 * len(constants))
            pe.wait_ge(presets, 13)
            tok_w = w_tok[:].rearrange("p (k n) -> p k n", k=KP)
            qkv_w = w_qkv[:].rearrange("p (k n) -> p k n", k=2)
            proj_w = w_proj[:].rearrange("p (k n) -> p k n", k=2)
            route_w = w_route[:].rearrange("p (k n) -> p k n", k=2)

            def turn(kind, u, prior, slot):
                prev = 1 - slot
                pairs, has_next, has_prev = parts_of(kind)

                def room(pos):
                    before = fills(kind, u, pos) - 1
                    if kind != "pro" or before > 0:
                        pe.wait_ge(free[pos % NB], before)
                    return bank[pos % NB]

                def copied(jobs):
                    for pos in jobs[-NB:]:
                        pe.wait_ge(free[pos % NB], fills(kind, u, pos))

                def transposed(jobs, src):
                    for k, pos in enumerate(jobs):
                        out = room(pos)
                        for t in range(4):
                            last = nc.tensor.transpose(out[0:KD, t * TP:(t + 1) * TP],
                                                       src[:, t, k * KD:(k + 1) * KD], ident[:])
                        last.then_inc(full[pos % NB], 1)

                def product(out, lhs, rhs, width):
                    for k in range(2):
                        last = nc.tensor.matmul(out, lhs[:, k, :], rhs[:, k, 0:width], start=(k == 0), stop=(k == 1))
                    return last

                def tile(x, t):
                    return x[:, :, t * TP:(t + 1) * TP]

                def transpose_qk(g):
                    pos = QKT[g]
                    out = halfwords(room(pos))
                    for i in range(2):
                        for t in range(4):
                            at = (2 * g + i) * 2 * QW
                            src = qk[:, t].rearrange("p a x -> p (a x)")[:, at:at + 2 * QW]
                            last = nc.tensor.transpose(out[:, i * UT + t * TP:i * UT + (t + 1) * TP], src, ident16[:])
                    last.then_inc(full[pos % NB], 1)

                for n in range(PAIRS):
                    if pairs:
                        if n < PAIRS - 1:
                            scores(kind, u, n + 1, qk_t[slot])
                        if n >= LAG:
                            attend(kind, u, n - LAG, v[slot])
                    if n < LAG and has_prev:
                        attend("mid", u - 1, n - LAG + PAIRS, v[prev])
                    if n < 4 and has_next:
                        if n == 0:
                            pe.wait_ge(patches_in[prev], 16 * (prior + 2) if kind == "mid" else 16)
                        x = patches[prev][:].rearrange("p (k t) -> p k t", k=KP)
                        pos, at = TOK[n // 2], n % 2 * D
                        out = room(pos) if n % 2 == 0 else bank[pos % NB]
                        for i in range(KP):
                            last = nc.tensor.matmul(out[0:TP, at:at + D], x[:, i, n * TP:(n + 1) * TP], tok_w[:, i, :],
                                                    start=(i == 0), stop=(i == KP - 1))
                        if n % 2:
                            last.then_inc(full[pos % NB], 1)
                    if n == 4 and has_prev:
                        pe.wait_ge(y_ready, 2 * u)
                        transposed(YT, y[:].rearrange("p t h d -> p t (h d)"))
                    if n == 5 and has_prev:
                        copied(YT)
                        for k, pos in enumerate(PROJ):
                            out = room(pos)
                            for c in range(2):
                                last = product(out[0:TP, c * D:(c + 1) * D], tile(y_t, 2 * k + c), proj_w, D)
                            last.then_inc(full[pos % NB], 1)
                    if n == 6 and has_next:
                        pe.wait_ge(normed_ready, 4 * u + 8)
                        transposed(LN1T, normed)
                    if n in (6, 7) and has_next:
                        if n == 6:
                            copied(LN1T)
                        for t in range(2 * n - 12, 2 * n - 10):
                            out = room(QK[t])
                            product(out[0:TP, 0:2 * D], tile(normed_t, t), qkv_w, 2 * D).then_inc(full[QK[t] % NB], 1)
                        pos = VV[n - 6]
                        out = room(pos)
                        for c in range(2):
                            last = product(out[0:TP, c * D:(c + 1) * D], tile(normed_t, 2 * (n - 6) + c),
                                           qkv_w[:, :, 2 * D:3 * D], D)
                        last.then_inc(full[pos % NB], 1)
                    if n == 9 and has_prev:
                        pe.wait_ge(x2_ready, 4 * u)
                        for pos, turn_part in zip(X2T, (turn_near, turn_far)):
                            out = room(pos)
                            for t in range(4):
                                last = turn_part(nc, out[:, t * TP:(t + 1) * TP], x2[prev][:, t, :], ident[:])
                            last.then_inc(full[pos % NB], 1)
                    if n == 10 and has_prev:
                        copied(X2T)
                        out = room(ROUTE[0])
                        x = x2_t[prev][:].rearrange("p (k t) -> p k t", k=2)
                        for t in range(4):
                            logit = out[0:TP, t * E:(t + 1) * E]
                            nc.tensor.matmul(logit, tile(x, t)[:, 0], route_w[:, 0], start=True, stop=False)
                            last = nc.tensor.matmul(logit, tile(x, t)[0:D - 128, 1], route_w[0:D - 128, 1],
                                                    start=False, stop=True)
                        last.then_inc(full[ROUTE[0] % NB], 1)
                    if n == 11 and has_next:
                        pe.wait_ge(roped, 4 * u + 8)
                        for g in range(6):
                            transpose_qk(g)
                if has_next:
                    copied(QKT)
                    scores("first" if kind == "pro" else "mid", u + 1, 0, qk_t[prev])

            def scores(kind, u, n, qk_t):
                image, at = n // (PAIRS // 2), 2 * (n % (PAIRS // 2))
                if kind != "first" or n >= 2:
                    pe.wait_ge(copied_out, PAIRS * u + n - 1)
                for c, head in enumerate((at, at + 1)):
                    p = QW * (head % 2)
                    q = qk_t[p:p + QR, head // 2, 2 * image * TP:(2 * image + 2) * TP]
                    k = qk_t[p:p + QR, NH // 2 + head // 2, 2 * image * TP:(2 * image + 2) * TP]
                    out = score[n % 2][0:TP, c, :]
                    near = out[:, 0:3 * TP].rearrange("p (c s) -> p c s", c=3)[:, 0:3:2, :]
                    nc.tensor.matmul(near, k[:, 0:TP], q.rearrange("p (c s) -> p c s", c=2), start=True, stop=True)
                    last = nc.tensor.matmul(out[:, TP:2 * TP], k[:, TP:2 * TP], q[:, TP:2 * TP], start=True,
                                            stop=True)
                last.then_inc(scored, 1)

            def attend(kind, u, n, v):
                image, at = n // (PAIRS // 2), 2 * (n % (PAIRS // 2))
                pe.wait_ge(floored, PAIRS * u + n + 1)
                pe.wait_ge(masked, PAIRS * u + n + 1)
                if at == 0 and kind != "first":
                    pe.wait_ge(y_ready, 2 * u + image - 1)
                out = y_sum[image][0:TP, 0:2 * NH * VW].rearrange("p (t h d) -> p t h d", t=2, d=VW)
                for c, head in enumerate((at, at + 1)):
                    w = weights[:, n % 4, c]
                    near, far = v[:, 2 * image, head, :], v[:, 2 * image + 1, head, :]
                    nc.tensor.matmul(out[:, 0, head, :], w[:, 0:TP], near, start=True, stop=True)
                    nc.tensor.matmul(out[:, 1, head, :], w[:, 2 * TP:3 * TP], near, start=True, stop=False)
                    last = nc.tensor.matmul(out[:, 1, head, :], w[:, TP:2 * TP], far, start=False, stop=True)
                last.then_inc(attended, 1)

            turns(pe, turn)


def routing(nc, dram, logits, slot_of, weight_of):
    BITS = 30
    with ExitStack() as ctx:
        def sb(name, shape, dt=F32):
            return ctx.enter_context(nc.sbuf_tensor(name, shape, dt))

        def sem(name):
            return ctx.enter_context(nc.semaphore(name))

        full3 = [TP, TILES, E]
        probs, first, second, keep, key, scratch = (
            sb(n, full3) for n in ("probs", "first_choice", "second_choice", "keep", "key", "scratch"))
        ones_row = sb("ones_row", [TP, TILES])
        tile_sums = sb("tile_sums", full3)
        running = sb("running", full3)
        top, norm, best, w1, w2 = (sb(n, [TP, TILES]) for n in ("top", "norm", "best", "w1", "w2"))
        before = sb("before", [TP, TP])
        ones = sb("ones", [TP, TP])
        rank = sb("rank", [TP, E])
        base = sb("base", [TP, E])
        bits = sb("bits", [TP, BITS * E], I32)
        floor = sb("floor", [TP, E], I32)
        trial = sb("trial", [TP, E], I32)
        enough = sb("enough", [TP, E], I32)
        count = sb("count", [TP, E])
        room = sb("room", [TP, E])
        total = ctx.enter_context(nc.psum_tensor("total", [128, 512], F32))
        in_tile = ctx.enter_context(nc.psum_tensor("in_tile", [128, 2, 512], F32))
        of_tile = ctx.enter_context(nc.psum_tensor("of_tile", [128, 2, 512], F32))
        consts_in, shifted, powered, vec, counted, totalled, marked, summed, spacer = map(sem, (
            "route_consts_in", "shifted", "powered", "route_steps", "counted", "totalled", "marked", "prefix_summed", "route_spacer"))
        block = ctx.enter_context(nc.Block())
        constants = ((before, "before"), (ones, "ones"), (rank, "rank"), (base, "base"), (bits, "bits"))

        @block.sync
        def _(sp):
            for dst, src in constants:
                sp.dma_start(dst[:], dram[src]).then_inc(consts_in, 16)

        @block.scalar
        def _(act):
            act.wait_ge(shifted, 1)
            nc.scalar.activation(probs[:], probs[:], ACT.Exp).then_inc(powered, 1)

        @block.tensor
        def _(pe):
            pe.wait_ge(consts_in, 16 * len(constants))
            with pe.Fori(0, BITS + 1) as i:
                pe.wait_ge(counted, i + 1)
                nc.tensor.matmul(total[0:TP, 0:E], ones[:], count[:], start=True, stop=True).then_inc(totalled, 1)
            for n in range(2):
                pe.wait_ge(marked, n + 1)
                src = (key, keep)[n][:].rearrange("p t e -> p (t e)").rearrange("p (c x) -> p c x", c=2)
                for out, mat in ((in_tile, before), (of_tile, ones)):
                    for c in range(2):
                        last = nc.tensor.matmul(out[0:TP, c, :], mat[:], src[:, c, :], start=True, stop=True)
                last.then_inc(summed, 1)

        @block.vector
        def _(dve):
            chain = Tally()

            def step(ins):
                chain.step(ins, vec)
                dve.wait_ge(vec, chain.value)

            def tt(out, a, b, op):
                step(nc.vector.tensor_tensor(out, a, b, op))

            def ts(out, a, s1, s2, op0, op1=None):
                step(nc.vector.tensor_scalar(out, a, s1, s2, op0, op1) if op1 is not None
                     else nc.vector.tensor_scalar(out, a, s1, None, op0))

            def per_tile(x):
                return x[:].unsqueeze(2).to_broadcast(full3)

            def per_expert(x):
                return x.unsqueeze(1).to_broadcast(full3)

            def by_expert(x):
                return x[:].rearrange("p t e -> p e t")

            def choose(out, top):
                step(nc.vector.tensor_reduce(top[:], probs[:], AX.X, ALU.max))
                tt(out[:], probs[:], per_tile(top), ALU.is_equal)
                tt(out[:], out[:], per_expert(rank[:]), ALU.mult)
                step(nc.vector.tensor_reduce(best[:], out[:], AX.X, ALU.max))
                tt(out[:], out[:], per_tile(best), ALU.is_equal)

            def prefix(n, src):
                dve.wait_ge(summed, n + 1)
                flat = tile_sums[:].rearrange("p t e -> p (t e)").rearrange("p (c x) -> p c x", c=2)
                step(nc.vector.tensor_copy(flat, of_tile[0:TP]))
                for e in range(E):
                    step(nc.vector.tensor_tensor_scan(running[:, :, e], ones_row[:], tile_sums[:, :, e], 0.0,
                                                      ALU.mult, ALU.add))
                tt(running[:], running[:], tile_sums[:], ALU.subtract)
                flat = running[:].rearrange("p t e -> p (t e)").rearrange("p (c x) -> p c x", c=2)
                tt(flat, flat, in_tile[0:TP], ALU.add)

            dve.wait_ge(consts_in, 16 * len(constants))
            step(nc.vector.memset(ones_row[:], 1.0))
            step(nc.vector.memset(floor[:], 0))
            view = logits[:].rearrange("p (t e) -> p t e", e=E)
            step(nc.vector.tensor_reduce(top[:], view, AX.X, ALU.max))
            nc.vector.tensor_tensor(probs[:], view, per_tile(top), ALU.subtract).then_inc(shifted, 1)
            dve.wait_ge(powered, 1)
            step(nc.vector.tensor_reduce(norm[:], probs[:], AX.X, ALU.add))
            step(nc.vector.reciprocal(norm[:], norm[:]))
            tt(probs[:], probs[:], per_tile(norm), ALU.mult)
            choose(first, w1)
            step(nc.vector.scalar_tensor_tensor(probs[:], first[:], -2.0, probs[:], ALU.mult, ALU.add))
            choose(second, w2)
            tt(norm[:], w1[:], w2[:], ALU.add)
            ts(norm[:], norm[:], 1e-9, None, ALU.max)
            step(nc.vector.reciprocal(norm[:], norm[:]))
            tt(w1[:], w1[:], norm[:], ALU.mult)
            tt(w2[:], w2[:], norm[:], ALU.mult)
            shares = weight_of[:].rearrange("p (t c) -> p t c", c=2)
            step(nc.vector.tensor_copy(shares[:, :, 0], w1[:]))
            step(nc.vector.tensor_copy(shares[:, :, 1], w2[:]))
            tt(key[:], first[:], per_tile(w1), ALU.mult)
            tt(scratch[:], second[:], per_tile(w2), ALU.mult)
            tt(key[:], key[:], scratch[:], ALU.add)
            tt(scratch[:], first[:], second[:], ALU.add)
            step(nc.vector.scalar_tensor_tensor(key[:], scratch[:], -1.0, key[:], ALU.add, ALU.add))

            with dve.Fori(0, BITS) as i:
                chain.enter(i, 4)
                tt(trial[:], floor[:], bits[:, bass.ds(i * E, E)], ALU.bitwise_or)
                tt(scratch[:], key[:], per_expert(trial[:].bitcast(F32)), ALU.is_ge)
                nc.vector.tensor_reduce(count[:], by_expert(scratch), AX.X, ALU.add).then_inc(counted, 1)
                dve.wait_ge(totalled, i + 1)
                step(nc.vector.tensor_scalar(enough[:], total[0:TP, 0:E], float(CAP), None, ALU.is_ge))
                dve.sem_inc(spacer, 1)
                step(nc.vector.copy_predicated(floor[:], enough[:], trial[:]))
            chain.leave(BITS)

            level = per_expert(floor[:].bitcast(F32))
            tt(scratch[:], key[:], level, ALU.is_gt)
            nc.vector.tensor_reduce(count[:], by_expert(scratch), AX.X, ALU.add).then_inc(counted, 1)
            dve.wait_ge(totalled, BITS + 1)
            ts(room[:], total[0:TP, 0:E], -1.0, float(CAP), ALU.mult, ALU.add)
            nc.vector.tensor_tensor(key[:], key[:], level, ALU.is_equal).then_inc(marked, 1)
            prefix(0, key)
            tt(running[:], running[:], per_expert(room[:]), ALU.is_lt)
            tt(running[:], running[:], key[:], ALU.mult)
            nc.vector.tensor_tensor(keep[:], running[:], scratch[:], ALU.add).then_inc(marked, 1)
            prefix(1, keep)
            tt(running[:], running[:], per_expert(base[:]), ALU.add)
            tt(running[:], running[:], keep[:], ALU.mult)
            slots = slot_of[:].rearrange("p (t c) -> p t c", c=2)
            for c, choice in enumerate((first, second)):
                tt(scratch[:], choice[:], running[:], ALU.mult)
                step(nc.vector.tensor_reduce(best[:], scratch[:], AX.X, ALU.add))
                ts(slots[:, :, c], best[:], float(SLOTS), None, ALU.add)


TOKEN_SCALE, WEIGHT_SCALE, HIDDEN_SCALE = 2.0 ** 6, 2.0 ** 6, 2.0 ** 4


def ffn_tensors(ctx, nc, of, slots):
    def sb(name, shape, dt=F32):
        return ctx.enter_context(nc.sbuf_tensor(f"{of}_{name}", shape, dt))

    def sem(name):
        return ctx.enter_context(nc.semaphore(f"{of}_{name}"))

    class T:
        pass

    T.raw = [sb(f"raw{n}", [128, 2 * INNER]) for n in (1, 3)] + [sb("raw2", [128, MI * D])]
    T.w_hi = [[sb(f"w{n}_hi{s}", [128, 2 * INNER], F16) for n in (1, 3)] + [sb(f"w2_hi{s}", [128, MI * D], F16)]
              for s in range(slots)]
    T.w_lo = [[sb(f"w{n}_lo{s}", [128, 2 * INNER], F16) for n in (1, 3)] + [sb(f"w2_lo{s}", [128, MI * D], F16)]
              for s in range(slots)]
    T.tokens_near_hi = sb("tokens_near_hi", [128, UT], F16)
    T.tokens_near_lo = sb("tokens_near_lo", [128, UT], F16)
    T.tokens_far = sb("tokens_far", [128, UT], F16)
    T.silu = sb("silu", [128, 2, UT])
    T.hidden = sb("hidden", [128, 2, UT])
    T.hidden_hi = [sb(f"hidden_hi{s}", [128, MI, UT], F16) for s in range(2)]
    T.hidden_lo = [sb(f"hidden_lo{s}", [128, MI, UT], F16) for s in range(2)]
    T.gate, T.up, T.out = (
        [ctx.enter_context(nc.psum_tensor(f"{of}_{name}{b}", [128, 512], F32)) for b in range(2)]
        for name in ("gate", "up", "out"))
    (T.gated, T.silued, T.multiplied, T.hi_ready, T.lo_ready, T.out_full, T.out_used, T.tokens_hi, T.tokens_lo,
     T.weights_hi, T.weights_lo) = map(sem, (
         "gated", "silued", "multiplied", "hi_ready", "lo_ready", "out_full", "out_used", "tokens_hi", "tokens_lo",
         "weights_hi", "weights_lo"))
    return T


def weights_hi(nc, T, ws):
    for raw, hi in zip(T.raw, T.w_hi[ws]):
        nc.scalar.activation(hi[:], raw[:], ACT.Copy, scale=WEIGHT_SCALE).then_inc(T.weights_hi, 1)


def weights_lo(nc, T, ws):
    for raw, hi, lo in zip(T.raw, T.w_hi[ws], T.w_lo[ws]):
        nc.vector.scalar_tensor_tensor(lo[:], raw[:], WEIGHT_SCALE, hi[:], ALU.mult, ALU.subtract)\
          .then_inc(T.weights_lo, 1)


def tokens_hi(nc, T, near, far):
    nc.scalar.activation(T.tokens_near_hi[:], near, ACT.Copy, scale=TOKEN_SCALE).then_inc(T.tokens_hi, 1)
    nc.scalar.activation(T.tokens_far[:], far, ACT.Copy, scale=TOKEN_SCALE).then_inc(T.tokens_hi, 1)


def tokens_lo(nc, dve, T, g, near, far):
    dve.wait_ge(T.tokens_hi, 2 * g + 2)
    nc.vector.scalar_tensor_tensor(T.tokens_near_lo[:], near, TOKEN_SCALE, T.tokens_near_hi[:],
                                   ALU.mult, ALU.subtract).then_inc(T.tokens_lo, 1)
    nc.vector.scalar_tensor_tensor(T.tokens_far[D - 128:128], far, TOKEN_SCALE, T.tokens_far[D - 128:128],
                                   ALU.mult, ALU.subtract).then_inc(T.tokens_lo, 1)


def units_of(eng, count, first, half, unit):
    unit(first, half, 0, "first")
    with eng.Fori(0, count // 2 - 1) as j:
        unit(first + 2 * j + 1, half + j, 1, "mid")
        unit(first + 2 * j + 2, half + j + 1, 0, "mid")
    unit(first + count - 1, half + count // 2 - 1, 1, "last")


def pairs_of_units(eng, count, unit):
    unit(0, 0, 0)
    unit(1, 0, 1)
    with eng.Fori(1, count // 2) as half:
        unit(2 * half, half, 0)
        unit(2 * half + 1, half, 1)


def tensor_unit(nc, pe, T, g, ws):
    pe.wait_ge(T.tokens_lo, 2 * g + 6)
    for m in range(MI):
        pe.wait_ge(T.multiplied, MI * g + m + 1)
        near = slice(m * 128, (m + 1) * 128)
        far = slice(INNER + m * 128, INNER + (m + 1) * 128)
        for out, hi, lo in ((T.gate[m % 2], T.w_hi[ws][0], T.w_lo[ws][0]), (T.up[m % 2], T.w_hi[ws][1], T.w_lo[ws][1])):
            out = out[:, 0:UT]
            nc.tensor.matmul(out, hi[:, near], T.tokens_near_hi[:], start=True, stop=False)
            nc.tensor.matmul(out, hi[:, near], T.tokens_near_lo[:], start=False, stop=False)
            nc.tensor.matmul(out, lo[:, near], T.tokens_near_hi[:], start=False, stop=False)
            nc.tensor.matmul(out, hi[:, far], T.tokens_far[:], start=False, stop=False)
            last = nc.tensor.matmul(out, lo[0:D - 128, far], T.tokens_far[0:D - 128], start=False, stop=True)
        last.then_inc(T.gated, 1)


def tensor_out(nc, pe, T, g, slot, ws):
    pe.wait_ge(T.lo_ready, MI * g + MI + 2)
    w_hi, w_lo = (w[ws][2][:].rearrange("p (m n) -> p m n", m=MI) for w in (T.w_hi, T.w_lo))
    for n in range(2):
        pe.wait_ge(T.out_used, 2 * g + n + 1)
        for c in range(2):
            tokens = slice((2 * n + c) * TP, (2 * n + c + 1) * TP)
            out = T.out[n][0:TP, c * D:(c + 1) * D]
            for m in range(MI):
                hi, lo = T.hidden_hi[slot][:, m, tokens], T.hidden_lo[slot][:, m, tokens]
                nc.tensor.matmul(out, hi, w_hi[:, m, :], start=(m == 0), stop=False)
                nc.tensor.matmul(out, hi, w_lo[:, m, :], start=False, stop=False)
                last = nc.tensor.matmul(out, lo, w_hi[:, m, :], start=False, stop=(m == MI - 1))
        last.then_inc(T.out_full, 1)


def scalar_unit(nc, act, T, g, slot):
    def hi(m):
        act.wait_ge(T.multiplied, MI * g + m + 3)
        nc.scalar.copy(T.hidden_hi[slot][:, m, :], T.hidden[:, m % 2, :]).then_inc(T.hi_ready, 1)

    for m in range(MI):
        act.wait_ge(T.gated, MI * g + m + 1)
        act.wait_ge(T.multiplied, MI * g + m + 1)
        nc.scalar.activation(T.silu[:, m % 2, :], T.gate[m % 2][:, 0:UT], ACT.Silu,
                             scale=1.0 / (TOKEN_SCALE * WEIGHT_SCALE)).then_inc(T.silued, 1)
        if m:
            hi(m - 1)
    hi(MI - 1)


def vector_unit(nc, dve, T, g, slot):
    def lo(m):
        dve.wait_ge(T.hi_ready, MI * g + m + 1)
        nc.vector.tensor_tensor(T.hidden_lo[slot][:, m, :], T.hidden[:, m % 2, :], T.hidden_hi[slot][:, m, :],
                                ALU.subtract).then_inc(T.lo_ready, 1)

    for m in range(MI):
        dve.wait_ge(T.silued, MI * g + m + 1)
        dve.wait_ge(T.lo_ready, MI * g + m + 1)
        nc.vector.scalar_tensor_tensor(T.hidden[:, m % 2, :], T.up[m % 2][:, 0:UT],
                                       HIDDEN_SCALE / (TOKEN_SCALE * WEIGHT_SCALE), T.silu[:, m % 2, :],
                                       ALU.mult, ALU.mult).then_inc(T.multiplied, 1)
        if m:
            lo(m - 1)
    lo(MI - 1)


def shared_half(nc, dram, T, first, bufs, sems):
    x_t, rows, sums = bufs
    xt_in, rows_in, sums_out = sems

    class Half:
        pass

    def load(sp, g, half, slot):
        sp.wait_ge(T.tokens_lo, 2 * g + 2)
        sp.dma_start(x_t[slot][:], dram["x2_t"][bass.ds((first + g) * 128, 128), :]).then_inc(xt_in[slot], 16)
        sp.wait_ge(T.out_used, 2 * g)
        sp.dma_start(rows[slot][:], unit_rows(dram["h2"], first + g)).then_inc(rows_in[slot], 16)

    def multiply(pe, g, slot, opens):
        tensor_unit(nc, pe, T, g, 0)
        if not opens:
            tensor_out(nc, pe, T, g - 1, 1 - slot, 0)

    def store(act, g, slot):
        act.wait_ge(T.out_used, 2 * g + 4)
        act.dma_start(unit_rows(dram["h2"], first + g), sums[slot][:]).then_inc(sums_out[slot], 16)

    def split_hi(act, half, slot):
        act.wait_ge(xt_in[slot], 16 * half + 16)
        tokens_hi(nc, T, x_t[slot][:, 0:UT], x_t[slot][:, UT:2 * UT])

    def split_lo(dve, g, slot):
        tokens_lo(nc, dve, T, g, x_t[slot][:, 0:UT], x_t[slot][D - 128:128, UT:2 * UT])

    def add(dve, g, half, slot, primed):
        dve.wait_ge(rows_in[slot], 16 * half + 16)
        dve.wait_ge(sums_out[slot], 16 * half + primed)
        for n in range(2):
            dve.wait_ge(T.out_full, 2 * g + n + 1)
            nc.vector.scalar_tensor_tensor(
                sums[slot][:, 2 * n:2 * n + 2, :],
                T.out[n][0:TP, 0:2 * D].rearrange("p (t d) -> p t d", t=2),
                1.0 / (HIDDEN_SCALE * WEIGHT_SCALE), rows[slot][:, 2 * n:2 * n + 2, :],
                ALU.mult, ALU.add).then_inc(T.out_used, 1)

    Half.load, Half.multiply, Half.store, Half.split_hi, Half.split_lo, Half.add = (
        load, multiply, store, split_hi, split_lo, add)
    return Half


def shared(nc, dram, slot_of):
    with ExitStack() as ctx:
        def sb(name, shape, dt=F32):
            return ctx.enter_context(nc.sbuf_tensor(name, shape, dt))

        def sem(name):
            return ctx.enter_context(nc.semaphore(name))

        T = ffn_tensors(ctx, nc, "shared", 1)
        bufs = [[sb(f"{n}{s}", shape) for s in range(2)] for n, shape in (
            ("x_t", [128, 2 * UT]), ("rows", [TP, 4, D]), ("sums", [TP, 4, D]))]
        sent = [sb(f"sent{s}", [TP, 4, D]) for s in range(2)]
        index = [sb(f"index{s}", [TP, 8], U32) for s in range(2)]
        weights_in = sem("shared_in")
        xt_in, rows_in, sums_out, sent_in, scattered = (
            [sem(f"{n}{s}") for s in range(2)] for n in ("xt_in", "rows_in", "sums_out", "sent_in", "scattered"))
        indexed, spacer, load_spacer = sem("indexed"), sem("scatter_spacer"), sem("sent_spacer")
        ffn = shared_half(nc, dram, T, 0, bufs, (xt_in, rows_in, sums_out))
        block = ctx.enter_context(nc.Block())

        @block.sync
        def _(sp):
            for dst, src in zip(T.raw, ("w1", "w3", "w2")):
                sp.dma_start(dst[:], dram[src][E * 128:(E + 1) * 128, :]).then_inc(weights_in, 16)

            def unit(g, half, slot):
                ffn.load(sp, g, half, slot)
                for s in range(2):
                    sp.wait_ge(scattered[s], 128 * g)
                    sp.sem_inc(load_spacer, 1)
                    sp.dma_start(sent[s][:], unit_rows(dram["x2"], 2 * g + s)).then_inc(sent_in[s], 16)

            pairs_of_units(sp, HALF, unit)

        @block.gpsimd
        def _(pool):
            def unit(g, half, slot):
                pool.wait_ge(scattered[slot], 128 * half)
                pool.sem_inc(spacer, 1)
                nc.gpsimd.tensor_copy(index[slot][:], slot_of[:, bass.ds(g * 8, 8)]).then_inc(indexed, 1)
                pool.wait_ge(indexed, g + 1)
                pool.wait_ge(sent_in[slot], 16 * half + 16)
                pool.sem_inc(spacer, 1)
                for t in range(4):
                    for c in range(2):
                        nc.gpsimd.indirect_dma_start(
                            out=dram["slots"][:, :],
                            out_offset=bass.IndirectOffsetOnAxis(ap=index[slot][:, 2 * t + c:2 * t + c + 1], axis=0),
                            in_=sent[slot][:, t, :], in_offset=None, bounds_check=SLOTS - 1, oob_is_err=False)\
                          .then_inc(scattered[slot], 16)

            pairs_of_units(pool, UNITS, unit)
            for s in range(2):
                pool.wait_ge(scattered[s], 128 * (UNITS // 2))

        @block.tensor
        def _(pe):
            pe.wait_ge(T.weights_lo, 3)

            def unit(g, half, slot, place):
                ffn.multiply(pe, g, slot, place == "first")

            units_of(pe, HALF, 0, 0, unit)
            tensor_out(nc, pe, T, HALF - 1, 1, 0)

        @block.scalar
        def _(act):
            act.wait_ge(weights_in, 48)
            weights_hi(nc, T, 0)
            ffn.split_hi(act, 0, 0)

            def unit(g, half, slot, place):
                scalar_unit(nc, act, T, g, slot)
                if place != "last":
                    ffn.split_hi(act, half + slot, 1 - slot)
                if place != "first":
                    ffn.store(act, g - 1, 1 - slot)

            units_of(act, HALF, 0, 0, unit)
            ffn.store(act, HALF - 1, 1)
            for s in range(2):
                act.wait_ge(sums_out[s], 16 * (HALF // 2 + 1))

        @block.vector
        def _(dve):
            for primed in (T.multiplied, T.lo_ready, T.out_used):
                dve.sem_inc(primed, 2)
            dve.sem_inc(T.tokens_lo, 4)
            for s in range(2):
                dve.sem_inc(sums_out[s], 16)
            dve.wait_ge(T.weights_hi, 3)
            weights_lo(nc, T, 0)
            ffn.split_lo(dve, 0, 0)

            def unit(g, half, slot, place):
                vector_unit(nc, dve, T, g, slot)
                if place != "last":
                    ffn.split_lo(dve, g + 1, 1 - slot)
                if place != "first":
                    ffn.add(dve, g - 1, half - (1 - slot), 1 - slot, 16)

            units_of(dve, HALF, 0, 0, unit)
            ffn.add(dve, HALF - 1, HALF // 2 - 1, 1, 16)


def experts(nc, dram):
    with ExitStack() as ctx:
        def sb(name, shape, dt=F32):
            return ctx.enter_context(nc.sbuf_tensor(name, shape, dt))

        def sem(name):
            return ctx.enter_context(nc.semaphore(name))

        T = ffn_tensors(ctx, nc, "experts", 2)
        rows = [sb(f"tokens{s}", [TP, 4, D]) for s in range(2)]
        done = [sb(f"done{s}", [TP, 4, D]) for s in range(2)]
        ident = sb("ident2", [TP, TP])
        turned = [ctx.enter_context(nc.psum_tensor(f"turned{k}", [128, 512], F32)) for k in range(2)]
        ident_in, turned_full, weights_in = map(sem, ("ident_in", "turned_full", "weights_in"))
        rows_in, stored = ([sem(f"{n}{s}") for s in range(2)] for n in ("tokens_in", "stored"))
        block = ctx.enter_context(nc.Block())

        def passes(eng, expert):
            with eng.Fori(0, E // 2) as pair:
                expert(2 * pair, 0)
                expert(2 * pair + 1, 1)

        @block.sync
        def _(sp):
            sp.dma_start(ident[:], dram["ident"]).then_inc(ident_in, 16)

            def load(e):
                for dst, src in zip(T.raw, ("w1", "w3", "w2")):
                    sp.dma_start(dst[:], dram[src][bass.ds(e * 128, 128), :]).then_inc(weights_in, 16)

            load(0)

            def expert(e, ws):
                def unit(g, half, slot, place):
                    sp.wait_ge(T.tokens_lo, 2 * g + 2)
                    sp.dma_start(rows[slot][:], unit_rows(dram["slots"], g)).then_inc(rows_in[slot], 16)
                    if place == "first":
                        sp.wait_ge(T.weights_lo, 3 * e + 3)
                        load(e + 1)

                units_of(sp, EU, e * EU, e * (EU // 2), unit)

            passes(sp, expert)
            sp.wait_ge(weights_in, 48 * (E + 1))

        @block.tensor
        def _(pe):
            pe.wait_ge(ident_in, 16)

            def expert(e, ws):
                def turn(g, half, slot):
                    pe.wait_ge(rows_in[slot], 16 * half + 16)
                    pe.wait_ge(T.tokens_lo, 2 * g + 4)
                    for t in range(4):
                        src = rows[slot][:, t, :]
                        tokens = slice(t * TP, (t + 1) * TP)
                        turn_near(nc, turned[0][:, tokens], src, ident[:])
                        last = turn_far(nc, turned[1][:, tokens], src, ident[:])
                    last.then_inc(turned_full, 1)

                def unit(g, half, slot, place):
                    if place == "first":
                        turn(g, half, slot)
                        pe.wait_ge(T.weights_lo, 3 * e + 3)
                    tensor_unit(nc, pe, T, g, ws)
                    if place != "last":
                        turn(g + 1, half + slot, 1 - slot)
                    if place != "first":
                        tensor_out(nc, pe, T, g - 1, 1 - slot, ws)

                units_of(pe, EU, e * EU, e * (EU // 2), unit)
                tensor_out(nc, pe, T, e * EU + EU - 1, 1, ws)

            passes(pe, expert)

        @block.scalar
        def _(act):
            def put(g, half, slot):
                act.wait_ge(stored[slot], 16 * half + 16)
                for n in range(2):
                    act.wait_ge(T.out_full, 2 * g + n + 1)
                    nc.scalar.activation(done[slot][:, 2 * n:2 * n + 2, :],
                                         T.out[n][0:TP, 0:2 * D].rearrange("p (t d) -> p t d", t=2),
                                         ACT.Copy, scale=1.0 / (HIDDEN_SCALE * WEIGHT_SCALE)).then_inc(T.out_used, 1)
                act.wait_ge(T.out_used, 2 * g + 4)
                act.dma_start(unit_rows(dram["expert_rows"], g), done[slot][:]).then_inc(stored[slot], 16)

            def split(g):
                act.wait_ge(turned_full, g + 1)
                tokens_hi(nc, T, turned[0][:, 0:UT], turned[1][:, 0:UT])

            act.wait_ge(weights_in, 48)
            weights_hi(nc, T, 0)

            def expert(e, ws):
                def unit(g, half, slot, place):
                    if place == "first":
                        split(g)
                    scalar_unit(nc, act, T, g, slot)
                    if place != "last":
                        split(g + 1)
                    if place == "first":
                        act.wait_ge(weights_in, 48 * e + 96)
                        weights_hi(nc, T, 1 - ws)
                    else:
                        put(g - 1, half - (1 - slot), 1 - slot)

                units_of(act, EU, e * EU, e * (EU // 2), unit)
                put(e * EU + EU - 1, e * (EU // 2) + EU // 2 - 1, 1)

            passes(act, expert)
            for s in range(2):
                act.wait_ge(stored[s], 16 * (E * EU // 2 + 1))

        @block.vector
        def _(dve):
            for primed in (T.multiplied, T.lo_ready, T.out_used):
                dve.sem_inc(primed, 2)
            dve.sem_inc(T.tokens_lo, 4)
            for s in range(2):
                dve.sem_inc(stored[s], 16)
            dve.wait_ge(T.weights_hi, 3)
            weights_lo(nc, T, 0)

            def split(g):
                tokens_lo(nc, dve, T, g, turned[0][:, 0:UT], turned[1][D - 128:128, 0:UT])

            def expert(e, ws):
                def unit(g, half, slot, place):
                    if place == "first":
                        split(g)
                    vector_unit(nc, dve, T, g, slot)
                    if place != "last":
                        split(g + 1)
                    if place == "first":
                        dve.wait_ge(T.weights_hi, 3 * e + 6)
                        weights_lo(nc, T, 1 - ws)

                units_of(dve, EU, e * EU, e * (EU // 2), unit)

            passes(dve, expert)


def steps_of(eng, step):
    for j in range(4):
        step(j, j // 2, j % 2)
    with eng.Fori(2, HALF // 2 - 1) as half:
        step(2 * half, half, 0)
        step(2 * half + 1, half, 1)
    for j in range(HALF - 2, HALF + 3):
        step(j, j // 2, j % 2)


def within(j, first, last):
    return not isinstance(j, int) or first <= j <= last


def combine(nc, dram, slot_of, weight_of):
    with ExitStack() as ctx:
        def sb(name, shape, dt=F32):
            return ctx.enter_context(nc.sbuf_tensor(name, shape, dt))

        def sem(name):
            return ctx.enter_context(nc.semaphore(name))

        T = ffn_tensors(ctx, nc, "late", 1)
        bufs = [[sb(f"late_{n}{s}", shape) for s in range(2)] for n, shape in (
            ("x_t", [128, 2 * UT]), ("rows", [TP, 4, D]), ("sums", [TP, 4, D]))]
        base = [sb(f"base{s}", [TP, 4, D]) for s in range(2)]
        gathered = [sb(f"gathered{s}", [TP, 8, D]) for s in range(2)]
        index = [sb(f"from{s}", [TP, 8], U32) for s in range(2)]
        weights_in = sem("late_in")
        xt_in, rows_in, sums_out, base_in, gathered_in, stored = (
            [sem(f"late_{n}{s}") for s in range(2)]
            for n in ("xt_in", "rows_in", "sums_out", "base_in", "gathered_in", "out_stored"))
        indexed, combined, spacer, load_spacer = map(sem, (
            "from_indexed", "combined", "gather_spacer", "base_spacer"))
        ffn = shared_half(nc, dram, T, HALF, bufs, (xt_in, rows_in, sums_out))
        start = 16 * (HALF // 2)
        block = ctx.enter_context(nc.Block())

        @block.sync
        def _(sp):
            for dst, src in zip(T.raw, ("w1", "w3", "w2")):
                sp.dma_start(dst[:], dram[src][E * 128:(E + 1) * 128, :]).then_inc(weights_in, 16)

            def step(j, half, slot):
                if within(j, 0, HALF - 1):
                    ffn.load(sp, j, half, slot)
                if within(j, 3, HALF + 2):
                    for s in range(2):
                        sp.wait_ge(combined, 16 * (j - 3) + 8 * s + 16)
                        sp.sem_inc(load_spacer, 1)
                        sp.dma_start(unit_rows(dram["out"], 2 * (j - 3) + s), base[s][:]).then_inc(stored[s], 16)
                if within(j, 2, HALF + 1):
                    for s in range(2):
                        sp.wait_ge(stored[s], 16 * (j - 2))
                        sp.sem_inc(load_spacer, 1)
                        sp.wait_ge(sums_out[s], 16 * (j - 1))
                        sp.sem_inc(load_spacer, 1)
                        sp.dma_start(base[s][:], unit_rows(dram["h2"], 2 * (j - 2) + s)).then_inc(base_in[s], 16)

            steps_of(sp, step)
            for s in range(2):
                sp.wait_ge(stored[s], 16 * (UNITS // 2))

        @block.gpsimd
        def _(pool):
            def unit(g, half, slot):
                pool.wait_ge(combined, 8 * g)
                pool.wait_ge(gathered_in[slot], 128 * half)
                pool.sem_inc(spacer, 1)
                nc.gpsimd.tensor_copy(index[slot][:], slot_of[:, bass.ds(g * 8, 8)]).then_inc(indexed, 1)
                pool.wait_ge(indexed, g + 1)
                pool.sem_inc(spacer, 1)
                for n in range(8):
                    nc.gpsimd.indirect_dma_start(
                        out=gathered[slot][:, n, :], out_offset=None, in_=dram["expert_rows"][:, :],
                        in_offset=bass.IndirectOffsetOnAxis(ap=index[slot][:, n:n + 1], axis=0),
                        bounds_check=SLOTS, oob_is_err=False).then_inc(gathered_in[slot], 16)

            pairs_of_units(pool, UNITS, unit)

        @block.tensor
        def _(pe):
            pe.wait_ge(T.weights_lo, 3)

            def step(j, half, slot):
                if within(j, 0, HALF - 1):
                    ffn.multiply(pe, j, slot, not within(j, 1, HALF))
                elif j == HALF:
                    tensor_out(nc, pe, T, HALF - 1, 1, 0)

            steps_of(pe, step)

        @block.scalar
        def _(act):
            act.wait_ge(weights_in, 48)
            weights_hi(nc, T, 0)
            ffn.split_hi(act, 0, 0)

            def step(j, half, slot):
                if within(j, 0, HALF - 1):
                    scalar_unit(nc, act, T, j, slot)
                if within(j, 0, HALF - 2):
                    ffn.split_hi(act, half + slot, 1 - slot)
                if within(j, 1, HALF):
                    ffn.store(act, j - 1, 1 - slot)

            steps_of(act, step)
            for s in range(2):
                act.wait_ge(sums_out[s], start + 16 * (HALF // 2))

        @block.vector
        def _(dve):
            for primed in (T.multiplied, T.lo_ready, T.out_used):
                dve.sem_inc(primed, 2)
            dve.sem_inc(T.tokens_lo, 4)
            dve.sem_inc(combined, 8)
            for s in range(2):
                dve.sem_inc(sums_out[s], start)
            dve.wait_ge(T.weights_hi, 3)
            weights_lo(nc, T, 0)
            ffn.split_lo(dve, 0, 0)

            def weigh(g, half, slot):
                dve.wait_ge(base_in[slot], 16 * half + 16)
                dve.wait_ge(gathered_in[slot], 128 * half + 128)
                for c in range(2):
                    if c:
                        dve.wait_ge(combined, 8 * g + 12)
                    for t in range(4):
                        nc.vector.scalar_tensor_tensor(
                            base[slot][:, t, :], gathered[slot][:, 2 * t + c, :],
                            weight_of[:, bass.ds(g * 8 + 2 * t + c, 1)], base[slot][:, t, :], ALU.mult, ALU.add)\
                          .then_inc(combined, 1)

            def step(j, half, slot):
                if within(j, 0, HALF - 1):
                    vector_unit(nc, dve, T, j, slot)
                if within(j, 0, HALF - 2):
                    ffn.split_lo(dve, j + 1, 1 - slot)
                if within(j, 1, HALF):
                    ffn.add(dve, j - 1, half - (1 - slot), 1 - slot, start)
                if within(j, 2, HALF + 1):
                    for s in range(2):
                        weigh(2 * (j - 2) + s, j - 2, s)

            steps_of(dve, step)


def build(nc, dram):
    with (nc.sbuf_tensor("logits", [TP, TILES * E], F32) as logits,
          nc.sbuf_tensor("slot_of", [TP, TILES * 2], U32) as slot_of,
          nc.sbuf_tensor("weight_of", [TP, TILES * 2], F32) as weight_of):
        attention(nc, dram, logits)
        routing(nc, dram, logits, slot_of, weight_of)
        shared(nc, dram, slot_of)
        experts(nc, dram)
        combine(nc, dram, slot_of, weight_of)


def rope_table():
    half = HD // 2
    freq = (np.float32(1.0) / np.power(np.float32(10000.0), np.arange(half, dtype=np.float32) / np.float32(half)))
    angle = np.arange(S, dtype=np.float32)[:, None] * freq.astype(np.float32)[None, :]
    table = np.stack([np.cos(angle), np.sin(angle)], 1).astype(np.float32) * np.float32(QK_SCALE)
    return np.ascontiguousarray(table.reshape(2, TP, 2, half).transpose(1, 0, 2, 3).reshape(TP, -1))


def halves(w):
    return np.ascontiguousarray(w.reshape(2, KD, -1).transpose(1, 0, 2).reshape(KD, -1))


def near_far(w):
    return np.concatenate([w[:128], np.concatenate([w[128:], w[128:]])], 1)


def inner_rows(w):
    return np.ascontiguousarray(w.reshape(MI, 128, D).transpose(1, 0, 2).reshape(128, -1))


def layout(x, L0_tok_W, L0_tok_b, L0_attn_Wq, L0_attn_Wk, L0_attn_Wv, L0_attn_Wproj, L0_ffn_Wr, L0_ffn_w1, L0_ffn_w3,
           L0_ffn_w2, L0_ffn_s1, L0_ffn_s3, L0_ffn_s2):
    p = x.reshape(UNITS, 2, GRID, PATCH, GRID, PATCH * 3).transpose(0, 3, 5, 1, 2, 4).reshape(UNITS, KP, 128, UT)
    split = np.arange(D).reshape(NH, HD // 2, 2).transpose(0, 2, 1).reshape(-1)
    qkv = np.concatenate([L0_attn_Wq.T[:, split], L0_attn_Wk.T[:, split], L0_attn_Wv.T], 1)
    return {
        "patches": np.ascontiguousarray(p.transpose(0, 2, 1, 3)).reshape(UNITS * 128, KP * UT),
        "w_tok": np.ascontiguousarray(L0_tok_W.reshape(KP, 128, D).transpose(1, 0, 2)).reshape(128, KP * D),
        "bias": np.ascontiguousarray(np.broadcast_to(L0_tok_b, (TP, D))),
        "w_qkv": halves(qkv),
        "w_proj": halves(np.ascontiguousarray(L0_attn_Wproj.T)),
        "w_route": near_far(L0_ffn_Wr),
        "rope": rope_table(),
        "ident": np.eye(TP, dtype=np.float32),
        "causal": np.triu(np.ones((TP, TP), np.float32)),
        "before": np.triu(np.ones((TP, TP), np.float32), 1),
        "ones": np.ones((TP, TP), np.float32),
        "rank": np.tile(np.arange(E, 0, -1, dtype=np.float32), (TP, 1)),
        "base": np.tile(np.arange(E, dtype=np.float32) * CAP - SLOTS, (TP, 1)),
        "bits": np.tile(np.repeat(1 << np.arange(29, -1, -1, dtype=np.int32), E), (TP, 1)).astype(np.int32),
        "w1": np.concatenate([near_far(w) for w in (*L0_ffn_w1, L0_ffn_s1)]),
        "w3": np.concatenate([near_far(w) for w in (*L0_ffn_w3, L0_ffn_s3)]),
        "w2": np.concatenate([inner_rows(w) for w in (*L0_ffn_w2, L0_ffn_s2)]),
    }


def kernel(**inputs):
    import concourse.bacc as _bacc
    from concourse.bass_utils import run_bass_kernel_spmd as _run

    arrays = layout(**{k: np.asarray(v) for k, v in inputs.items()})
    nc = _bacc.Bacc("TRN2", target_bir_lowering=False, num_devices=1)
    dram = {n: nc.dram_tensor("in_" + n, a.shape, mybir.dt.from_np(a.dtype), kind="ExternalInput").ap()
            for n, a in arrays.items()}
    for n, shape in (("h2", (N, D)), ("x2", (N, D)), ("x2_t", (UNITS * 128, 2 * UT)), ("slots", (SLOTS, D)),
                     ("expert_rows", (SLOTS + 1, D))):
        dram[n] = nc.dram_tensor("dram_" + n, shape, F32, kind="Internal").ap()
    dram["out"] = nc.dram_tensor("out_rows", (N, D), F32, kind="ExternalOutput").ap()
    build(nc, dram)
    r = _run(nc, [{"in_" + n: a for n, a in arrays.items()}], core_ids=[0])
    return r.results[0]["out_rows"].reshape(B, S, D)
```
